# Optimizing a Trainium2 kernel written in Bass

```python
import numpy as np
import jax
import jax.numpy as jnp

def _softmax(x, axis=-1):
    return jax.nn.softmax(x, axis=axis)

def _gelu(x):
    return jax.nn.gelu(x, approximate=True)

def _silu(x):
    return jax.nn.silu(x)

def _sigmoid(x):
    return jax.nn.sigmoid(x)

def _layernorm(x, axis=-1, eps=1e-05):
    m = jnp.mean(x, axis=axis, keepdims=True)
    v = jnp.var(x, axis=axis, keepdims=True)
    return (x - m) / jnp.sqrt(v + eps)

def _scatter_add(tgt, idx, src, axis=0):
    return tgt.at[idx].add(src)

def _segment_sum(src, seg, n):
    return jax.ops.segment_sum(src, seg, n)
kernel_name = 'mk_gnn_preln_d4_gnn_r64_367a11'

def setup_inputs(seed: int=0):
    np.random.seed(seed)
    _w = jnp.asarray

    def _rec_inputs():
        import jax
        import jax.numpy as jnp
        _gk = jax.random.key(seed)
        x = -0.0003713 + 1 * jax.random.normal(jax.random.fold_in(_gk, 1), (100000, 128), jnp.float32)
        src = jax.random.randint(jax.random.fold_in(_gk, 2), (50000,), 0, 100000, jnp.int32)
        dst = jax.random.randint(jax.random.fold_in(_gk, 3), (50000,), 0, 100000, jnp.int32)
        _o = jnp.argsort(dst, stable=True)
        src = src[_o]
        dst = dst[_o]
        return (x, src, dst)
    x, src, dst = _rec_inputs()

    def _L0_gnn_setup():
        import jax, jax.numpy as jnp
        import numpy as np
        N_NODES = 100000
        N_EDGES = 25000
        D_IN = 128
        D_HID = 128
        D_OUT = 128

        def _sage_conv(x, src, dst, W_l, b_l, W_r, num_nodes):
            msgs = x[src]
            agg = jax.ops.segment_sum(msgs, dst, num_segments=num_nodes)
            deg = jax.ops.segment_sum(jnp.ones((src.shape[0],), x.dtype), dst, num_segments=num_nodes)
            mean = agg / jnp.maximum(deg, 1.0)[:, None]
            return mean @ W_l.T + b_l + x @ W_r.T
        key = jax.random.key(seed)
        ks = jax.random.split(key, 8)
        x = jax.random.normal(ks[0], (N_NODES, D_IN), dtype=jnp.float32)
        edge_index = jax.random.randint(ks[1], (2, N_EDGES), 0, N_NODES, dtype=jnp.int64)
        s1 = 1.0 / np.sqrt(D_IN)
        s2 = 1.0 / np.sqrt(D_HID)
        W1_l = jax.random.uniform(ks[2], (D_HID, D_IN), jnp.float32, -s1, s1)
        b1_l = jnp.zeros((D_HID,), jnp.float32)
        W1_r = jax.random.uniform(ks[3], (D_HID, D_IN), jnp.float32, -s1, s1)
        W2_l = jax.random.uniform(ks[4], (D_OUT, D_HID), jnp.float32, -s2, s2)
        b2_l = jnp.zeros((D_OUT,), jnp.float32)
        W2_r = jax.random.uniform(ks[5], (D_OUT, D_HID), jnp.float32, -s2, s2)
        return {'x': x, 'edge_index': edge_index, 'W1_l': W1_l, 'b1_l': b1_l, 'W1_r': W1_r, 'W2_l': W2_l, 'b2_l': b2_l, 'W2_r': W2_r}
    _L0_gnn_all = _L0_gnn_setup()
    _L0_gnn_in = {k: v for k, v in _L0_gnn_all.items() if k in ('W1_l', 'b1_l', 'W1_r', 'W2_l', 'b2_l', 'W2_r')}
    del _L0_gnn_all

    def _L1_gnn_setup():
        import jax, jax.numpy as jnp
        import numpy as np
        N, E, F_IN, H, D = (50000, 12500, 128, 4, 32)
        NEG_SLOPE = 0.2
        key = jax.random.key(seed)
        ks = jax.random.split(key, 8)
        x = jax.random.normal(ks[0], (N, F_IN), dtype=jnp.float32)
        src = jax.random.randint(ks[1], (E,), 0, N, dtype=jnp.int32)
        dst = jax.random.randint(ks[2], (E,), 0, N, dtype=jnp.int32)
        s = 1.0 / np.sqrt(F_IN)
        W_src = jax.random.uniform(ks[3], (F_IN, H * D), jnp.float32, -s, s)
        b_src = jnp.zeros((H * D,), jnp.float32)
        W_dst = jax.random.uniform(ks[4], (F_IN, H * D), jnp.float32, -s, s)
        b_dst = jnp.zeros((H * D,), jnp.float32)
        attn = jax.random.normal(ks[5], (H, D), dtype=jnp.float32) / np.sqrt(D)
        return {'x': x, 'src': src, 'dst': dst, 'W_src': W_src, 'b_src': b_src, 'W_dst': W_dst, 'b_dst': b_dst, 'attn': attn}
    _L1_gnn_all = _L1_gnn_setup()
    _L1_gnn_in = {k: v for k, v in _L1_gnn_all.items() if k in ('W_src', 'b_src', 'W_dst', 'b_dst', 'attn')}
    del _L1_gnn_all

    def _L2_gnn_setup():
        import jax, jax.numpy as jnp
        import numpy as np
        N_NODES = 50000
        key = jax.random.key(seed)
        k1, k2, k3, k4 = jax.random.split(key, 4)
        N, E, D_IN, D_OUT = (N_NODES, 25000, 128, 128)
        x = jax.random.normal(k1, (N, D_IN), dtype=jnp.float32)
        edge_index = jax.random.randint(k2, (2, E), 0, N, dtype=jnp.int64)
        W = jax.random.normal(k3, (D_IN, D_OUT), dtype=jnp.float32) * (1.0 / np.sqrt(D_IN))
        b = jax.random.normal(k4, (D_OUT,), dtype=jnp.float32) * 0.01
        return {'x': x, 'edge_index': edge_index, 'W': W, 'b': b}
    _L2_gnn_all = _L2_gnn_setup()
    _L2_gnn_in = {k: v for k, v in _L2_gnn_all.items() if k in ('W', 'b')}
    del _L2_gnn_all

    def _L3_gnn_setup():
        import jax, jax.numpy as jnp
        import numpy as np
        N = 50000
        E = 12500
        HID = 128
        NH = 8
        HD = 16
        FFN = 512
        EPS = 1e-05

        def _layer_norm(x, g, b):
            m = jnp.mean(x, axis=-1, keepdims=True)
            v = jnp.mean((x - m) ** 2, axis=-1, keepdims=True)
            return (x - m) * jax.lax.rsqrt(v + EPS) * g + b

        def _gnn_layer(x, edge_index, Wq, bq, Wk, bk, Wv, bv, Wo, bo, g1, b1, g2, b2, W1, bf1, W2, bf2):
            n = x.shape[0]
            residual = x
            h = _layer_norm(x, g1, b1)
            q = (h @ Wq + bq).reshape(n, NH, HD)
            k = (h @ Wk + bk).reshape(n, NH, HD)
            v = (h @ Wv + bv).reshape(n, NH, HD)
            src, dst = (edge_index[0], edge_index[1])
            deg = jax.ops.segment_sum(jnp.ones(src.shape, x.dtype), dst, num_segments=n)
            loops = jnp.arange(n, dtype=src.dtype)
            s_all = jnp.concatenate([src, loops])
            d_all = jnp.concatenate([dst, loops])
            e = jnp.sum(q[d_all] * k[s_all], axis=-1) / np.sqrt(HD).astype(np.float32)
            m = jax.lax.stop_gradient(jax.ops.segment_max(e, d_all, num_segments=n))
            p = jnp.exp(e - m[d_all])
            z = jax.ops.segment_sum(p, d_all, num_segments=n)
            alpha = p / z[d_all]
            agg = jax.ops.segment_sum(alpha[:, :, None] * v[s_all], d_all, num_segments=n)
            agg = jnp.where(deg[:, None, None] > 0, agg, jnp.zeros_like(agg))
            att = agg.reshape(n, NH * HD) @ Wo + bo
            x = residual + att
            residual = x
            h = _layer_norm(x, g2, b2)
            ffn = jax.nn.gelu(h @ W1 + bf1, approximate=False) @ W2 + bf2
            return residual + ffn
        key = jax.random.key(seed)
        ks = jax.random.split(key, 12)
        s = 0.02
        d = {}
        d['x'] = jax.random.normal(ks[0], (N, HID), jnp.float32)
        d['edge_index'] = jax.random.randint(ks[1], (2, E), 0, N, dtype=jnp.int32)
        d['Wq'] = jax.random.normal(ks[2], (HID, NH * HD), jnp.float32) * s
        d['bq'] = jnp.zeros((NH * HD,), jnp.float32)
        d['Wk'] = jax.random.normal(ks[3], (HID, NH * HD), jnp.float32) * s
        d['bk'] = jnp.zeros((NH * HD,), jnp.float32)
        d['Wv'] = jax.random.normal(ks[4], (HID, NH * HD), jnp.float32) * s
        d['bv'] = jnp.zeros((NH * HD,), jnp.float32)
        d['Wo'] = jax.random.normal(ks[5], (NH * HD, HID), jnp.float32) * s
        d['bo'] = jnp.zeros((HID,), jnp.float32)
        d['g1'] = jnp.ones((HID,), jnp.float32)
        d['b1'] = jnp.zeros((HID,), jnp.float32)
        d['g2'] = jnp.ones((HID,), jnp.float32)
        d['b2'] = jnp.zeros((HID,), jnp.float32)
        d['W1'] = jax.random.normal(ks[6], (HID, FFN), jnp.float32) * s
        d['bf1'] = jnp.zeros((FFN,), jnp.float32)
        d['W2'] = jax.random.normal(ks[7], (FFN, HID), jnp.float32) * s
        d['bf2'] = jnp.zeros((HID,), jnp.float32)
        return d
    _L3_gnn_all = _L3_gnn_setup()
    _L3_gnn_in = {k: v for k, v in _L3_gnn_all.items() if k in ('Wq', 'bq', 'Wk', 'bk', 'Wv', 'bv', 'Wo', 'bo', 'g1', 'b1', 'g2', 'b2', 'W1', 'bf1', 'W2', 'bf2')}
    del _L3_gnn_all
    return {'x': x, 'src': src, 'dst': dst, 'L0_gnn_W1_l': _L0_gnn_in['W1_l'], 'L0_gnn_b1_l': _L0_gnn_in['b1_l'], 'L0_gnn_W1_r': _L0_gnn_in['W1_r'], 'L0_gnn_W2_l': _L0_gnn_in['W2_l'], 'L0_gnn_b2_l': _L0_gnn_in['b2_l'], 'L0_gnn_W2_r': _L0_gnn_in['W2_r'], 'L1_gnn_W_src': _L1_gnn_in['W_src'], 'L1_gnn_b_src': _L1_gnn_in['b_src'], 'L1_gnn_W_dst': _L1_gnn_in['W_dst'], 'L1_gnn_b_dst': _L1_gnn_in['b_dst'], 'L1_gnn_attn': _L1_gnn_in['attn'], 'L2_gnn_W': _L2_gnn_in['W'], 'L2_gnn_b': _L2_gnn_in['b'], 'L3_gnn_Wq': _L3_gnn_in['Wq'], 'L3_gnn_bq': _L3_gnn_in['bq'], 'L3_gnn_Wk': _L3_gnn_in['Wk'], 'L3_gnn_bk': _L3_gnn_in['bk'], 'L3_gnn_Wv': _L3_gnn_in['Wv'], 'L3_gnn_bv': _L3_gnn_in['bv'], 'L3_gnn_Wo': _L3_gnn_in['Wo'], 'L3_gnn_bo': _L3_gnn_in['bo'], 'L3_gnn_g1': _L3_gnn_in['g1'], 'L3_gnn_b1': _L3_gnn_in['b1'], 'L3_gnn_g2': _L3_gnn_in['g2'], 'L3_gnn_b2': _L3_gnn_in['b2'], 'L3_gnn_W1': _L3_gnn_in['W1'], 'L3_gnn_bf1': _L3_gnn_in['bf1'], 'L3_gnn_W2': _L3_gnn_in['W2'], 'L3_gnn_bf2': _L3_gnn_in['bf2']}

def reference(x, src, dst, L0_gnn_W1_l, L0_gnn_b1_l, L0_gnn_W1_r, L0_gnn_W2_l, L0_gnn_b2_l, L0_gnn_W2_r, L1_gnn_W_src, L1_gnn_b_src, L1_gnn_W_dst, L1_gnn_b_dst, L1_gnn_attn, L2_gnn_W, L2_gnn_b, L3_gnn_Wq, L3_gnn_bq, L3_gnn_Wk, L3_gnn_bk, L3_gnn_Wv, L3_gnn_bv, L3_gnn_Wo, L3_gnn_bo, L3_gnn_g1, L3_gnn_b1, L3_gnn_g2, L3_gnn_b2, L3_gnn_W1, L3_gnn_bf1, L3_gnn_W2, L3_gnn_bf2):
    import jax
    import jax.numpy as jnp

    def _L0_gnn_ref(x, edge_index, W1_l, b1_l, W1_r, W2_l, b2_l, W2_r):
        import jax, jax.numpy as jnp
        import numpy as np
        N_NODES = 100000
        N_EDGES = 25000
        D_IN = 128
        D_HID = 128
        D_OUT = 128

        def _sage_conv(x, src, dst, W_l, b_l, W_r, num_nodes):
            msgs = x[src]
            agg = jax.ops.segment_sum(msgs, dst, num_segments=num_nodes)
            deg = jax.ops.segment_sum(jnp.ones((src.shape[0],), x.dtype), dst, num_segments=num_nodes)
            mean = agg / jnp.maximum(deg, 1.0)[:, None]
            return mean @ W_l.T + b_l + x @ W_r.T
        src, dst = (edge_index[0], edge_index[1])
        n = x.shape[0]
        h = _sage_conv(x, src, dst, W1_l, b1_l, W1_r, n)
        h = jax.nn.relu(h)
        out = _sage_conv(h, src, dst, W2_l, b2_l, W2_r, n)
        out = jnp.nan_to_num(out, nan=0.0, posinf=10000.0, neginf=-10000.0)
        return out

    def _L1_gnn_ref(x, src, dst, W_src, b_src, W_dst, b_dst, attn):
        import jax, jax.numpy as jnp
        import numpy as np
        N, E, F_IN, H, D = (50000, 12500, 128, 4, 32)
        NEG_SLOPE = 0.2
        n = x.shape[0]
        fs = (x @ W_src + b_src).reshape(n, H, D)
        fd = (x @ W_dst + b_dst).reshape(n, H, D)
        e = jax.nn.leaky_relu(fs[src] + fd[dst], NEG_SLOPE)
        score = jnp.einsum('ehd,hd->eh', e, attn)
        smax = jax.ops.segment_max(score, dst, num_segments=n)
        smax = jnp.where(jnp.isfinite(smax), smax, 0.0)
        ex = jnp.exp(score - smax[dst])
        denom = jax.ops.segment_sum(ex, dst, num_segments=n)
        alpha = ex / denom[dst]
        h = jax.ops.segment_sum(alpha[:, :, None] * fs[src], dst, num_segments=n)
        h = jax.nn.relu(h)
        return h.reshape(n, H * D)

    def _L2_gnn_ref(x, edge_index, W, b):
        import jax, jax.numpy as jnp
        import numpy as np
        N_NODES = 50000
        N = x.shape[0]
        loops = jnp.arange(N, dtype=edge_index.dtype)
        row = jnp.concatenate([edge_index[0], loops])
        col = jnp.concatenate([edge_index[1], loops])
        deg = jax.ops.segment_sum(jnp.ones_like(col, dtype=x.dtype), col, num_segments=N)
        deg_inv_sqrt = jnp.where(deg > 0, jax.lax.rsqrt(jnp.maximum(deg, 1.0)), 0.0)
        norm = deg_inv_sqrt[row] * deg_inv_sqrt[col]
        xl = x @ W + b
        msg = norm[:, None] * xl[col]
        out = jax.ops.segment_sum(msg, row, num_segments=N)
        return out

    def _L3_gnn_ref(x, edge_index, Wq, bq, Wk, bk, Wv, bv, Wo, bo, g1, b1, g2, b2, W1, bf1, W2, bf2):
        import jax, jax.numpy as jnp
        import numpy as np
        N = 50000
        E = 12500
        HID = 128
        NH = 8
        HD = 16
        FFN = 512
        EPS = 1e-05

        def _layer_norm(x, g, b):
            m = jnp.mean(x, axis=-1, keepdims=True)
            v = jnp.mean((x - m) ** 2, axis=-1, keepdims=True)
            return (x - m) * jax.lax.rsqrt(v + EPS) * g + b

        def _gnn_layer(x, edge_index, Wq, bq, Wk, bk, Wv, bv, Wo, bo, g1, b1, g2, b2, W1, bf1, W2, bf2):
            n = x.shape[0]
            residual = x
            h = _layer_norm(x, g1, b1)
            q = (h @ Wq + bq).reshape(n, NH, HD)
            k = (h @ Wk + bk).reshape(n, NH, HD)
            v = (h @ Wv + bv).reshape(n, NH, HD)
            src, dst = (edge_index[0], edge_index[1])
            deg = jax.ops.segment_sum(jnp.ones(src.shape, x.dtype), dst, num_segments=n)
            loops = jnp.arange(n, dtype=src.dtype)
            s_all = jnp.concatenate([src, loops])
            d_all = jnp.concatenate([dst, loops])
            e = jnp.sum(q[d_all] * k[s_all], axis=-1) / np.sqrt(HD).astype(np.float32)
            m = jax.lax.stop_gradient(jax.ops.segment_max(e, d_all, num_segments=n))
            p = jnp.exp(e - m[d_all])
            z = jax.ops.segment_sum(p, d_all, num_segments=n)
            alpha = p / z[d_all]
            agg = jax.ops.segment_sum(alpha[:, :, None] * v[s_all], d_all, num_segments=n)
            agg = jnp.where(deg[:, None, None] > 0, agg, jnp.zeros_like(agg))
            att = agg.reshape(n, NH * HD) @ Wo + bo
            x = residual + att
            residual = x
            h = _layer_norm(x, g2, b2)
            ffn = jax.nn.gelu(h @ W1 + bf1, approximate=False) @ W2 + bf2
            return residual + ffn
        return _gnn_layer(x, edge_index, Wq, bq, Wk, bk, Wv, bv, Wo, bo, g1, b1, g2, b2, W1, bf1, W2, bf2)
    edge_index = jnp.stack([src, dst])
    h = jnp.maximum(_layernorm(x, axis=-1), 0.0)
    x = x + _L0_gnn_ref(h, edge_index, L0_gnn_W1_l, L0_gnn_b1_l, L0_gnn_W1_r, L0_gnn_W2_l, L0_gnn_b2_l, L0_gnn_W2_r)
    h = jnp.maximum(_layernorm(x, axis=-1), 0.0)
    x = x + _L1_gnn_ref(h, src, dst, L1_gnn_W_src, L1_gnn_b_src, L1_gnn_W_dst, L1_gnn_b_dst, L1_gnn_attn)
    h = jnp.maximum(_layernorm(x, axis=-1), 0.0)
    x = x + _L2_gnn_ref(h, edge_index, L2_gnn_W, L2_gnn_b)
    h = jnp.maximum(_layernorm(x, axis=-1), 0.0)
    x = x + _L3_gnn_ref(h, edge_index, L3_gnn_Wq, L3_gnn_bq, L3_gnn_Wk, L3_gnn_bk, L3_gnn_Wv, L3_gnn_bv, L3_gnn_Wo, L3_gnn_bo, L3_gnn_g1, L3_gnn_b1, L3_gnn_g2, L3_gnn_b2, L3_gnn_W1, L3_gnn_bf1, L3_gnn_W2, L3_gnn_bf2)
    return x

_drawn_inputs = setup_inputs


def setup_inputs(seed=0):
    import zlib

    import numpy as np

    out = dict(_drawn_inputs(seed))
    spreads = {'L0_gnn_b1_l': (0.0, 0.1),
     'L0_gnn_b2_l': (0.0, 0.1),
     'L1_gnn_b_src': (0.0, 0.1),
     'L1_gnn_b_dst': (0.0, 2.0),
     'L3_gnn_bq': (0.0, 0.8),
     'L3_gnn_bk': (0.0, 2.0),
     'L3_gnn_bv': (0.0, 0.8),
     'L3_gnn_bo': (0.0, 0.1),
     'L3_gnn_g1': (1.0, 0.6),
     'L3_gnn_b1': (0.0, 0.8),
     'L3_gnn_g2': (1.0, 0.6),
     'L3_gnn_b2': (0.0, 2.0),
     'L3_gnn_bf1': (0.0, 0.643),
     'L3_gnn_bf2': (0.0, 0.1)}
    factors = {'L1_gnn_W_dst': 8.0,
     'L1_gnn_attn': 6.644,
     'L2_gnn_b': 6.103,
     'L3_gnn_Wq': 8.0,
     'L3_gnn_Wk': 8.0,
     'L3_gnn_Wv': 4.113,
     'L3_gnn_Wo': 3.851}
    for name, (base, spread) in spreads.items():
        noise = np.random.default_rng([zlib.crc32(name.encode()), seed]).standard_normal(out[name].shape)
        drawn = base * np.exp(spread * noise) if base else spread * noise
        out[name] = jnp.asarray(drawn.astype(out[name].dtype))
    for name, factor in factors.items():
        out[name] = (out[name] * factor).astype(out[name].dtype)
    return out
```

```python
from contextlib import ExitStack

import numpy as np

import concourse.bass as bass
from concourse import mybir

ALU = mybir.AluOpType
ACT = mybir.ActivationFunctionType
F32 = mybir.dt.float32
BF16 = mybir.dt.bfloat16
I32 = mybir.dt.int32

P = 128
TILES = 4
ROWS = P * TILES
WIDE = 132
PAD = 1 << 20
EPS = 1e-5
LOW = -3.0e38
NAN_LIMIT = 1e4


def tiles(x, rows=P, width=P):
    return x[0:rows, :].rearrange("p (a d) -> p a d", d=width)


class Machine:

    def __init__(self, nc, ins, out, ctx):
        self.nc, self.ins, self.out, self.ctx = nc, ins, out, ctx
        self.N = ins["x"].shape[0]
        self.E = ins["src"].shape[0]
        pair = 2 * ROWS
        self.EP = -(-self.E // pair) * pair
        self.G = self.EP // ROWS
        self.T = self.EP // P
        self.J = self.EP // P
        self.edge_pairs = self.G // 2
        self.node_pairs = self.N // pair
        rest = self.N - self.node_pairs * pair
        self.rest = []
        g, s = 2 * self.node_pairs, 0
        while rest > 0:
            r = min(rest, ROWS)
            assert r % TILES == 0
            self.rest.append((s, g, r // TILES))
            g, s, rest = g + 1, s + 1, rest - r

    def dram(self, name, shape, dt=F32):
        return self.nc.dram_tensor(name, shape, dt, kind="Internal").ap()

    def keep(self, name, shape, dt=F32):
        return self.ctx.enter_context(self.nc.sbuf_tensor(name, shape, dt))


class Phase:

    def __init__(self, m, name, ctx):
        self.m, self.name, self.ctx = m, name, ctx
        self.primed = []

    def sb(self, name, shape, dt=F32):
        return self.ctx.enter_context(self.m.nc.sbuf_tensor(f"{self.name}_{name}", shape, dt))

    def two(self, name, shape, dt=F32):
        return [self.sb(f"{name}{s}", shape, dt) for s in range(2)]

    def ps(self, name):
        return self.ctx.enter_context(self.m.nc.psum_tensor(f"{self.name}_ps_{name}", [P, 512], F32))

    def ps2(self, name):
        return [self.ps(f"{name}{s}") for s in range(2)]

    def sem(self, name):
        return self.ctx.enter_context(self.m.nc.semaphore(f"{self.name}_{name}"))

    def counter(self, name):
        return self.m.ctx.enter_context(self.m.nc.semaphore(f"{self.name}_{name}"))

    def prime(self, eng, n, *sems):
        for sem in sems:
            eng.sem_inc(sem, n)
            self.primed.append((sem, n))

    def retire(self):
        with self.m.nc.Block() as block:
            @block.vector
            def _(dve):
                for sem, n in self.primed:
                    dve.wait_ge(sem, n)
                    dve.sem_inc(sem, -n)

    def sem2(self, name):
        return [self.sem(f"{name}{s}") for s in range(2)]



def moments(nc, dve, own, xs, stats, mv, ve, rows=P):
    n = len(xs)
    for a, x in enumerate(xs):
        last = nc.vector.bn_stats(stats[0:rows, a, :], x)
    last.then_inc(own, 1)
    dve.wait_ge(own, 1)
    dve.sem_inc(own, -1)
    for a in range(n):
        last = nc.vector.bn_aggr(mv[0:rows, a, :], stats[0:rows, a, :])
    last.then_inc(own, 1)
    dve.wait_ge(own, 1)
    dve.sem_inc(own, -1)
    return nc.vector.tensor_scalar(ve[0:rows, 0:n], mv[0:rows, 0:n, 1], EPS, None, ALU.add)


def normalise(nc, outs, xs, mv, rs, rows=P):
    for a, (o, x) in enumerate(zip(outs, xs)):
        last = nc.vector.tensor_scalar(o, x, mv[0:rows, a, 0:1], rs[0:rows, a:a + 1], ALU.subtract, ALU.mult)
    return last


def turn(nc, ps, x, ident, rows=P):
    for a in range(TILES):
        last = nc.tensor.transpose(ps[:, a * rows:(a + 1) * rows], x[:, a, :], ident[0:rows, 0:rows])
    return last


def rows_product(nc, ps, terms, bias_row, ones_row, rows=P):
    for a in range(TILES):
        out = ps[0:rows, a * P:(a + 1) * P]
        nc.tensor.matmul(out, ones_row[0:1, 0:rows], bias_row[0:1, :], start=True, stop=False)
        for k, (cols, w) in enumerate(terms):
            last = nc.tensor.matmul(out, cols[:, a * rows:(a + 1) * rows], w, start=False, stop=(k == len(terms) - 1))
    return last



def weights(m):
    nc, ins = m.nc, m.ins
    m.ident = m.keep("ident", [P, P])
    m.ones_row = m.keep("ones_row", [1, P])
    m.half = m.keep("half", [P, 8])
    names = ["W1l", "W1r", "W2l", "W2r"]
    m.wT = {k: m.keep(k, [P, P]) for k in names}
    m.wn = {k: m.keep(k, [P, P]) for k in ["Ws", "Wd", "W", "Wq", "Wk", "Wv", "Wo"]}
    m.W1 = m.keep("W1", [P, 512])
    m.W2 = m.keep("W2", [P, 4, P])
    m.bias = {k: m.keep("row_" + k, [1, P]) for k in ["b1", "b2", "b", "bo", "bf2"]}
    m.attn_heads = m.keep("attn_heads", [P, P])
    m.sum_heads = m.keep("sum_heads", [P, P])
    m.col = {k: m.keep("col_" + k, [P, 1]) for k in ["bs", "bsd", "bd", "at", "bq", "bv", "g1", "b1", "g2", "b2"]}
    m.bf1 = m.keep("col_bf1", [P, 4])
    m.bo_rows = m.keep("bo_rows", [32, P])
    with ExitStack() as ctx:
        ph = Phase(m, "w", ctx)
        raw = {k: ph.sb("raw" + k, [P, P]) for k in names}
        folded = {k: ph.ps("f" + k) for k in ["a", "b"]}
        landed, made = ph.counter("landed"), ph.counter("made")
        chosen, turned, own = (ph.sem(n) for n in ["chosen", "turned", "own"])
        loads = [(raw["W1l"][:, :], ins["L0_gnn_W1_l"]), (raw["W1r"][:, :], ins["L0_gnn_W1_r"]),
                 (raw["W2l"][:, :], ins["L0_gnn_W2_l"]), (raw["W2r"][:, :], ins["L0_gnn_W2_r"]),
                 (m.wn["Ws"][:, :], ins["L1_gnn_W_src"]), (m.wn["Wd"][:, :], ins["L1_gnn_W_dst"]),
                 (m.wn["W"][:, :], ins["L2_gnn_W"]), (m.wn["Wq"][:, :], ins["L3_gnn_Wq"]),
                 (m.wn["Wk"][:, :], ins["L3_gnn_Wk"]), (m.wn["Wv"][:, :], ins["L3_gnn_Wv"]),
                 (m.wn["Wo"][:, :], ins["L3_gnn_Wo"]), (m.W1[:, :], ins["L3_gnn_W1"]),
                 (m.W2[:, :, :], ins["L3_gnn_W2"].rearrange("(h p) d -> p h d", p=P)),
                 (m.bf1[:, :], ins["L3_gnn_bf1"].rearrange("(h p) -> p h", p=P)),
                 (m.col["at"][:, :], ins["L1_gnn_attn"].rearrange("h d -> (h d)").rearrange("(p o) -> p o", o=1)),
                 (m.bo_rows[:, :], ins["L3_gnn_bo"].rearrange("(o d) -> o d", o=1).broadcast_to([32, P]))]
        loads += [(m.col[k][:, :], ins[v].rearrange("(p o) -> p o", o=1)) for k, v in
                  [("bs", "L1_gnn_b_src"), ("bd", "L1_gnn_b_dst"), ("bq", "L3_gnn_bq"), ("bv", "L3_gnn_bv"),
                   ("g1", "L3_gnn_g1"), ("b1", "L3_gnn_b1"), ("g2", "L3_gnn_g2"), ("b2", "L3_gnn_b2")]]
        loads += [(m.bias[k][0:1, :], ins[v].rearrange("(o d) -> o d", o=1)) for k, v in
                  [("b1", "L0_gnn_b1_l"), ("b2", "L0_gnn_b2_l"), ("b", "L2_gnn_b"), ("bo", "L3_gnn_bo"),
                   ("bf2", "L3_gnn_bf2")]]
        with nc.Block() as block:
            @block.sync
            def _(sp):
                with nc.allow_non_contiguous_dma(reason="bias columns"):
                    for dst, src in loads:
                        sp.dma_start(dst, src).then_inc(landed, 16)
                sp.wait_ge(landed, 16 * len(loads))

            @block.gpsimd
            def _(pool):
                nc.gpsimd.memset(m.ident[:, :], 0.0).then_inc(made, 1)
                nc.gpsimd.memset(m.attn_heads[:, :], 1.0).then_inc(made, 1)
                nc.gpsimd.memset(m.sum_heads[:, :], 0.25).then_inc(made, 1)
                nc.gpsimd.memset(m.half[:, :], -0.5).then_inc(made, 1)
                nc.gpsimd.memset(m.ones_row[:, :], 1.0).then_inc(made, 1)
                pool.wait_ge(made, 5)
                nc.gpsimd.affine_select(out=m.ident[:, :], in_=m.ident[:, :], compare_op=ALU.not_equal, fill=1.0,
                                        base=0, pattern=[[-1, P]], channel_multiplier=1).then_inc(made, 1)
                n = 6
                for t, w in ((m.attn_heads, 32), (m.sum_heads, 16)):
                    v = t[:, :].rearrange("p (h c) -> p h c", c=w)
                    pool.wait_ge(made, n)
                    nc.gpsimd.affine_select(out=v, in_=v, compare_op=ALU.is_ge, fill=0.0, base=0,
                                            pattern=[[-w, P // w], [0, w]], channel_multiplier=1).then_inc(made, 1)
                    pool.wait_ge(made, n + 1)
                    nc.gpsimd.affine_select(out=v, in_=v, compare_op=ALU.is_ge, fill=0.0, base=w - 1,
                                            pattern=[[w, P // w], [0, w]], channel_multiplier=-1).then_inc(made, 1)
                    n += 2
                pool.wait_ge(made, n)
                pool.sem_inc(chosen, 2)

            @block.tensor
            def _(pe):
                pe.wait_ge(chosen, 1)
                pe.sem_inc(chosen, -1)
                pe.wait_ge(landed, 16 * len(loads))
                for n, k in enumerate(names):
                    last = nc.tensor.transpose(folded["a"][:, n * P:(n + 1) * P], raw[k][:, :], m.ident[:, :])
                cols = [(m.wn["Wq"][:, :], m.col["b1"]), (m.wn["Wv"][:, :], m.col["b1"])]
                cols += [(m.W1[:, h * P:(h + 1) * P], m.col["b2"]) for h in range(4)]
                for n, (w, c) in enumerate(cols):
                    last = nc.tensor.matmul(folded["b"][:, n:n + 1], w, c[:, :], start=True, stop=True)
                last.then_inc(turned, 1)

            @block.vector
            def _(dve):
                dve.wait_ge(turned, 1)
                dve.sem_inc(turned, -1)
                dve.wait_ge(chosen, 1)
                dve.sem_inc(chosen, -1)
                for n, k in enumerate(names):
                    nc.vector.tensor_copy(m.wT[k][:, :], folded["a"][:, n * P:(n + 1) * P])
                nc.vector.tensor_tensor(m.col["bq"][:, :], m.col["bq"][:, :], folded["b"][:, 0:1], ALU.add)
                nc.vector.tensor_tensor(m.col["bv"][:, :], m.col["bv"][:, :], folded["b"][:, 1:2], ALU.add)
                nc.vector.tensor_tensor(m.bf1[:, :], m.bf1[:, :], folded["b"][:, 2:6], ALU.add)
                nc.vector.tensor_tensor(m.col["bsd"][:, :], m.col["bs"][:, :], m.col["bd"][:, :], ALU.add)
                for k in ("Wq", "Wk", "Wv"):
                    nc.vector.tensor_scalar(m.wn[k][:, :], m.wn[k][:, :], m.col["g1"][:, :], None, ALU.mult)
                nc.vector.tensor_scalar(m.W1[:, :], m.W1[:, :], m.col["g2"][:, :], None, ALU.mult)
                last = nc.vector.tensor_scalar(m.attn_heads[:, :], m.attn_heads[:, :], m.col["at"][:, :], None,
                                               ALU.mult)
                last.then_inc(own, 1)
                dve.wait_ge(own, 1)
                dve.sem_inc(own, -1)



def edges(m):
    nc, ins = m.nc, m.ins
    J, G, T, E, EP = m.J, m.G, m.T, m.E, m.EP
    full, rest = E // J, E % J
    m.gather_idx = m.dram("gather_idx", (P, G, 8), I32)
    m.scatter_idx = m.dram("scatter_idx", (P, G, 4), I32)
    m.last_idx = m.dram("last_idx", (P, G, 4), I32)
    m.edge_col = m.dram("edge_col", (P, G, 8))
    m.row = {k: m.dram("row_" + k, (EP,)) for k in ["src", "dst", "key", "sidx", "lidx", "dis", "rdeg"]}
    m.keep_row = m.dram("keep_row", (EP,), BF16)
    m.neg_row = m.dram("neg_row", (EP,), BF16)
    with ExitStack() as ctx:
        ph = Phase(m, "e", ctx)
        ints = {k: ph.sb("i" + k, [P, J], I32) for k in ["dst", "prev", "next", "src"]}
        f = {k: ph.sb("f" + k, [P, J]) for k in
             ["dst", "prev", "next", "src", "same", "nsame", "cnt", "ones", "head", "tail", "tmp", "num", "sidx",
              "lidx", "rdeg", "ve", "dis", "half", "rem", "key", "tmp2"]}
        number = ph.sb("number", [P, J], I32)
        keep16, neg16 = ph.sb("keep16", [P, J], BF16), ph.sb("neg16", [P, J], BF16)
        diag = [ph.sb(f"diag{i}", [P, P]) for i in range(2)]
        link = [ph.sb(f"link{i}", [P, P]) for i in range(2)]
        upper, lower, ones = ph.sb("upper", [P, P]), ph.sb("lower", [P, P]), ph.sb("onesm", [P, P])
        in_head = ph.sb("in_head", [P, 1])
        carry = [ph.sb(f"carry{i}", [P, 1]) for i in range(2)]
        psa, psb, psc = ph.ps("a"), ph.ps("b"), ph.ps("c")
        own_pool = ph.sem("own_pool")
        landed, stored = ph.counter("landed"), ph.counter("stored")
        filled, made, own, diags, spread, links, closed, ve_ready, dis_ready = (
            ph.sem(n) for n in ["filled", "made", "own", "diags", "spread", "links", "closed", "ve", "dis"])
        dst, src = ins["dst"], ins["src"]

        def flat(v, a, b):
            return v[a:b].rearrange("(o d) -> o d", o=1)

        def block_of(v, a, n):
            return v[a:a + n * J].rearrange("(p j) -> p j", j=J)

        loads = [(ints["dst"][0:full, :], block_of(dst, 0, full)), (ints["src"][0:full, :], block_of(src, 0, full)),
                 (ints["prev"][0:1, 1:J], flat(dst, 0, J - 1)), (ints["prev"][1:full, :], block_of(dst, J - 1, full - 1))]
        if rest:
            loads += [(ints["dst"][full:full + 1, 0:rest], flat(dst, full * J, E)),
                      (ints["src"][full:full + 1, 0:rest], flat(src, full * J, E)),
                      (ints["prev"][full:full + 1, 0:rest], flat(dst, full * J - 1, E - 1)),
                      (ints["next"][0:full, :], block_of(dst, 1, full))]
            if rest > 1:
                loads += [(ints["next"][full:full + 1, 0:rest - 1], flat(dst, full * J + 1, E))]
        else:
            loads += [(ints["next"][0:full - 1, :], block_of(dst, 1, full - 1)),
                      (ints["next"][full - 1:full, 0:J - 1], flat(dst, (full - 1) * J + 1, E))]
        rows_out = [(m.row[k], f[k]) for k in ["src", "dst", "key", "sidx", "lidx", "dis", "rdeg"]]
        rows_out += [(m.keep_row, keep16), (m.neg_row, neg16)]

        with nc.Block() as block:
            @block.sync
            def _(sp):
                sp.wait_ge(filled, 1)
                sp.sem_inc(filled, -1)
                for o, i in loads:
                    sp.dma_start(o, i).then_inc(landed, 16)
                sp.wait_ge(closed, 1)
                sp.sem_inc(closed, -1)
                for o, i in rows_out:
                    sp.dma_start(o.rearrange("(p j) -> p j", j=J), i[:, :]).then_inc(stored, 16)
                sp.wait_ge(stored, 16 * len(rows_out))

            @block.gpsimd
            def _(pool):
                nc.gpsimd.memset(ints["dst"][:, :], PAD)
                nc.gpsimd.memset(ints["prev"][:, :], -1)
                nc.gpsimd.memset(ints["next"][:, :], PAD)
                nc.gpsimd.memset(ints["src"][:, :], m.N).then_inc(own_pool, 1)
                pool.wait_ge(own_pool, 1)
                pool.sem_inc(own_pool, -1)
                pool.sem_inc(filled, 1)
                nc.gpsimd.iota(number[:, :], pattern=[[1, J]], base=0, channel_multiplier=J)
                nc.gpsimd.memset(f["half"][:, :], -0.5)
                for t, b, c in ((upper, -1, -1), (lower, -1, 1)):
                    nc.gpsimd.memset(t[:, :], 1.0).then_inc(own_pool, 1)
                    pool.wait_ge(own_pool, 1)
                    pool.sem_inc(own_pool, -1)
                    nc.gpsimd.affine_select(out=t[:, :], in_=t[:, :], compare_op=ALU.is_ge, fill=0.0, base=b,
                                            pattern=[[-c, P]], channel_multiplier=c).then_inc(own_pool, 1)
                    pool.wait_ge(own_pool, 1)
                    pool.sem_inc(own_pool, -1)
                pool.sem_inc(made, 1)
                pool.wait_ge(ve_ready, 1)
                pool.sem_inc(ve_ready, -1)
                nc.gpsimd.tensor_tensor(f["dis"][:, :], f["ve"][:, :], f["half"][:, :], ALU.pow).then_inc(dis_ready, 1)

            @block.tensor
            def _(pe):
                pe.wait_ge(diags, 1)
                pe.sem_inc(diags, -1)
                nc.tensor.matmul(psa[:, 0:P], ones[:, :], diag[0][:, :], start=True, stop=True)
                nc.tensor.matmul(psb[:, 0:P], ones[:, :], diag[1][:, :], start=True, stop=True).then_inc(spread, 1)
                pe.wait_ge(links, 1)
                pe.sem_inc(links, -1)
                nc.tensor.matmul(psa[:, 0:1], link[0][:, :], f["cnt"][:, J - 1:J], start=True, stop=True)
                nc.tensor.matmul(psb[:, 0:1], link[1][:, :], in_head[:, :], start=True, stop=True).then_inc(spread, 1)

            @block.vector
            def _(dve):
                v = nc.vector
                first, last = f["dst"][:, 0:1], f["dst"][:, J - 1:J]
                dve.wait_ge(landed, 16 * len(loads))
                dve.wait_ge(made, 1)
                dve.sem_inc(made, -1)
                for k, i in [("dst", "dst"), ("prev", "prev"), ("next", "next"), ("key", "src")]:
                    v.tensor_copy(f[k][:, :], ints[i][:, :])
                v.memset(ones[:, :], 1.0)
                v.memset(f["ones"][:, :], 1.0)
                v.tensor_copy(f["num"][:, :], number[:, :]).then_inc(own, 1)
                dve.wait_ge(own, 1)
                dve.sem_inc(own, -1)
                v.tensor_tensor(f["same"][:, :], f["dst"][:, :], f["prev"][:, :], ALU.is_equal)
                v.tensor_tensor(f["nsame"][:, :], f["dst"][:, :], f["next"][:, :], ALU.is_equal)
                v.tensor_scalar(f["head"][:, :], f["dst"][:, :], first, None, ALU.is_equal)
                v.tensor_scalar(f["tail"][:, :], f["dst"][:, :], last, None, ALU.is_equal)
                v.tensor_scalar(diag[0][:, :], m.ident[:, :], first, None, ALU.mult)
                v.tensor_scalar(diag[1][:, :], m.ident[:, :], last, None, ALU.mult).then_inc(own, 1)
                dve.wait_ge(own, 1)
                dve.sem_inc(own, -1)
                dve.sem_inc(diags, 1)
                v.tensor_copy(keep16[:, :], f["same"][:, :])
                v.tensor_scalar(neg16[:, :], f["same"][:, :], -1.0, -LOW, ALU.add, ALU.mult)
                v.tensor_tensor_scan(f["cnt"][:, :], f["same"][:, :], f["ones"][:, :], 0.0, ALU.mult, ALU.add)
                v.tensor_tensor_scan(f["rem"][:, ::-1], f["nsame"][:, ::-1], f["nsame"][:, ::-1], -1.0,
                                     ALU.mult, ALU.add)
                v.reduce_sum(in_head[:, :], f["head"][:, :], mybir.AxisListType.X)
                dve.wait_ge(spread, 1)
                dve.sem_inc(spread, -1)
                v.tensor_scalar(link[0][:, :], psa[:, 0:P], last, None, ALU.is_equal)
                v.tensor_scalar(link[1][:, :], psb[:, 0:P], first, None, ALU.is_equal).then_inc(own, 1)
                dve.wait_ge(own, 1)
                dve.sem_inc(own, -1)
                v.tensor_tensor(link[0][:, :], link[0][:, :], upper[:, :], ALU.mult)
                v.tensor_tensor(link[1][:, :], link[1][:, :], lower[:, :], ALU.mult).then_inc(own, 1)
                dve.wait_ge(own, 1)
                dve.sem_inc(own, -1)
                dve.sem_inc(links, 1)
                dve.wait_ge(spread, 1)
                dve.sem_inc(spread, -1)
                v.tensor_copy(carry[0][:, :], psa[:, 0:1])
                v.tensor_copy(carry[1][:, :], psb[:, 0:1]).then_inc(own, 1)
                dve.wait_ge(own, 1)
                dve.sem_inc(own, -1)
                v.tensor_scalar(f["head"][:, :], f["head"][:, :], carry[0][:, :], None, ALU.mult)
                v.tensor_scalar(f["tail"][:, :], f["tail"][:, :], carry[1][:, :], None, ALU.mult).then_inc(own, 1)
                dve.wait_ge(own, 1)
                dve.sem_inc(own, -1)
                v.tensor_tensor(f["cnt"][:, :], f["cnt"][:, :], f["head"][:, :], ALU.add)
                v.tensor_tensor(f["rem"][:, :], f["rem"][:, :], f["tail"][:, :], ALU.add).then_inc(own, 1)
                dve.wait_ge(own, 1)
                dve.sem_inc(own, -1)
                v.tensor_tensor(f["lidx"][:, :], f["rem"][:, :], f["num"][:, :], ALU.add)
                v.tensor_scalar(f["ve"][:, :], f["cnt"][:, :], 1.0, None, ALU.add).then_inc(ve_ready, 1)
                v.reciprocal(f["rdeg"][:, :], f["cnt"][:, :])
                v.scalar_tensor_tensor(f["sidx"][:, :], f["nsame"][:, :], float(PAD), f["dst"][:, :], ALU.mult, ALU.add)
                v.tensor_scalar(f["tmp2"][:, :], f["key"][:, :], float(m.N), None, ALU.is_lt)
                v.tensor_scalar(f["tmp"][:, :], f["dst"][:, :], float(PAD), None, ALU.is_lt).then_inc(own, 1)
                dve.wait_ge(own, 1)
                dve.sem_inc(own, -1)
                v.tensor_tensor(f["src"][:, :], f["key"][:, :], f["tmp2"][:, :], ALU.mult)
                v.tensor_tensor(f["dst"][:, :], f["dst"][:, :], f["tmp"][:, :], ALU.mult).then_inc(own, 1)
                dve.wait_ge(own, 1)
                dve.sem_inc(own, -1)
                dve.wait_ge(dis_ready, 1)
                dve.sem_inc(dis_ready, -1)
                dve.sem_inc(closed, 1)

    with ExitStack() as ctx:
        ph = Phase(m, "c", ctx)
        keys = ["src", "dst", "key", "sidx", "lidx", "dis"]
        back = {k: ph.sb("back" + k, [G, 4, P]) for k in keys}
        col = {k: ph.sb("col" + k, [P, T]) for k in keys}
        gi, si, li = (ph.sb(n, [P, G, w], I32) for n, w in (("gi", 8), ("si", 4), ("li", 4)))
        ec = ph.sb("ec", [P, G, 8])
        ps = {k: ph.ps(k) for k in keys}
        landed, stored = ph.counter("landed"), ph.counter("stored")
        turned, own, closed = (ph.sem(n) for n in ["turned", "own", "closed"])
        outs = [(m.gather_idx, gi), (m.scatter_idx, si), (m.last_idx, li), (m.edge_col, ec)]
        with nc.Block() as block:
            @block.sync
            def _(sp):
                for k in keys:
                    sp.dma_start(back[k][:, :, :], m.row[k].rearrange("(b r p) -> r b p", b=4, p=P)).then_inc(landed, 16)
                sp.wait_ge(closed, 1)
                sp.sem_inc(closed, -1)
                for o, i in outs:
                    sp.dma_start(o, i[:, :, :]).then_inc(stored, 16)
                sp.wait_ge(stored, 16 * len(outs))

            @block.tensor
            def _(pe):
                pe.wait_ge(landed, 16 * len(keys))
                for k in keys:
                    for b in range(4):
                        last = nc.tensor.transpose(ps[k][:, b * G:(b + 1) * G], back[k][:, b, :], m.ident[0:G, 0:G])
                last.then_inc(turned, 1)

            @block.vector
            def _(dve):
                dve.wait_ge(turned, 1)
                dve.sem_inc(turned, -1)
                for k in keys:
                    last = nc.vector.tensor_copy(col[k][:, :], ps[k][:, 0:T])
                last.then_inc(own, 1)
                dve.wait_ge(own, 1)
                dve.sem_inc(own, -1)

                def by_group(k):
                    return col[k][:, :].rearrange("p (g a) -> p g a", a=4)
                nc.vector.tensor_copy(gi[:, :, 0:4], by_group("src"))
                nc.vector.tensor_copy(gi[:, :, 4:8], by_group("dst"))
                nc.vector.tensor_copy(si[:, :, :], by_group("sidx"))
                nc.vector.tensor_copy(li[:, :, :], by_group("lidx"))
                nc.vector.tensor_copy(ec[:, :, 0:4], by_group("dis"))
                nc.vector.tensor_copy(ec[:, :, 4:8], by_group("key")).then_inc(own, 1)
                dve.wait_ge(own, 1)
                dve.sem_inc(own, -1)
                dve.sem_inc(closed, 1)



def over_node_pairs(m, eng, body, first=0, shift=0):
    if m.node_pairs > first:
        with eng.Fori(first, m.node_pairs) as i:
            body([(0, 2 * i, P), (1, 2 * i + 1, P)])
    if m.rest:
        body(m.rest)


def node_rows(table, g, rows):
    if isinstance(g, int):
        part = table[g * ROWS:g * ROWS + rows * TILES, :]
    else:
        part = table[bass.ds(g * ROWS, rows * TILES), :]
    return part.rearrange("(p a) d -> p a d", a=TILES)


def guard_parts(nc, pool, own, y, pos, neg, rows):
    nc.gpsimd.tensor_scalar(pos[0:rows, :], y[0:rows, :], 0.0, NAN_LIMIT, ALU.max, ALU.min)
    nc.gpsimd.tensor_scalar(neg[0:rows, :], y[0:rows, :], 0.0, -NAN_LIMIT, ALU.min, ALU.max).then_inc(own, 1)
    pool.wait_ge(own, 1)
    pool.sem_inc(own, -1)
    return nc.gpsimd.tensor_tensor(pos[0:rows, :], pos[0:rows, :], neg[0:rows, :], ALU.add)



def nodes_first(m):
    nc = m.nc
    x = m.ins["x"]
    m.h1 = m.dram("h1", (m.N, P))
    m.x1 = m.dram("x1", (m.N, WIDE))
    m.x3 = m.dram("x3", (m.N + 2 * ROWS, P))
    with ExitStack() as ctx:
        ph = Phase(m, "n", ctx)
        X = ph.two("x", [P, TILES, P])
        N0, H1, Y, POS, NEG, N1, X3 = (ph.two(k, [P, ROWS]) for k in ["n0", "h1", "y", "pos", "neg", "n1", "x3"])
        FIN = ph.two("fin", [P, ROWS], I32)
        HT, H1T, NT = (ph.two(k, [P, ROWS]) for k in ["ht", "h1t", "nt"])
        X1 = ph.two("x1", [P, TILES, WIDE])
        ST, MV, VE, RS = ph.two("st", [P, 4, 6]), ph.two("mv", [P, 4, 2]), ph.two("ve", [P, 4]), ph.two("rs", [P, 4])
        PA, PB, PC, PD = ph.ps2("a"), ph.ps2("b"), ph.ps2("c"), ph.ps2("d")
        x_in, saved = ph.sem2("x_in"), ph.sem2("saved")
        (x_free, ve, rs, n0, t0, ht, h1_ps, h1_pe, h1_out, t1, h1t, y_ps, y_pool, y_dve, fixed, x1_out, n1, t2, nt,
         xl_ps, x3_out, h1_free, x1_free, x3_free, own_d, own_a, own_p, zeroed) = (ph.sem(k) for k in [
             "x_free", "ve", "rs", "n0", "t0", "ht", "h1_ps", "h1_pe", "h1_out", "t1", "h1t", "y_ps", "y_pool",
             "y_dve", "fixed", "x1_out", "n1", "t2", "nt", "xl_ps", "x3_out", "h1_free", "x1_free", "x3_free",
             "own_d", "own_a", "own_p", "zeroed"])

        with nc.Block() as block:
            @block.sync
            def _(sp):
                def load(slots):
                    for s, g, r in slots:
                        sp.wait_ge(x_free, 1)
                        sp.sem_inc(x_free, -1)
                        sp.dma_start(X[s][0:r, :, :], node_rows(x, g, r)).then_inc(x_in[s], 16)

                def store(slots):
                    for ready_sem, table, of in ((h1_out, m.h1, lambda s, r: tiles(H1[s], r)),
                                                 (x1_out, m.x1, lambda s, r: X1[s][0:r, :, :]),
                                                 (x3_out, m.x3, lambda s, r: tiles(X3[s], r))):
                        for s, g, r in slots:
                            sp.wait_ge(ready_sem, 1)
                            sp.sem_inc(ready_sem, -1)
                            sp.dma_start(node_rows(table, g, r), of(s, r)).then_inc(saved[s], 16)
                    for s, g, r in slots:
                        sp.wait_ge(saved[s], 48)
                        sp.sem_inc(saved[s], -48)
                        for sem in (h1_free, x1_free, x3_free):
                            sp.sem_inc(sem, 1)

                load([(0, 0, P), (1, 1, P)])
                sp.wait_ge(zeroed, 1)
                sp.sem_inc(zeroed, -1)
                for k in range(2):
                    part = m.x3[m.N + k * ROWS:m.N + (k + 1) * ROWS, :].rearrange("(p a) d -> p a d", a=TILES)
                    sp.dma_start(part, tiles(X3[0])).then_inc(saved[0], 16)
                sp.wait_ge(saved[0], 32)
                sp.sem_inc(saved[0], -32)
                ph.prime(sp, 2, x3_free)
                with sp.Fori(0, m.node_pairs - 1) as i:
                    load([(0, 2 * i + 2, P), (1, 2 * i + 3, P)])
                    store([(0, 2 * i, P), (1, 2 * i + 1, P)])
                load(m.rest)
                store([(0, 2 * m.node_pairs - 2, P), (1, 2 * m.node_pairs - 1, P)])
                store(m.rest)

            @block.gpsimd
            def _(pool):
                def power(slots):
                    for s, g, r in slots:
                        pool.wait_ge(ve, 1)
                        pool.sem_inc(ve, -1)
                        nc.gpsimd.tensor_tensor(RS[s][0:r, :], VE[s][0:r, :], m.half[0:r, 0:4], ALU.pow).then_inc(rs, 1)

                def body(slots):
                    power(slots)
                    for s, g, r in slots:
                        pool.wait_ge(y_pool, 1)
                        pool.sem_inc(y_pool, -1)
                        guard_parts(nc, pool, own_p, Y[s], POS[s], NEG[s], r).then_inc(fixed, 1)
                    power(slots)
                over_node_pairs(m, pool, body)

            @block.vector
            def _(dve):
                ph.prime(dve, 2, x_free, h1_free, x1_free)
                nc.vector.memset(X3[0][:, :], 0.0)
                for s in range(2):
                    last = nc.vector.memset(X1[s][:, :, :], 1.0)
                last.then_inc(own_d, 1)
                dve.wait_ge(own_d, 1)
                dve.sem_inc(own_d, -1)
                dve.sem_inc(zeroed, 1)

                def body(slots):
                    for s, g, r in slots:
                        dve.wait_ge(x_in[s], 16)
                        dve.sem_inc(x_in[s], -16)
                        moments(nc, dve, own_d, [X[s][0:r, a, :] for a in range(4)], ST[s], MV[s], VE[s], r
                                ).then_inc(ve, 1)
                    for s, g, r in slots:
                        dve.wait_ge(rs, 1)
                        dve.sem_inc(rs, -1)
                        n = tiles(N0[s], r)
                        normalise(nc, [n[:, a, :] for a in range(4)], [X[s][0:r, a, :] for a in range(4)], MV[s],
                                  RS[s], r).then_inc(n0, 1)
                    for s, g, r in slots:
                        dve.wait_ge(y_dve, 1)
                        dve.sem_inc(y_dve, -1)
                        nc.vector.tensor_scalar(FIN[s][0:r, :], Y[s][0:r, :], 0.0, 0.0, ALU.mult,
                                                          ALU.is_equal).then_inc(own_d, 1)
                        dve.wait_ge(own_d, 1)
                        dve.sem_inc(own_d, -1)
                        dve.wait_ge(fixed, 1)
                        dve.sem_inc(fixed, -1)
                        nc.vector.copy_predicated(POS[s][0:r, :], FIN[s][0:r, :], Y[s][0:r, :]).then_inc(own_d, 1)
                        dve.wait_ge(own_d, 1)
                        dve.sem_inc(own_d, -1)
                        dve.wait_ge(x1_free, 1)
                        dve.sem_inc(x1_free, -1)
                        nc.vector.tensor_tensor(X1[s][0:r, :, 0:P], X[s][0:r, :, :], tiles(POS[s], r),
                                                          ALU.add).then_inc(own_d, 1)
                        dve.wait_ge(own_d, 1)
                        dve.sem_inc(own_d, -1)
                        dve.sem_inc(x1_out, 1)
                        dve.sem_inc(x_free, 1)
                        moments(nc, dve, own_d, [X1[s][0:r, a, 0:P] for a in range(4)], ST[s], MV[s], VE[s], r
                                ).then_inc(ve, 1)
                    for s, g, r in slots:
                        dve.wait_ge(rs, 1)
                        dve.sem_inc(rs, -1)
                        n = tiles(N1[s], r)
                        normalise(nc, [n[:, a, :] for a in range(4)], [X1[s][0:r, a, 0:P] for a in range(4)], MV[s],
                                  RS[s], r).then_inc(n1, 1)
                    for s, g, r in slots:
                        dve.wait_ge(xl_ps, 1)
                        dve.sem_inc(xl_ps, -1)
                        dve.wait_ge(x3_free, 1)
                        dve.sem_inc(x3_free, -1)
                        nc.vector.tensor_tensor(tiles(X3[s], r), tiles(PB[s], r), X1[s][0:r, :, 0:P], ALU.add
                                                ).then_inc(x3_out, 1)
                over_node_pairs(m, dve, body)

            @block.tensor
            def _(pe):
                def body(slots):
                    for s, g, r in slots:
                        pe.wait_ge(n0, 1)
                        pe.sem_inc(n0, -1)
                        turn(nc, PA[s], tiles(N0[s], r), m.ident, r).then_inc(t0, 1)
                    for s, g, r in slots:
                        pe.wait_ge(ht, 1)
                        pe.sem_inc(ht, -1)
                        rows_product(nc, PB[s], [(HT[s], m.wT["W1r"][:, :])], m.bias["b1"], m.ones_row, r
                                     ).then_inc(h1_ps, 1)
                    for s, g, r in slots:
                        pe.wait_ge(h1_pe, 1)
                        pe.sem_inc(h1_pe, -1)
                        turn(nc, PC[s], tiles(H1[s], r), m.ident, r).then_inc(t1, 1)
                    for s, g, r in slots:
                        pe.wait_ge(h1t, 1)
                        pe.sem_inc(h1t, -1)
                        rows_product(nc, PD[s], [(H1T[s], m.wT["W2r"][:, :])], m.bias["b2"], m.ones_row, r
                                     ).then_inc(y_ps, 1)
                    for s, g, r in slots:
                        pe.wait_ge(n1, 1)
                        pe.sem_inc(n1, -1)
                        turn(nc, PA[s], tiles(N1[s], r), m.ident, r).then_inc(t2, 1)
                    for s, g, r in slots:
                        pe.wait_ge(nt, 1)
                        pe.sem_inc(nt, -1)
                        rows_product(nc, PB[s], [(NT[s], m.wn["W"][:, :])], m.bias["b"], m.ones_row, r
                                     ).then_inc(xl_ps, 1)
                over_node_pairs(m, pe, body)

            @block.scalar
            def _(act):
                def body(slots):
                    for s, g, r in slots:
                        c = r * TILES
                        act.wait_ge(t0, 1)
                        act.sem_inc(t0, -1)
                        nc.scalar.activation(HT[s][:, 0:c], PA[s][:, 0:c], ACT.Relu).then_inc(ht, 1)
                    for s, g, r in slots:
                        act.wait_ge(h1_ps, 1)
                        act.sem_inc(h1_ps, -1)
                        act.wait_ge(h1_free, 1)
                        act.sem_inc(h1_free, -1)
                        nc.scalar.activation(H1[s][0:r, :], PB[s][0:r, :], ACT.Relu).then_inc(own_a, 1)
                        act.wait_ge(own_a, 1)
                        act.sem_inc(own_a, -1)
                        act.sem_inc(h1_pe, 1)
                        act.sem_inc(h1_out, 1)
                    for s, g, r in slots:
                        c = r * TILES
                        act.wait_ge(t1, 1)
                        act.sem_inc(t1, -1)
                        nc.scalar.activation(H1T[s][:, 0:c], PC[s][:, 0:c], ACT.Copy).then_inc(h1t, 1)
                    for s, g, r in slots:
                        act.wait_ge(y_ps, 1)
                        act.sem_inc(y_ps, -1)
                        nc.scalar.activation(Y[s][0:r, :], PD[s][0:r, :], ACT.Copy).then_inc(own_a, 1)
                        act.wait_ge(own_a, 1)
                        act.sem_inc(own_a, -1)
                        act.sem_inc(y_pool, 1)
                        act.sem_inc(y_dve, 1)
                    for s, g, r in slots:
                        c = r * TILES
                        act.wait_ge(t2, 1)
                        act.sem_inc(t2, -1)
                        nc.scalar.activation(NT[s][:, 0:c], PA[s][:, 0:c], ACT.Relu).then_inc(nt, 1)
                over_node_pairs(m, act, body)
        ph.retire()



def nodes_last(m):
    nc = m.nc
    with ExitStack() as ctx:
        ph = Phase(m, "f", ctx)
        X, AT = ph.two("x", [P, TILES, P]), ph.two("at", [P, TILES, P])
        N0, XM, N1, R, OUT = (ph.two(k, [P, ROWS]) for k in ["n0", "xm", "n1", "r", "out"])
        NT = ph.two("nt", [P, ROWS])
        HID = ph.two("hid", [P, 4, ROWS])
        ST, MV, VE, RS = ph.two("st", [P, 4, 6]), ph.two("mv", [P, 4, 2]), ph.two("ve", [P, 4]), ph.two("rs", [P, 4])
        PT, PO = ph.ps2("t"), ph.ps2("o")
        PH = [ph.ps(f"h{i}") for i in range(4)]
        x_in, saved = ph.sem2("x_in"), ph.sem2("saved")
        (x_free, ve, rs, xm_ready, n1, t0, nt, hid_ps, hid_free, hid, o_ps, out_ready, out_free, own_d,
         own_a) = (ph.sem(k) for k in ["x_free", "ve", "rs", "xm", "n1", "t0", "nt", "hid_ps", "hid_free", "hid",
                                       "o_ps", "out", "out_free", "own_d", "own_a"])

        with nc.Block() as block:
            @block.sync
            def _(sp):
                def load(slots):
                    for s, g, r in slots:
                        sp.wait_ge(x_free, 1)
                        sp.sem_inc(x_free, -1)
                        sp.dma_start(X[s][0:r, :, :], node_rows(m.x3, g, r)).then_inc(x_in[s], 16)
                        sp.dma_start(AT[s][0:r, :, :], node_rows(m.att, g, r)).then_inc(x_in[s], 16)

                def store(slots):
                    for s, g, r in slots:
                        sp.wait_ge(out_ready, 1)
                        sp.sem_inc(out_ready, -1)
                        sp.dma_start(node_rows(m.out, g, r), tiles(OUT[s], r)).then_inc(saved[s], 16)
                    for s, g, r in slots:
                        sp.wait_ge(saved[s], 16)
                        sp.sem_inc(saved[s], -16)
                        sp.sem_inc(out_free, 1)

                load([(0, 0, P), (1, 1, P)])
                with sp.Fori(0, m.node_pairs - 1) as i:
                    load([(0, 2 * i + 2, P), (1, 2 * i + 3, P)])
                    store([(0, 2 * i, P), (1, 2 * i + 1, P)])
                load(m.rest)
                store([(0, 2 * m.node_pairs - 2, P), (1, 2 * m.node_pairs - 1, P)])
                store(m.rest)

            @block.gpsimd
            def _(pool):
                def body(slots):
                    for n in range(2):
                        for s, g, r in slots:
                            pool.wait_ge(ve, 1)
                            pool.sem_inc(ve, -1)
                            nc.gpsimd.tensor_tensor(RS[s][0:r, :], VE[s][0:r, :], m.half[0:r, 0:4], ALU.pow
                                                    ).then_inc(rs, 1)
                over_node_pairs(m, pool, body)

            @block.vector
            def _(dve):
                ph.prime(dve, 2, x_free, out_free)
                ph.prime(dve, 4, hid_free)

                def body(slots):
                    for s, g, r in slots:
                        dve.wait_ge(x_in[s], 32)
                        dve.sem_inc(x_in[s], -32)
                        moments(nc, dve, own_d, [X[s][0:r, a, :] for a in range(4)], ST[s], MV[s], VE[s], r
                                ).then_inc(ve, 1)
                    for s, g, r in slots:
                        dve.wait_ge(rs, 1)
                        dve.sem_inc(rs, -1)
                        n = tiles(N0[s], r)
                        normalise(nc, [n[:, a, :] for a in range(4)], [X[s][0:r, a, :] for a in range(4)],
                                            MV[s], RS[s], r).then_inc(own_d, 1)
                        dve.wait_ge(own_d, 1)
                        dve.sem_inc(own_d, -1)
                        nc.vector.scalar_tensor_tensor(tiles(XM[s], r), n, 0.0, AT[s][0:r, :, :], ALU.max,
                                                                 ALU.add).then_inc(own_d, 1)
                        dve.wait_ge(own_d, 1)
                        dve.sem_inc(own_d, -1)
                        moments(nc, dve, own_d, [tiles(XM[s], r)[:, a, :] for a in range(4)], ST[s], MV[s], VE[s], r
                                ).then_inc(ve, 1)
                        nc.vector.tensor_tensor(tiles(R[s], r), X[s][0:r, :, :], tiles(XM[s], r), ALU.add
                                                ).then_inc(x_free, 1)
                    for s, g, r in slots:
                        dve.wait_ge(rs, 1)
                        dve.sem_inc(rs, -1)
                        n, xm = tiles(N1[s], r), tiles(XM[s], r)
                        normalise(nc, [n[:, a, :] for a in range(4)], [xm[:, a, :] for a in range(4)], MV[s],
                                  RS[s], r).then_inc(n1, 1)
                    for s, g, r in slots:
                        dve.wait_ge(o_ps, 1)
                        dve.sem_inc(o_ps, -1)
                        dve.wait_ge(out_free, 1)
                        dve.sem_inc(out_free, -1)
                        nc.vector.tensor_tensor(OUT[s][0:r, :], PO[s][0:r, :], R[s][0:r, :], ALU.add
                                                ).then_inc(out_ready, 1)
                over_node_pairs(m, dve, body)

            @block.tensor
            def _(pe):
                def body(slots):
                    for s, g, r in slots:
                        pe.wait_ge(n1, 1)
                        pe.sem_inc(n1, -1)
                        turn(nc, PT[s], tiles(N1[s], r), m.ident, r).then_inc(t0, 1)
                    for s, g, r in slots:
                        c = r * TILES
                        pe.wait_ge(nt, 1)
                        pe.sem_inc(nt, -1)
                        for h in range(4):
                            pe.wait_ge(hid_free, 1)
                            pe.sem_inc(hid_free, -1)
                            nc.tensor.matmul(PH[h][:, 0:c], m.W1[:, h * P:(h + 1) * P], NT[s][:, 0:c], start=True,
                                             stop=True).then_inc(hid_ps, 1)
                    for s, g, r in slots:
                        pe.wait_ge(hid, 1)
                        pe.sem_inc(hid, -1)
                        rows_product(nc, PO[s], [(HID[s][:, h, :], m.W2[:, h, :]) for h in range(4)], m.bias["bf2"],
                                     m.ones_row, r).then_inc(o_ps, 1)
                over_node_pairs(m, pe, body)

            @block.scalar
            def _(act):
                def body(slots):
                    for s, g, r in slots:
                        c = r * TILES
                        act.wait_ge(t0, 1)
                        act.sem_inc(t0, -1)
                        nc.scalar.activation(NT[s][:, 0:c], PT[s][:, 0:c], ACT.Copy).then_inc(nt, 1)
                    for s, g, r in slots:
                        c = r * TILES
                        for h in range(4):
                            act.wait_ge(hid_ps, 1)
                            act.sem_inc(hid_ps, -1)
                            one = nc.scalar.activation(HID[s][:, h, 0:c], PH[h][:, 0:c], ACT.Gelu,
                                                       bias=m.bf1[:, h:h + 1])
                            if h < 3:
                                one.then_inc(hid_free, 1)
                            else:
                                one.then_inc(own_a, 1)
                                act.wait_ge(own_a, 1)
                                act.sem_inc(own_a, -1)
                                act.sem_inc(hid_free, 1)
                                act.sem_inc(hid, 1)
                over_node_pairs(m, act, body)
        ph.retire()



def over_edge_pairs(m, eng, body):
    with eng.Fori(0, m.edge_pairs) as i:
        body(i, [(0, 2 * i), (1, 2 * i + 1)])


def row_of(v, g):
    return v[bass.ds(g * ROWS, ROWS)].rearrange("(o d) -> o d", o=1).broadcast_to([P, ROWS])


def edge_rows(table, g):
    return table[bass.ds(g * ROWS, ROWS), :].rearrange("(a p) d -> p a d", p=P)


class Sockets:

    def __init__(self, ph, gathers, scatter, adds=False):
        self.ph, self.m, self.gathers, self.scatter, self.adds = ph, ph.m, gathers, scatter, adds
        self.gi = ph.two("gi", [P, 8], I32)
        self.gi_in, self.gi_free, self.buf_free = ph.sem2("gi_in"), ph.sem("gi_free"), ph.sem("buf_free")
        self.got = [ph.counter(f"got{s}") for s in range(2)]
        self.ticks = ph.counter("ticks")
        if scatter:
            self.si = ph.two("si", [P, 4], I32)
            self.si_in, self.si_free = ph.sem2("si_in"), ph.sem("si_free")
            self.ready, self.out_free = ph.sem("sc_ready"), ph.sem("sc_free")
            self.put = [ph.counter(f"put{s}") for s in range(2)]
            self.si_made = ph.sem("si_made")
        self.each = 64 * len(gathers)

    def prime(self, eng):
        self.ph.prime(eng, 2, self.gi_free, self.buf_free)
        if self.scatter:
            self.ph.prime(eng, 2, self.si_free, self.out_free)

    def load_gather_idx(self, sp, source, slots):
        for s, g in slots:
            sp.wait_ge(self.gi_free, 1)
            sp.sem_inc(self.gi_free, -1)
            w = source.shape[2]
            sp.dma_start(self.gi[s][:, 0:w], source[:, bass.ds(g, 1), :].rearrange("p o w -> p (o w)")
                         ).then_inc(self.gi_in[s], 16)

    def load_scatter_idx(self, sp, slots):
        for s, g in slots:
            sp.wait_ge(self.si_free, 1)
            sp.sem_inc(self.si_free, -1)
            sp.dma_start(self.si[s][:, :], self.m.scatter_idx[:, bass.ds(g, 1), :].rearrange("p o w -> p (o w)")
                         ).then_inc(self.si_in[s], 16)

    def gather(self, pool, slots, bounds):
        nc = self.m.nc
        for s, g in slots:
            pool.wait_ge(self.buf_free, 1)
            pool.sem_inc(self.buf_free, -1)
            pool.wait_ge(self.gi_in[s], 16)
            pool.sem_inc(self.gi_in[s], -16)
            for table, buf, c in self.gathers:
                for a in range(TILES):
                    nc.gpsimd.indirect_dma_start(
                        buf[s][:, a, :], None, table,
                        bass.IndirectOffsetOnAxis(ap=self.gi[s][:, c + a:c + a + 1], axis=0),
                        bounds_check=bounds, oob_is_err=False).then_inc(self.got[s], 16)

    def free_gather_idx(self, pool, i, slots):
        for s, g in slots:
            pool.wait_ge(self.got[s], i * self.each + self.each)
            pool.sem_inc(self.ticks, 1)
            pool.sem_inc(self.gi_free, 1)

    def scatter_rows(self, pool, slots, bounds):
        nc = self.m.nc
        table, buf = self.scatter
        for s, g in slots:
            pool.wait_ge(self.ready, 1)
            pool.sem_inc(self.ready, -1)
            if self.adds:
                pool.wait_ge(self.si_made, 1)
                pool.sem_inc(self.si_made, -1)
            else:
                pool.wait_ge(self.si_in[s], 16)
                pool.sem_inc(self.si_in[s], -16)
            for a in range(TILES):
                where = bass.IndirectOffsetOnAxis(ap=self.si[s][:, a:a + 1], axis=0)
                if self.adds:
                    nc.gpsimd.indirect_dma_start(table, where, buf[s][:, a, :], None, bounds_check=bounds,
                                                 oob_is_err=True, compute_op=ALU.add).then_inc(self.put[s], 16)
                else:
                    nc.gpsimd.indirect_dma_start(table, where, buf[s][:, a, :], None, bounds_check=bounds,
                                                 oob_is_err=False).then_inc(self.put[s], 16)

    def scattered(self, pool, i, slots):
        for s, g in slots:
            pool.wait_ge(self.put[s], i * 64 + 64)
            pool.sem_inc(self.ticks, 1)
            pool.sem_inc(self.si_free, 1)
            pool.sem_inc(self.out_free, 1)

    def drive(self, pool, bounds_in, bounds_out, *between):
        m = self.m
        pairs = m.edge_pairs
        bi, bo = pool.to_reg(bounds_in), pool.to_reg(bounds_out)

        def turn_of(i, more):
            now, ahead = [(0, 2 * i), (1, 2 * i + 1)], [(0, 2 * i + 2), (1, 2 * i + 3)]
            self.free_gather_idx(pool, i, now)
            for work in between:
                work(now)
            if more:
                self.gather(pool, ahead, bi)
            if self.scatter and not self.adds:
                self.scatter_rows(pool, now, bo)
                self.scattered(pool, i, now)
            if self.adds:
                for one in now:
                    self.scatter_rows(pool, [one], bo)
                    self.scattered(pool, i, [one])

        self.gather(pool, [(0, 0), (1, 1)], bi)
        if pairs > 1:
            with pool.Fori(0, pairs - 1) as i:
                turn_of(i, True)
        turn_of(pairs - 1, False)


def segment_sum(nc, out, s, keep, cols):
    return nc.vector.tensor_tensor_scan(out[s][:, :], keep, cols, out[1 - s][:, ROWS - 1:ROWS], ALU.mult, ALU.add)


def finish_guard(nc, dve, own, y, pos, neg, fin):
    nc.vector.tensor_scalar(pos[:, :], y[:, :], 0.0, NAN_LIMIT, ALU.max, ALU.min)
    nc.vector.tensor_scalar(neg[:, :], y[:, :], 0.0, -NAN_LIMIT, ALU.min, ALU.max)
    nc.vector.tensor_scalar(fin[:, :], y[:, :], 0.0, 0.0, ALU.mult, ALU.is_equal).then_inc(own, 1)
    dve.wait_ge(own, 1)
    dve.sem_inc(own, -1)
    nc.vector.tensor_tensor(pos[:, :], pos[:, :], neg[:, :], ALU.add).then_inc(own, 1)
    dve.wait_ge(own, 1)
    dve.sem_inc(own, -1)
    nc.vector.copy_predicated(pos[:, :], fin[:, :], y[:, :]).then_inc(own, 1)
    dve.wait_ge(own, 1)
    dve.sem_inc(own, -1)



def sage_first(m):
    nc = m.nc
    x = m.ins["x"]
    m.h1_edge = m.dram("h1_edge", (m.EP, P))
    m.x_edge = m.dram("x_edge", (m.EP, P))
    m.att = m.dram("att", (m.N, P))
    with ExitStack() as ctx:
        ph = Phase(m, "s", ctx)
        XS, XD, N0, N1, H1 = (ph.two(k, [P, TILES, P]) for k in ["xs", "xd", "n0", "n1", "h1"])
        ST, MV, VE, RS = ph.two("st", [P, 8, 6]), ph.two("mv", [P, 8, 2]), ph.two("ve", [P, 8]), ph.two("rs", [P, 8])
        KEEP, RD = ph.two("keep", [P, ROWS], BF16), ph.two("rd", [P, ROWS])
        HS, HD, AG, MEAN = (ph.two(k, [P, ROWS]) for k in ["hs", "hd", "ag", "mean"])
        PA, PB, PC = ph.ps2("a"), ph.ps2("b"), ph.ps2("c")
        so = Sockets(ph, [(x, XS, 0), (x, XD, 4)], (m.h1, H1))
        row_in, saved = ph.sem2("row_in"), ph.sem2("saved")
        (row_free, ve, rs, n01, turned, hs, hd, mean, h1_ps, h1_out, h1_saved, xd_read, own_d, own_a) = (
            ph.sem(k) for k in [
             "row_free", "ve", "rs", "n01", "turned", "hs", "hd", "mean", "h1_ps", "h1_out", "h1_saved", "xd_read",
             "own_d", "own_a"])
        filled, tick_sp, tick_d = (ph.counter(k) for k in ["filled", "tick_sp", "tick_d"])
        parts = 5
        run = m.N // 32 // parts

        with nc.Block() as block:
            @block.sync
            def _(sp):
                def indices(slots):
                    so.load_gather_idx(sp, m.gather_idx, slots)

                def ahead(slots):
                    for s, g in slots:
                        sp.wait_ge(row_free, 1)
                        sp.sem_inc(row_free, -1)
                        sp.dma_start(KEEP[s][:, :], row_of(m.keep_row, g)).then_inc(row_in[s], 16)
                        sp.dma_start(RD[s][:, :], row_of(m.row["rdeg"], g)).then_inc(row_in[s], 16)

                def now(i, slots):
                    so.load_scatter_idx(sp, slots)
                    for s, g in slots:
                        sp.wait_ge(so.got[s], i * so.each + so.each)
                        sp.sem_inc(tick_sp, 1)
                        sp.dma_start(edge_rows(m.x_edge, g), XD[s][:, :, :]).then_inc(saved[s], 16)
                    for s, g in slots:
                        sp.wait_ge(saved[s], 16)
                        sp.sem_inc(saved[s], -16)
                        sp.sem_inc(xd_read, 1)

                def results(i, slots):
                    for s, g in slots:
                        sp.wait_ge(h1_out, 1)
                        sp.sem_inc(h1_out, -1)
                        sp.dma_start(edge_rows(m.h1_edge, g), H1[s][:, :, :]).then_inc(saved[s], 16)
                    for s, g in slots:
                        sp.wait_ge(saved[s], 16)
                        sp.sem_inc(saved[s], -16)
                        sp.sem_inc(h1_saved, 1)
                indices([(0, 0), (1, 1)])
                ahead([(0, 0), (1, 1)])
                with sp.Fori(0, m.edge_pairs - 1) as i:
                    now(i, [(0, 2 * i), (1, 2 * i + 1)])
                    indices([(0, 2 * i + 2), (1, 2 * i + 3)])
                    ahead([(0, 2 * i + 2), (1, 2 * i + 3)])
                    results(i, [(0, 2 * i), (1, 2 * i + 1)])
                now(m.edge_pairs - 1, [(0, m.G - 2), (1, m.G - 1)])
                results(m.edge_pairs - 1, [(0, m.G - 2), (1, m.G - 1)])

            @block.gpsimd
            def _(pool):
                def between(slots):
                    for s, g in slots:
                        pool.wait_ge(ve, 1)
                        pool.sem_inc(ve, -1)
                        nc.gpsimd.tensor_tensor(RS[s][:, :], VE[s][:, :], m.half[:, :], ALU.pow).then_inc(rs, 1)
                so.drive(pool, m.N - 1, m.N - 1, between)

            @block.vector
            def _(dve):
                so.prime(dve)
                ph.prime(dve, 2, row_free)
                ph.prime(dve, 2, h1_saved)
                nc.vector.memset(AG[1][:, ROWS - 1:ROWS], 0.0).then_inc(own_d, 1)
                dve.wait_ge(own_d, 1)
                dve.sem_inc(own_d, -1)

                def body(i, slots):
                    for s, g in slots:
                        dve.wait_ge(so.got[s], i * so.each + so.each)
                        dve.sem_inc(tick_d, 1)
                        moments(nc, dve, own_d, [b[s][:, a, :] for b in (XS, XD) for a in range(4)], ST[s], MV[s],
                                VE[s]).then_inc(ve, 1)
                    for s, g in slots:
                        dve.wait_ge(rs, 1)
                        dve.sem_inc(rs, -1)
                        normalise(nc, [b[s][:, a, :] for b in (N0, N1) for a in range(4)],
                                            [b[s][:, a, :] for b in (XS, XD) for a in range(4)], MV[s], RS[s]).then_inc(own_d, 1)
                        dve.wait_ge(own_d, 1)
                        dve.sem_inc(own_d, -1)
                        dve.sem_inc(n01, 1)
                        dve.wait_ge(xd_read, 1)
                        dve.sem_inc(xd_read, -1)
                        dve.sem_inc(so.buf_free, 1)
                    for s, g in slots:
                        dve.wait_ge(hs, 1)
                        dve.sem_inc(hs, -1)
                        dve.wait_ge(row_in[s], 32)
                        dve.sem_inc(row_in[s], -32)
                        segment_sum(nc, AG, s, KEEP[s][:, :], HS[s][:, :]).then_inc(own_d, 1)
                        dve.wait_ge(own_d, 1)
                        dve.sem_inc(own_d, -1)
                        nc.vector.tensor_tensor(MEAN[s][:, :], AG[s][:, :], RD[s][:, :], ALU.mult).then_inc(own_d, 1)
                        dve.wait_ge(own_d, 1)
                        dve.sem_inc(own_d, -1)
                        dve.sem_inc(mean, 1)
                        dve.sem_inc(row_free, 1)
                over_edge_pairs(m, dve, body)

            @block.tensor
            def _(pe):
                def body(i, slots):
                    for s, g in slots:
                        pe.wait_ge(n01, 1)
                        pe.sem_inc(n01, -1)
                        turn(nc, PA[s], N0[s], m.ident)
                        turn(nc, PB[s], N1[s], m.ident).then_inc(turned, 1)
                    for s, g in slots:
                        pe.wait_ge(hd, 1)
                        pe.sem_inc(hd, -1)
                        pe.wait_ge(mean, 1)
                        pe.sem_inc(mean, -1)
                        rows_product(nc, PC[s], [(MEAN[s], m.wT["W1l"][:, :]), (HD[s], m.wT["W1r"][:, :])],
                                     m.bias["b1"], m.ones_row).then_inc(h1_ps, 1)
                over_edge_pairs(m, pe, body)

            @block.scalar
            def _(act):
                for k in range(parts):
                    part = m.att[k * 32 * run:(k + 1) * 32 * run, :].rearrange("(p r) d -> p r d", p=32)
                    fill = m.bo_rows[:, :].rearrange("p (o d) -> p o d", o=1).broadcast_to([32, run, P])
                    act.dma_start(part, fill).then_inc(filled, 16)

                def body(i, slots):
                    for s, g in slots:
                        act.wait_ge(turned, 1)
                        act.sem_inc(turned, -1)
                        nc.scalar.activation(HS[s][:, :], PA[s][:, :], ACT.Relu).then_inc(hs, 1)
                        nc.scalar.activation(HD[s][:, :], PB[s][:, :], ACT.Relu).then_inc(hd, 1)
                    for s, g in slots:
                        act.wait_ge(h1_ps, 1)
                        act.sem_inc(h1_ps, -1)
                        act.wait_ge(h1_saved, 1)
                        act.sem_inc(h1_saved, -1)
                        act.wait_ge(so.out_free, 1)
                        act.sem_inc(so.out_free, -1)
                        nc.scalar.activation(H1[s][:, :, :].rearrange("p a d -> p (a d)"), PC[s][:, :],
                                                       ACT.Relu).then_inc(own_a, 1)
                        act.wait_ge(own_a, 1)
                        act.sem_inc(own_a, -1)
                        act.sem_inc(h1_out, 1)
                        act.sem_inc(so.ready, 1)
                over_edge_pairs(m, act, body)
                act.wait_ge(filled, 16 * parts)
        ph.retire()



def sage_second(m):
    nc = m.nc
    with ExitStack() as ctx:
        ph = Phase(m, "t", ctx)
        HS0, HD0, XD = (ph.two(k, [P, TILES, P]) for k in ["hs0", "hd0", "xd"])
        KEEP, RD = ph.two("keep", [P, ROWS], BF16), ph.two("rd", [P, ROWS])
        EC = ph.two("ec", [P, 8])
        HS, HD, AG, MEAN, Y, POS, NEG = (ph.two(k, [P, ROWS]) for k in ["hs", "hd", "ag", "mean", "y", "pos", "neg"])
        FIN = ph.two("fin", [P, ROWS], I32)
        X1 = ph.two("x1", [P, TILES, WIDE])
        PA, PB, PC = ph.ps2("a"), ph.ps2("b"), ph.ps2("c")
        so = Sockets(ph, [(m.h1, HS0, 0)], (m.x1, X1))
        row_in, x_in = ph.sem2("row_in"), ph.sem2("x_in")
        (row_free, x_free, turned, hs, hd, mean, y_ps, y, own_d, own_a) = (ph.sem(k) for k in [
            "row_free", "x_free", "turned", "hs", "hd", "mean", "y_ps", "y", "own_d", "own_a"])
        tick_pe = ph.counter("tick_pe")

        with nc.Block() as block:
            @block.sync
            def _(sp):
                def indices(slots):
                    so.load_gather_idx(sp, m.gather_idx, slots)

                def ahead(slots):
                    for s, g in slots:
                        sp.wait_ge(row_free, 1)
                        sp.sem_inc(row_free, -1)
                        sp.dma_start(KEEP[s][:, :], row_of(m.keep_row, g)).then_inc(row_in[s], 16)
                        sp.dma_start(RD[s][:, :], row_of(m.row["rdeg"], g)).then_inc(row_in[s], 16)
                    for s, g in slots:
                        sp.wait_ge(x_free, 1)
                        sp.sem_inc(x_free, -1)
                        sp.dma_start(HD0[s][:, :, :], edge_rows(m.h1_edge, g)).then_inc(x_in[s], 16)
                        sp.dma_start(XD[s][:, :, :], edge_rows(m.x_edge, g)).then_inc(x_in[s], 16)
                        sp.dma_start(EC[s][:, :], m.edge_col[:, bass.ds(g, 1), :].rearrange("p o w -> p (o w)")
                                     ).then_inc(x_in[s], 16)

                def now(i, slots):
                    so.load_scatter_idx(sp, slots)
                indices([(0, 0), (1, 1)])
                ahead([(0, 0), (1, 1)])
                with sp.Fori(0, m.edge_pairs - 1) as i:
                    now(i, [(0, 2 * i), (1, 2 * i + 1)])
                    indices([(0, 2 * i + 2), (1, 2 * i + 3)])
                    ahead([(0, 2 * i + 2), (1, 2 * i + 3)])
                now(m.edge_pairs - 1, [(0, m.G - 2), (1, m.G - 1)])

            @block.gpsimd
            def _(pool):
                so.drive(pool, m.N - 1, m.N - 1)

            @block.vector
            def _(dve):
                so.prime(dve)
                ph.prime(dve, 2, row_free)
                ph.prime(dve, 2, x_free)
                for s in range(2):
                    nc.vector.memset(X1[s][:, :, :], 1.0)
                nc.vector.memset(AG[1][:, ROWS - 1:ROWS], 0.0).then_inc(own_d, 1)
                dve.wait_ge(own_d, 1)
                dve.sem_inc(own_d, -1)

                def body(i, slots):
                    for s, g in slots:
                        dve.wait_ge(hs, 1)
                        dve.sem_inc(hs, -1)
                        dve.wait_ge(row_in[s], 32)
                        dve.sem_inc(row_in[s], -32)
                        segment_sum(nc, AG, s, KEEP[s][:, :], HS[s][:, :]).then_inc(own_d, 1)
                        dve.wait_ge(own_d, 1)
                        dve.sem_inc(own_d, -1)
                        nc.vector.tensor_tensor(MEAN[s][:, :], AG[s][:, :], RD[s][:, :], ALU.mult).then_inc(own_d, 1)
                        dve.wait_ge(own_d, 1)
                        dve.sem_inc(own_d, -1)
                        dve.sem_inc(mean, 1)
                        dve.sem_inc(row_free, 1)
                    for s, g in slots:
                        dve.wait_ge(y, 1)
                        dve.sem_inc(y, -1)
                        finish_guard(nc, dve, own_d, Y[s], POS[s], NEG[s], FIN[s])
                        dve.wait_ge(so.out_free, 1)
                        dve.sem_inc(so.out_free, -1)
                        nc.vector.tensor_copy(X1[s][:, :, P], EC[s][:, 0:4])
                        nc.vector.tensor_tensor(X1[s][:, :, 0:P], XD[s][:, :, :], tiles(POS[s]), ALU.add).then_inc(own_d, 1)
                        dve.wait_ge(own_d, 1)
                        dve.sem_inc(own_d, -1)
                        dve.sem_inc(so.ready, 1)
                        dve.sem_inc(x_free, 1)
                over_edge_pairs(m, dve, body)

            @block.tensor
            def _(pe):
                def body(i, slots):
                    for s, g in slots:
                        pe.wait_ge(so.got[s], i * so.each + so.each)
                        pe.sem_inc(tick_pe, 1)
                        pe.wait_ge(x_in[s], 48)
                        pe.sem_inc(x_in[s], -48)
                        turn(nc, PA[s], HS0[s], m.ident)
                        turn(nc, PB[s], HD0[s], m.ident).then_inc(turned, 1)
                    for s, g in slots:
                        pe.wait_ge(hd, 1)
                        pe.sem_inc(hd, -1)
                        pe.wait_ge(mean, 1)
                        pe.sem_inc(mean, -1)
                        rows_product(nc, PC[s], [(MEAN[s], m.wT["W2l"][:, :]), (HD[s], m.wT["W2r"][:, :])],
                                     m.bias["b2"], m.ones_row).then_inc(y_ps, 1)
                over_edge_pairs(m, pe, body)

            @block.scalar
            def _(act):
                def body(i, slots):
                    for s, g in slots:
                        act.wait_ge(turned, 1)
                        act.sem_inc(turned, -1)
                        act.sem_inc(so.buf_free, 1)
                        nc.scalar.activation(HS[s][:, :], PA[s][:, :], ACT.Copy).then_inc(hs, 1)
                        nc.scalar.activation(HD[s][:, :], PB[s][:, :], ACT.Copy).then_inc(hd, 1)
                    for s, g in slots:
                        act.wait_ge(y_ps, 1)
                        act.sem_inc(y_ps, -1)
                        nc.scalar.activation(Y[s][:, :], PC[s][:, :], ACT.Copy).then_inc(y, 1)
                over_edge_pairs(m, act, body)
        ph.retire()



class Online:

    def __init__(self, ph):
        self.nc = ph.m.nc
        self.M = ph.two("m", [P, 1 + ROWS])
        self.D, self.W, self.V, self.Z, self.S = (ph.two(k, [P, ROWS]) for k in ["d", "w", "v", "z", "s"])
        self.diffs, self.exps = ph.sem("diffs"), ph.sem("exps")

    def start(self, dve, own):
        nc = self.nc
        for t in (self.M[0][:, 0:1], self.M[1][:, ROWS:ROWS + 1], self.Z[1][:, ROWS - 1:ROWS],
                  self.S[1][:, ROWS - 1:ROWS]):
            last = nc.vector.memset(t, 0.0)
        last.then_inc(own, 1)
        dve.wait_ge(own, 1)
        dve.sem_inc(own, -1)

    def maxima(self, dve, own, s, scores, neg, keep=None):
        nc, M, D, W = self.nc, self.M, self.D, self.W
        nc.vector.tensor_copy(M[s][:, 0:1], M[1 - s][:, ROWS:ROWS + 1])
        before = M[1 - s][:, ROWS:ROWS + 1]
        if keep is None:
            one = nc.vector.tensor_tensor_scan(M[s][:, 1:], neg, scores, before, ALU.add, ALU.max)
        else:
            one = nc.vector.tensor_tensor_scan(M[s][:, 1:], keep, scores, before, ALU.mult, ALU.max)
        one.then_inc(own, 1)
        dve.wait_ge(own, 1)
        dve.sem_inc(own, -1)
        nc.vector.tensor_tensor(D[s][:, :], M[s][:, 0:ROWS], M[s][:, 1:], ALU.subtract).then_inc(own, 1)
        dve.wait_ge(own, 1)
        dve.sem_inc(own, -1)
        nc.vector.tensor_tensor(D[s][:, :], D[s][:, :], neg, ALU.min)
        nc.vector.tensor_tensor(W[s][:, :], scores, M[s][:, 1:], ALU.subtract).then_inc(self.diffs, 1)

    def exponentials(self, act, s):
        act.wait_ge(self.diffs, 1)
        act.sem_inc(self.diffs, -1)
        self.nc.scalar.activation(self.D[s][:, :], self.D[s][:, :], ACT.Exp)
        return self.nc.scalar.activation(self.W[s][:, :], self.W[s][:, :], ACT.Exp)

    def sums(self, dve, own, s, values):
        nc, Z, S = self.nc, self.Z, self.S
        dve.wait_ge(self.exps, 1)
        dve.sem_inc(self.exps, -1)
        nc.vector.tensor_tensor(self.V[s][:, :], self.W[s][:, :], values, ALU.mult).then_inc(own, 1)
        dve.wait_ge(own, 1)
        dve.sem_inc(own, -1)
        nc.vector.tensor_tensor_scan(Z[s][:, :], self.D[s][:, :], self.W[s][:, :], Z[1 - s][:, ROWS - 1:ROWS],
                                     ALU.mult, ALU.add)
        nc.vector.tensor_tensor_scan(S[s][:, :], self.D[s][:, :], self.V[s][:, :],
                                               S[1 - s][:, ROWS - 1:ROWS], ALU.mult, ALU.add).then_inc(own, 1)
        dve.wait_ge(own, 1)
        dve.sem_inc(own, -1)



def gat(m):
    nc = m.nc
    m.xl_edge = m.dram("xl_edge", (m.EP, P))
    m.dis_src = m.dram("dis_src", (P, m.G, 4))
    with ExitStack() as ctx:
        ph = Phase(m, "g", ctx)
        XS, XD = ph.two("xs", [P, TILES, WIDE]), ph.two("xd", [P, TILES, WIDE])
        N0, N1 = ph.two("n0", [P, TILES, P]), ph.two("n1", [P, TILES, P])
        ST, MV, VE, RS = ph.two("st", [P, 8, 6]), ph.two("mv", [P, 8, 2]), ph.two("ve", [P, 8]), ph.two("rs", [P, 8])
        NEG = ph.two("neg", [P, ROWS], BF16)
        EC, DS = ph.two("ec", [P, 8]), ph.two("ds", [P, 4])
        HS, HD, FS, E1, E2 = (ph.two(k, [P, ROWS]) for k in ["hs", "hd", "fs", "e1", "e2"])
        X2, XL, X3 = (ph.two(k, [P, TILES, P]) for k in ["x2", "xl", "x3"])
        on = Online(ph)
        PA, PB, PC, PD = ph.ps2("a"), ph.ps2("b"), ph.ps2("c"), ph.ps2("d")
        so = Sockets(ph, [(m.x1, XS, 0), (m.x1, XD, 4)], (m.x3, X3))
        row_in, saved = ph.sem2("row_in"), ph.sem2("saved")
        (row_free, ve, rs, n01, turned, hs, hd, proj, e1, e2, score, h_out, h_ps, n2, t2, h2, xl_ps, xl_out, xl_saved,
         own_d) = (ph.sem(k) for k in [
             "row_free", "ve", "rs", "n01", "turned", "hs", "hd", "proj", "e1", "e2", "score", "h_out", "h_ps", "n2",
             "t2", "h2", "xl_ps", "xl_out", "xl_saved", "own_d"])
        tick_d = ph.counter("tick_d")

        with nc.Block() as block:
            @block.sync
            def _(sp):
                def indices(slots):
                    so.load_gather_idx(sp, m.gather_idx, slots)

                def ahead(slots):
                    for s, g in slots:
                        sp.wait_ge(row_free, 1)
                        sp.sem_inc(row_free, -1)
                        sp.dma_start(NEG[s][:, :], row_of(m.neg_row, g)).then_inc(row_in[s], 16)
                        sp.dma_start(EC[s][:, :], m.edge_col[:, bass.ds(g, 1), :].rearrange("p o w -> p (o w)")
                                     ).then_inc(row_in[s], 16)

                def now(i, slots):
                    so.load_scatter_idx(sp, slots)

                def results(i, slots):
                    for s, g in slots:
                        sp.wait_ge(xl_out, 1)
                        sp.sem_inc(xl_out, -1)
                        sp.dma_start(edge_rows(m.xl_edge, g), XL[s][:, :, :]).then_inc(saved[s], 16)
                        sp.dma_start(m.dis_src[:, bass.ds(g, 1), :].rearrange("p o w -> p (o w)"), DS[s][:, :]
                                     ).then_inc(saved[s], 16)
                    for s, g in slots:
                        sp.wait_ge(saved[s], 32)
                        sp.sem_inc(saved[s], -32)
                        sp.sem_inc(xl_saved, 1)
                indices([(0, 0), (1, 1)])
                ahead([(0, 0), (1, 1)])
                with sp.Fori(0, m.edge_pairs - 1) as i:
                    now(i, [(0, 2 * i), (1, 2 * i + 1)])
                    indices([(0, 2 * i + 2), (1, 2 * i + 3)])
                    results(i, [(0, 2 * i), (1, 2 * i + 1)])
                    ahead([(0, 2 * i + 2), (1, 2 * i + 3)])
                now(m.edge_pairs - 1, [(0, m.G - 2), (1, m.G - 1)])
                results(m.edge_pairs - 1, [(0, m.G - 2), (1, m.G - 1)])

            @block.gpsimd
            def _(pool):
                def between(slots):
                    for s, g in slots:
                        pool.wait_ge(ve, 1)
                        pool.sem_inc(ve, -1)
                        nc.gpsimd.tensor_tensor(RS[s][:, :], VE[s][:, :], m.half[:, :], ALU.pow).then_inc(rs, 1)

                def later(slots):
                    for s, g in slots:
                        pool.wait_ge(ve, 1)
                        pool.sem_inc(ve, -1)
                        nc.gpsimd.tensor_tensor(RS[s][:, 0:4], VE[s][:, 0:4], m.half[:, 0:4], ALU.pow).then_inc(rs, 1)
                so.drive(pool, m.N - 1, m.N - 1, between, later)

            @block.vector
            def _(dve):
                so.prime(dve)
                ph.prime(dve, 2, row_free)
                ph.prime(dve, 2, xl_saved)
                on.start(dve, own_d)

                def body(i, slots):
                    for s, g in slots:
                        dve.wait_ge(so.got[s], i * so.each + so.each)
                        dve.sem_inc(tick_d, 1)
                        moments(nc, dve, own_d, [b[s][:, a, 0:P] for b in (XS, XD) for a in range(4)], ST[s], MV[s],
                                VE[s]).then_inc(ve, 1)
                    for s, g in slots:
                        dve.wait_ge(rs, 1)
                        dve.sem_inc(rs, -1)
                        normalise(nc, [b[s][:, a, :] for b in (N0, N1) for a in range(4)],
                                  [b[s][:, a, 0:P] for b in (XS, XD) for a in range(4)], MV[s], RS[s]
                                  ).then_inc(n01, 1)
                    for s, g in slots:
                        dve.wait_ge(e1, 1)
                        dve.sem_inc(e1, -1)
                        nc.vector.scalar_tensor_tensor(E2[s][:, :], E1[s][:, :], 0.2, E1[s][:, :], ALU.mult, ALU.max
                                                       ).then_inc(e2, 1)
                    for s, g in slots:
                        dve.wait_ge(score, 1)
                        dve.sem_inc(score, -1)
                        dve.wait_ge(row_in[s], 32)
                        dve.sem_inc(row_in[s], -32)
                        on.maxima(dve, own_d, s, PD[s][:, :], NEG[s][:, :])
                    for s, g in slots:
                        on.sums(dve, own_d, s, FS[s][:, :])
                        nc.vector.reciprocal(on.V[s][:, :], on.Z[s][:, :]).then_inc(own_d, 1)
                        dve.wait_ge(own_d, 1)
                        dve.sem_inc(own_d, -1)
                        nc.vector.tensor_tensor(on.V[s][:, :], on.S[s][:, :], on.V[s][:, :], ALU.mult
                                                ).then_inc(h_out, 1)
                    for s, g in slots:
                        dve.wait_ge(h_ps, 1)
                        dve.sem_inc(h_ps, -1)
                        nc.vector.scalar_tensor_tensor(X2[s][:, :, :], tiles(PA[s]), 0.0, XD[s][:, :, 0:P],
                                                                 ALU.max, ALU.add).then_inc(own_d, 1)
                        dve.wait_ge(own_d, 1)
                        dve.sem_inc(own_d, -1)
                        moments(nc, dve, own_d, [X2[s][:, a, :] for a in range(4)], ST[s], MV[s], VE[s][:, 0:4]
                                ).then_inc(ve, 1)
                        dve.wait_ge(xl_saved, 1)
                        dve.sem_inc(xl_saved, -1)
                        nc.vector.tensor_copy(DS[s][:, :], XS[s][:, :, P]).then_inc(own_d, 1)
                        dve.wait_ge(own_d, 1)
                        dve.sem_inc(own_d, -1)
                        dve.sem_inc(so.buf_free, 1)
                    for s, g in slots:
                        dve.wait_ge(rs, 1)
                        dve.sem_inc(rs, -1)
                        normalise(nc, [N0[s][:, a, :] for a in range(4)], [X2[s][:, a, :] for a in range(4)], MV[s],
                                  RS[s]).then_inc(n2, 1)
                    for s, g in slots:
                        dve.wait_ge(xl_ps, 1)
                        dve.sem_inc(xl_ps, -1)
                        for a in range(4):
                            last = nc.vector.tensor_scalar(XL[s][:, a, :], PB[s][:, a * P:(a + 1) * P],
                                                           EC[s][:, a:a + 1], None, ALU.mult)
                        last.then_inc(own_d, 1)
                        dve.wait_ge(own_d, 1)
                        dve.sem_inc(own_d, -1)
                        dve.sem_inc(xl_out, 1)
                        dve.wait_ge(so.out_free, 1)
                        dve.sem_inc(so.out_free, -1)
                        for a in range(4):
                            last = nc.vector.scalar_tensor_tensor(X3[s][:, a, :], XL[s][:, a, :], EC[s][:, a:a + 1],
                                                                  X2[s][:, a, :], ALU.mult, ALU.add)
                        last.then_inc(own_d, 1)
                        dve.wait_ge(own_d, 1)
                        dve.sem_inc(own_d, -1)
                        dve.sem_inc(so.ready, 1)
                        dve.sem_inc(row_free, 1)
                over_edge_pairs(m, dve, body)

            @block.tensor
            def _(pe):
                def body(i, slots):
                    for s, g in slots:
                        pe.wait_ge(n01, 1)
                        pe.sem_inc(n01, -1)
                        turn(nc, PA[s], N0[s], m.ident)
                        turn(nc, PB[s], N1[s], m.ident).then_inc(turned, 1)
                    for s, g in slots:
                        pe.wait_ge(hs, 1)
                        pe.sem_inc(hs, -1)
                        pe.wait_ge(hd, 1)
                        pe.sem_inc(hd, -1)
                        nc.tensor.matmul(PC[s][:, :], m.wn["Ws"][:, :], HS[s][:, :], start=True, stop=True)
                        nc.tensor.matmul(PD[s][:, :], m.wn["Ws"][:, :], HS[s][:, :], start=True, stop=False)
                        nc.tensor.matmul(PD[s][:, :], m.wn["Wd"][:, :], HD[s][:, :], start=False, stop=True
                                         ).then_inc(proj, 1)
                    for s, g in slots:
                        pe.wait_ge(e2, 1)
                        pe.sem_inc(e2, -1)
                        nc.tensor.matmul(PD[s][:, :], m.attn_heads[:, :], E2[s][:, :], start=True, stop=True
                                         ).then_inc(score, 1)
                    for s, g in slots:
                        pe.wait_ge(h_out, 1)
                        pe.sem_inc(h_out, -1)
                        turn(nc, PA[s], tiles(on.V[s]), m.ident).then_inc(h_ps, 1)
                    for s, g in slots:
                        pe.wait_ge(n2, 1)
                        pe.sem_inc(n2, -1)
                        turn(nc, PC[s], N0[s], m.ident).then_inc(t2, 1)
                    for s, g in slots:
                        pe.wait_ge(h2, 1)
                        pe.sem_inc(h2, -1)
                        rows_product(nc, PB[s], [(HD[s], m.wn["W"][:, :])], m.bias["b"], m.ones_row
                                     ).then_inc(xl_ps, 1)
                over_edge_pairs(m, pe, body)

            @block.scalar
            def _(act):
                def body(i, slots):
                    for s, g in slots:
                        act.wait_ge(turned, 1)
                        act.sem_inc(turned, -1)
                        nc.scalar.activation(HS[s][:, :], PA[s][:, :], ACT.Relu).then_inc(hs, 1)
                        nc.scalar.activation(HD[s][:, :], PB[s][:, :], ACT.Relu).then_inc(hd, 1)
                    for s, g in slots:
                        act.wait_ge(proj, 1)
                        act.sem_inc(proj, -1)
                        nc.scalar.activation(FS[s][:, :], PC[s][:, :], ACT.Identity, bias=m.col["bs"][:, :])
                        nc.scalar.activation(E1[s][:, :], PD[s][:, :], ACT.Identity, bias=m.col["bsd"][:, :]
                                             ).then_inc(e1, 1)
                    for s, g in slots:
                        on.exponentials(act, s).then_inc(on.exps, 1)
                    for s, g in slots:
                        act.wait_ge(t2, 1)
                        act.sem_inc(t2, -1)
                        nc.scalar.activation(HD[s][:, :], PC[s][:, :], ACT.Relu).then_inc(h2, 1)
                over_edge_pairs(m, act, body)
        ph.retire()



def gcn(m):
    nc = m.nc
    with ExitStack() as ctx:
        ph = Phase(m, "l", ctx)
        XL, MS, OUT = (ph.two(k, [P, TILES, P]) for k in ["xl", "ms", "out"])
        KEYS = ph.two("keys", [P, ROWS])
        EC, DS = ph.two("ec", [P, 8]), ph.two("ds", [P, 4])
        EQ = ph.two("eq", [P, TILES, ROWS])
        LATER = ph.sb("later", [P, TILES, ROWS])
        SCR = ph.two("scr", [P, TILES, ROWS])
        CNT, DF, SEL = ph.two("cnt", [P, 4]), ph.two("df", [P, 4]), ph.two("sel", [P, 4])
        TRASH, TRASHI = ph.sb("trash", [P, 4]), ph.sb("trashi", [P, 4], I32)
        PA = ph.ps2("a")
        so = Sockets(ph, [(m.xl_edge, XL, 0)], (m.x3, OUT), adds=True)
        row_in = ph.sem2("row_in")
        row_free, ms, sums, later, own_d, own_a, own_p, eq_free = (ph.sem(k) for k in [
            "row_free", "ms", "sums", "later", "own_d", "own_a", "own_p", "eq_free"])
        tick_d = ph.counter("tick_d")

        with nc.Block() as block:
            @block.sync
            def _(sp):
                def indices(slots):
                    so.load_gather_idx(sp, m.last_idx, slots)

                def ahead(slots):
                    for s, g in slots:
                        sp.wait_ge(row_free, 1)
                        sp.sem_inc(row_free, -1)
                        sp.dma_start(KEYS[s][:, :], row_of(m.row["key"], g)).then_inc(row_in[s], 16)
                        sp.dma_start(EC[s][:, :], m.edge_col[:, bass.ds(g, 1), :].rearrange("p o w -> p (o w)")
                                     ).then_inc(row_in[s], 16)
                        sp.dma_start(DS[s][:, :], m.dis_src[:, bass.ds(g, 1), :].rearrange("p o w -> p (o w)")
                                     ).then_inc(row_in[s], 16)
                indices([(0, 0), (1, 1)])
                ahead([(0, 0), (1, 1)])
                with sp.Fori(0, m.edge_pairs - 1) as i:
                    indices([(0, 2 * i + 2), (1, 2 * i + 3)])
                    ahead([(0, 2 * i + 2), (1, 2 * i + 3)])

            @block.gpsimd
            def _(pool):
                nc.gpsimd.iota(TRASHI[:, :], pattern=[[P, 4]], base=m.N + 1, channel_multiplier=1)
                nc.gpsimd.memset(LATER[:, :, :], 1.0).then_inc(own_p, 1)
                pool.wait_ge(own_p, 1)
                pool.sem_inc(own_p, -1)
                nc.gpsimd.affine_select(out=LATER[:, :, :], in_=LATER[:, :, :], compare_op=ALU.is_ge, fill=0.0,
                                        base=-1, pattern=[[-P, TILES], [1, ROWS]], channel_multiplier=-1
                                        ).then_inc(own_p, 1)
                pool.wait_ge(own_p, 1)
                pool.sem_inc(own_p, -1)
                pool.sem_inc(later, 1)
                so.drive(pool, m.EP - 1, m.N + 2 * ROWS - 1)

            @block.vector
            def _(dve):
                so.prime(dve)
                ph.prime(dve, 2, row_free)
                ph.prime(dve, 2, eq_free)
                dve.wait_ge(later, 1)
                dve.sem_inc(later, -1)
                nc.vector.tensor_copy(TRASH[:, :], TRASHI[:, :]).then_inc(own_d, 1)
                dve.wait_ge(own_d, 1)
                dve.sem_inc(own_d, -1)

                def body(i, slots):
                    for s, g in slots:
                        dve.wait_ge(row_in[s], 48)
                        dve.sem_inc(row_in[s], -48)
                        dve.wait_ge(eq_free, 1)
                        dve.sem_inc(eq_free, -1)
                        for a in range(TILES):
                            nc.vector.tensor_scalar(EQ[s][:, a, :], KEYS[s][:, :], EC[s][:, 4 + a:5 + a], None,
                                                    ALU.is_equal)
                        nc.vector.tensor_tensor(DF[s][:, :], TRASH[:, :], EC[s][:, 4:8], ALU.subtract)
                        dve.wait_ge(so.got[s], i * so.each + so.each)
                        dve.sem_inc(tick_d, 1)
                        for a in range(TILES):
                            last = nc.vector.tensor_scalar(MS[s][:, a, :], XL[s][:, a, :], DS[s][:, a:a + 1], None,
                                                           ALU.mult)
                        last.then_inc(own_d, 1)
                        dve.wait_ge(own_d, 1)
                        dve.sem_inc(own_d, -1)
                        dve.sem_inc(ms, 1)
                        dve.sem_inc(so.buf_free, 1)
                    for s, g in slots:
                        for a in range(TILES):
                            last = nc.vector.scalar_tensor_tensor(SCR[s][:, a, :], EQ[s][:, a, :], 1.0, LATER[:, a, :],
                                                                  ALU.mult, ALU.mult, accum_out=CNT[s][:, a:a + 1])
                        last.then_inc(own_d, 1)
                        dve.wait_ge(own_d, 1)
                        dve.sem_inc(own_d, -1)
                        nc.vector.tensor_scalar(SEL[s][:, :], CNT[s][:, :], 1.0, None, ALU.min).then_inc(own_d, 1)
                        dve.wait_ge(own_d, 1)
                        dve.sem_inc(own_d, -1)
                        nc.vector.tensor_tensor(SEL[s][:, :], SEL[s][:, :], DF[s][:, :], ALU.mult).then_inc(own_d, 1)
                        dve.wait_ge(own_d, 1)
                        dve.sem_inc(own_d, -1)
                        dve.wait_ge(so.si_free, 1)
                        dve.sem_inc(so.si_free, -1)
                        nc.vector.tensor_tensor(so.si[s][:, :], SEL[s][:, :], EC[s][:, 4:8], ALU.add).then_inc(own_d, 1)
                        dve.wait_ge(own_d, 1)
                        dve.sem_inc(own_d, -1)
                        dve.sem_inc(so.si_made, 1)
                        dve.sem_inc(row_free, 1)
                over_edge_pairs(m, dve, body)

            @block.tensor
            def _(pe):
                def body(i, slots):
                    for s, g in slots:
                        pe.wait_ge(ms, 1)
                        pe.sem_inc(ms, -1)
                        for b in range(TILES):
                            for a in range(TILES):
                                last = nc.tensor.matmul(PA[s][:, b * P:(b + 1) * P], EQ[s][:, a, b * P:(b + 1) * P],
                                                        MS[s][:, a, :], start=(a == 0), stop=(a == TILES - 1))
                        last.then_inc(sums, 1)
                over_edge_pairs(m, pe, body)

            @block.scalar
            def _(act):
                def body(i, slots):
                    for s, g in slots:
                        act.wait_ge(sums, 1)
                        act.sem_inc(sums, -1)
                        act.wait_ge(so.out_free, 1)
                        act.sem_inc(so.out_free, -1)
                        nc.scalar.activation(OUT[s][:, :, :].rearrange("p a d -> p (a d)"), PA[s][:, :],
                                                       ACT.Copy).then_inc(own_a, 1)
                        act.wait_ge(own_a, 1)
                        act.sem_inc(own_a, -1)
                        act.sem_inc(so.ready, 1)
                        act.sem_inc(eq_free, 1)
                over_edge_pairs(m, act, body)
        ph.retire()



def attention(m):
    nc = m.nc
    with ExitStack() as ctx:
        ph = Phase(m, "a", ctx)
        XS, XD, N0, N1 = (ph.two(k, [P, TILES, P]) for k in ["xs", "xd", "n0", "n1"])
        ST, MV, VE, RS = ph.two("st", [P, 8, 6]), ph.two("mv", [P, 8, 2]), ph.two("ve", [P, 8]), ph.two("rs", [P, 8])
        KEEP, NEG = ph.two("keep", [P, ROWS], BF16), ph.two("neg", [P, ROWS], BF16)
        ND, DIF, Q, PR, E0 = (ph.two(k, [P, ROWS]) for k in ["nd", "dif", "q", "pr", "e0"])
        AO = ph.two("ao", [P, TILES, P])
        on = Online(ph)
        PA, PB, PC, PD = ph.ps2("a"), ph.ps2("b"), ph.ps2("c"), ph.ps2("d")
        so = Sockets(ph, [(m.x3[0:m.N, :], XS, 0), (m.x3[0:m.N, :], XD, 4)], (m.att, AO))
        row_in = ph.sem2("row_in")
        (row_free, ve, rs, n01, turned, nd, dif, qk, q, pr, score, agg, ao_ps, own_d) = (
            ph.sem(k) for k in ["row_free", "ve", "rs", "n01", "turned", "nd", "dif", "qk", "q", "pr", "score",
                                "agg", "ao_ps", "own_d"])
        tick_d = ph.counter("tick_d")

        with nc.Block() as block:
            @block.sync
            def _(sp):
                def indices(slots):
                    so.load_gather_idx(sp, m.gather_idx, slots)

                def ahead(slots):
                    for s, g in slots:
                        sp.wait_ge(row_free, 1)
                        sp.sem_inc(row_free, -1)
                        sp.dma_start(NEG[s][:, :], row_of(m.neg_row, g)).then_inc(row_in[s], 16)
                        sp.dma_start(KEEP[s][:, :], row_of(m.keep_row, g)).then_inc(row_in[s], 16)

                def now(i, slots):
                    so.load_scatter_idx(sp, slots)
                indices([(0, 0), (1, 1)])
                ahead([(0, 0), (1, 1)])
                with sp.Fori(0, m.edge_pairs - 1) as i:
                    now(i, [(0, 2 * i), (1, 2 * i + 1)])
                    indices([(0, 2 * i + 2), (1, 2 * i + 3)])
                    ahead([(0, 2 * i + 2), (1, 2 * i + 3)])
                now(m.edge_pairs - 1, [(0, m.G - 2), (1, m.G - 1)])

            @block.gpsimd
            def _(pool):
                def between(slots):
                    for n in range(2):
                        for s, g in slots:
                            pool.wait_ge(ve, 1)
                            pool.sem_inc(ve, -1)
                            nc.gpsimd.tensor_tensor(RS[s][:, :], VE[s][:, :], m.half[:, :], ALU.pow).then_inc(rs, 1)
                so.drive(pool, m.N - 1, m.N - 1, between)

            @block.vector
            def _(dve):
                so.prime(dve)
                ph.prime(dve, 2, row_free)
                on.start(dve, own_d)

                def body(i, slots):
                    for s, g in slots:
                        dve.wait_ge(so.got[s], i * so.each + so.each)
                        dve.sem_inc(tick_d, 1)
                        moments(nc, dve, own_d, [b[s][:, a, :] for b in (XS, XD) for a in range(4)], ST[s], MV[s],
                                VE[s]).then_inc(ve, 1)
                    for s, g in slots:
                        dve.wait_ge(rs, 1)
                        dve.sem_inc(rs, -1)
                        both = [b[s][:, a, :] for b in (N0, N1) for a in range(4)]
                        normalise(nc, both, [b[s][:, a, :] for b in (XS, XD) for a in range(4)], MV[s],
                                            RS[s]).then_inc(own_d, 1)
                        dve.wait_ge(own_d, 1)
                        dve.sem_inc(own_d, -1)
                        dve.sem_inc(so.buf_free, 1)
                        for b in (N0, N1):
                            one = nc.vector.tensor_scalar(b[s][:, :, :], b[s][:, :, :], 0.0, None, ALU.max)
                        one.then_inc(own_d, 1)
                        dve.wait_ge(own_d, 1)
                        dve.sem_inc(own_d, -1)
                        moments(nc, dve, own_d, both, ST[s], MV[s], VE[s]).then_inc(ve, 1)
                    for s, g in slots:
                        dve.wait_ge(rs, 1)
                        dve.sem_inc(rs, -1)
                        both = [b[s][:, a, :] for b in (N0, N1) for a in range(4)]
                        normalise(nc, both, both, MV[s], RS[s]).then_inc(n01, 1)
                    for s, g in slots:
                        dve.wait_ge(nd, 1)
                        dve.sem_inc(nd, -1)
                        nc.vector.tensor_tensor(DIF[s][:, :], PA[s][:, :], ND[s][:, :], ALU.subtract
                                                ).then_inc(dif, 1)
                    for s, g in slots:
                        dve.wait_ge(q, 1)
                        dve.sem_inc(q, -1)
                        nc.vector.tensor_tensor(PR[s][:, :], PD[s][:, :], Q[s][:, :], ALU.mult).then_inc(pr, 1)
                    for s, g in slots:
                        dve.wait_ge(score, 1)
                        dve.sem_inc(score, -1)
                        dve.wait_ge(row_in[s], 32)
                        dve.sem_inc(row_in[s], -32)
                        on.maxima(dve, own_d, s, PC[s][:, :], NEG[s][:, :], KEEP[s][:, :])
                    for s, g in slots:
                        on.sums(dve, own_d, s, PA[s][:, :])
                        nc.vector.tensor_tensor(on.V[s][:, :], on.Z[s][:, :], E0[s][:, :], ALU.add).then_inc(own_d, 1)
                        dve.wait_ge(own_d, 1)
                        dve.sem_inc(own_d, -1)
                        nc.vector.reciprocal(on.V[s][:, :], on.V[s][:, :]).then_inc(own_d, 1)
                        dve.wait_ge(own_d, 1)
                        dve.sem_inc(own_d, -1)
                        nc.vector.tensor_tensor(on.V[s][:, :], on.V[s][:, :], on.S[s][:, :], ALU.mult).then_inc(own_d, 1)
                        dve.wait_ge(own_d, 1)
                        dve.sem_inc(own_d, -1)
                        nc.vector.scalar_tensor_tensor(on.V[s][:, :], PB[s][:, :], m.col["bv"][:, :],
                                                                 on.V[s][:, :], ALU.add, ALU.add).then_inc(own_d, 1)
                        dve.wait_ge(own_d, 1)
                        dve.sem_inc(own_d, -1)
                        dve.sem_inc(agg, 1)
                        dve.sem_inc(row_free, 1)
                over_edge_pairs(m, dve, body)

            @block.tensor
            def _(pe):
                def body(i, slots):
                    for s, g in slots:
                        pe.wait_ge(n01, 1)
                        pe.sem_inc(n01, -1)
                        turn(nc, PA[s], N0[s], m.ident)
                        turn(nc, PB[s], N1[s], m.ident).then_inc(turned, 1)
                    for s, g in slots:
                        pe.wait_ge(dif, 1)
                        pe.sem_inc(dif, -1)
                        nc.tensor.matmul(PC[s][:, :], m.wn["Wq"][:, :], ND[s][:, :], start=True, stop=True)
                        nc.tensor.matmul(PD[s][:, :], m.wn["Wk"][:, :], DIF[s][:, :], start=True, stop=True
                                         ).then_inc(qk, 1)
                        nc.tensor.matmul(PA[s][:, :], m.wn["Wv"][:, :], DIF[s][:, :], start=True, stop=True)
                        nc.tensor.matmul(PB[s][:, :], m.wn["Wv"][:, :], ND[s][:, :], start=True, stop=True)
                    for s, g in slots:
                        pe.wait_ge(pr, 1)
                        pe.sem_inc(pr, -1)
                        nc.tensor.matmul(PC[s][:, :], m.sum_heads[:, :], PR[s][:, :], start=True, stop=True
                                         ).then_inc(score, 1)
                    for s, g in slots:
                        pe.wait_ge(agg, 1)
                        pe.sem_inc(agg, -1)
                        rows_product(nc, PD[s], [(on.V[s], m.wn["Wo"][:, :])], m.bias["bo"], m.ones_row
                                     ).then_inc(ao_ps, 1)
                over_edge_pairs(m, pe, body)

            @block.scalar
            def _(act):
                def body(i, slots):
                    for s, g in slots:
                        act.wait_ge(turned, 1)
                        act.sem_inc(turned, -1)
                        nc.scalar.activation(ND[s][:, :], PB[s][:, :], ACT.Copy).then_inc(nd, 1)
                    for s, g in slots:
                        act.wait_ge(qk, 1)
                        act.sem_inc(qk, -1)
                        nc.scalar.activation(Q[s][:, :], PC[s][:, :], ACT.Identity, bias=m.col["bq"][:, :]
                                             ).then_inc(q, 1)
                    for s, g in slots:
                        on.exponentials(act, s)
                        nc.scalar.activation(E0[s][:, :], on.M[s][:, 1:], ACT.Exp, scale=-1.0).then_inc(on.exps, 1)
                    for s, g in slots:
                        act.wait_ge(ao_ps, 1)
                        act.sem_inc(ao_ps, -1)
                        act.wait_ge(so.out_free, 1)
                        act.sem_inc(so.out_free, -1)
                        nc.scalar.activation(AO[s][:, :, :].rearrange("p a d -> p (a d)"), PD[s][:, :], ACT.Copy
                                             ).then_inc(so.ready, 1)
                over_edge_pairs(m, act, body)
        ph.retire()


def program(nc, ins, out):
    with ExitStack() as ctx:
        m = Machine(nc, ins, out, ctx)
        weights(m)
        edges(m)
        nodes_first(m)
        sage_first(m)
        sage_second(m)
        gat(m)
        gcn(m)
        attention(m)
        nodes_last(m)



def kernel(**inputs):
    import concourse.bacc as bacc
    from concourse.bass_utils import run_bass_kernel_spmd

    nc = bacc.Bacc("TRN2", target_bir_lowering=False, num_devices=1)
    arrays, ins = {}, {}
    for name, value in inputs.items():
        a = np.ascontiguousarray(value)
        arrays["in_" + name] = a
        ins[name] = nc.dram_tensor("in_" + name, a.shape, mybir.dt.from_np(a.dtype), kind="ExternalInput").ap()
    out = nc.dram_tensor("out", inputs["x"].shape, F32, kind="ExternalOutput").ap()
    program(nc, ins, out)
    r = run_bass_kernel_spmd(nc, [arrays], core_ids=[0])
    return r.results[0]["out"]
```

```python
from contextlib import ExitStack

import numpy as np

import concourse.bass as bass
from concourse import mybir

ALU = mybir.AluOpType
ACT = mybir.ActivationFunctionType
F32 = mybir.dt.float32
BF16 = mybir.dt.bfloat16
I32 = mybir.dt.int32

P = 128
TILES = 4
ROWS = P * TILES
SLOTS = 4
WIDE = 132
PAD = 1 << 20
EPS = 1e-5
LOW = -3.0e38
NAN_LIMIT = 1e4


def tiles(x, rows=P, width=P):
    return x[0:rows, :].rearrange("p (a d) -> p a d", d=width)


class Machine:

    def __init__(self, nc, ins, out, ctx):
        self.nc, self.ins, self.out, self.ctx = nc, ins, out, ctx
        self.N = ins["x"].shape[0]
        self.E = ins["src"].shape[0]
        lot = SLOTS * ROWS
        self.EP = -(-self.E // lot) * lot
        self.G = self.EP // ROWS
        self.T = self.EP // P
        self.J = self.EP // P
        self.edge_lots = self.G // SLOTS
        self.edge_pairs = self.G // 2
        self.node_lots = self.N // lot
        rest = self.N - self.node_lots * lot
        self.rest = []
        g, s = SLOTS * self.node_lots, 0
        while rest > 0:
            r = min(rest, ROWS)
            assert r % TILES == 0
            self.rest.append((s, g, r // TILES))
            g, s, rest = g + 1, s + 1, rest - r

    def dram(self, name, shape, dt=F32):
        return self.nc.dram_tensor(name, shape, dt, kind="Internal").ap()

    def keep(self, name, shape, dt=F32):
        return self.ctx.enter_context(self.nc.sbuf_tensor(name, shape, dt))


class Phase:

    def __init__(self, m, name, ctx, slots=2):
        self.m, self.name, self.ctx, self.slots = m, name, ctx, slots
        self.primed = []

    def sb(self, name, shape, dt=F32):
        return self.ctx.enter_context(self.m.nc.sbuf_tensor(f"{self.name}_{name}", shape, dt))

    def each(self, name, shape, dt=F32):
        return [self.sb(f"{name}{s}", shape, dt) for s in range(self.slots)]

    def ps(self, name):
        return self.ctx.enter_context(self.m.nc.psum_tensor(f"{self.name}_ps_{name}", [P, 512], F32))

    def ps_each(self, name):
        return [self.ps(f"{name}{s}") for s in range(self.slots)]

    def sem(self, name):
        return self.ctx.enter_context(self.m.nc.semaphore(f"{self.name}_{name}"))

    def counter(self, name):
        return self.m.ctx.enter_context(self.m.nc.semaphore(f"{self.name}_{name}"))

    def prime(self, eng, n, *sems):
        for sem in sems:
            eng.sem_inc(sem, n)
            self.primed.append((sem, n))

    def retire(self):
        with self.m.nc.Block() as block:
            @block.vector
            def _(dve):
                for sem, n in self.primed:
                    dve.wait_ge(sem, n)
                    dve.sem_inc(sem, -n)

    def sem_each(self, name):
        return [self.sem(f"{name}{s}") for s in range(self.slots)]



class Norm:

    def __init__(self, ph, name, per):
        n = 2 * per
        self.nc, self.m, self.per = ph.m.nc, ph.m, per
        self.st = [ph.sb(f"{name}_st{h}", [P, n, 6]) for h in range(2)]
        self.sum, self.dif, self.var, self.sd, self.r, self.u, self.nb = (
            [ph.sb(f"{name}_{k}{h}", [P, n]) for h in range(2)] for k in ["sum", "dif", "var", "sd", "r", "u", "nb"])
        self.ve, self.rooted = ph.sem(name + "_ve"), ph.sem(name + "_rooted")

    def start(self, dve, own):
        self.nc.vector.memset(self.st[0][:, :, :], 1.0)
        self.nc.vector.memset(self.st[1][:, :, :], 1.0).then_inc(own, 1)
        dve.wait_ge(own, 1)
        dve.sem_inc(own, -1)

    def stats(self, s, xs, rows=P):
        for a, x in enumerate(xs):
            last = self.nc.vector.bn_stats(self.st[s // 2][0:rows, s % 2 * self.per + a, :], x)
        return last

    def variances(self, dve, own, h):
        v, st, total, dif, var = self.nc.vector, self.st[h], self.sum[h], self.dif[h], self.var[h]
        v.tensor_tensor(total[:, :], st[:, :, 1], st[:, :, 4], ALU.add)
        v.tensor_tensor(dif[:, :], st[:, :, 1], st[:, :, 4], ALU.subtract)
        v.tensor_tensor(var[:, :], st[:, :, 2], st[:, :, 5], ALU.add).then_inc(own, 1)
        dve.wait_ge(own, 1)
        dve.sem_inc(own, -1)
        v.tensor_scalar(var[:, :], var[:, :], 1.0 / P, EPS, ALU.mult, ALU.add)
        v.scalar_tensor_tensor(dif[:, :], dif[:, :], 0.25, dif[:, :], ALU.mult, ALU.mult).then_inc(own, 1)
        dve.wait_ge(own, 1)
        dve.sem_inc(own, -1)
        v.tensor_tensor(var[:, :], var[:, :], dif[:, :], ALU.add).then_inc(self.ve, 1)

    def root(self, act, h):
        act.wait_ge(self.ve, 1)
        act.sem_inc(self.ve, -1)
        self.nc.scalar.activation(self.sd[h][:, :], self.var[h][:, :], ACT.Sqrt).then_inc(self.rooted, 1)

    def scales(self, dve, own, h):
        v, r, u, nb, var, sd, total = self.nc.vector, self.r[h], self.u[h], self.nb[h], self.var[h], self.sd[h], self.sum[h]
        dve.wait_ge(self.rooted, 1)
        dve.sem_inc(self.rooted, -1)
        v.reciprocal(r[:, :], sd[:, :]).then_inc(own, 1)
        dve.wait_ge(own, 1)
        dve.sem_inc(own, -1)
        v.tensor_tensor(u[:, :], var[:, :], r[:, :], ALU.mult).then_inc(own, 1)
        dve.wait_ge(own, 1)
        dve.sem_inc(own, -1)
        v.scalar_tensor_tensor(u[:, :], u[:, :], -0.5, r[:, :], ALU.mult, ALU.mult).then_inc(own, 1)
        dve.wait_ge(own, 1)
        dve.sem_inc(own, -1)
        v.scalar_tensor_tensor(r[:, :], u[:, :], 1.5, r[:, :], ALU.add, ALU.mult).then_inc(own, 1)
        dve.wait_ge(own, 1)
        dve.sem_inc(own, -1)
        v.scalar_tensor_tensor(nb[:, :], total[:, :], -0.5, r[:, :], ALU.mult, ALU.mult).then_inc(own, 1)
        dve.wait_ge(own, 1)
        dve.sem_inc(own, -1)

    def power(self, pool, h):
        pool.wait_ge(self.ve, 1)
        pool.sem_inc(self.ve, -1)
        self.nc.gpsimd.tensor_tensor(self.r[h][:, :], self.var[h][:, :], self.m.half[:, :], ALU.pow
                                     ).then_inc(self.rooted, 1)

    def shifts(self, dve, own, h):
        dve.wait_ge(self.rooted, 1)
        dve.sem_inc(self.rooted, -1)
        self.nc.vector.scalar_tensor_tensor(self.nb[h][:, :], self.sum[h][:, :], -0.5, self.r[h][:, :],
                                                      ALU.mult, ALU.mult).then_inc(own, 1)
        dve.wait_ge(own, 1)
        dve.sem_inc(own, -1)

    def on_vector(self, s, outs, xs, rows=P):
        r, nb = self.r[s // 2], self.nb[s // 2]
        for a, (o, x) in enumerate(zip(outs, xs)):
            k = s % 2 * self.per + a
            last = self.nc.vector.tensor_scalar(o, x, r[0:rows, k:k + 1], nb[0:rows, k:k + 1], ALU.mult, ALU.add)
        return last

    def on_scalar(self, s, outs, xs, func, rows=P, at=0):
        r, nb = self.r[s // 2], self.nb[s // 2]
        for a, (o, x) in enumerate(zip(outs, xs)):
            k = s % 2 * self.per + at + a
            last = self.nc.scalar.activation(o, x, func, scale=r[0:rows, k:k + 1], bias=nb[0:rows, k:k + 1])
        return last


def four(x, rows=P):
    return [x[0:rows, a, 0:P] for a in range(TILES)]


def turn(nc, ps, x, ident, rows=P):
    for a in range(TILES):
        last = nc.tensor.transpose(ps[:, a * rows:(a + 1) * rows], x[:, a, :], ident[0:rows, 0:rows])
    return last


def rows_product(nc, ps, terms, bias_row, ones_row, rows=P):
    for a in range(TILES):
        out = ps[0:rows, a * P:(a + 1) * P]
        nc.tensor.matmul(out, ones_row[0:3, 0:rows], bias_row[0:3, :], start=True, stop=False)
        for k, (cols, w) in enumerate(terms):
            last = nc.tensor.matmul(out, cols[:, a * rows:(a + 1) * rows], w, start=False, stop=(k == len(terms) - 1))
    return last



def weights(m):
    nc, ins = m.nc, m.ins
    m.ident = m.keep("ident", [P, P])
    m.ones_row = m.keep("ones_row", [3, P], BF16)
    m.half = m.keep("half", [P, 8])
    m.heads4 = m.keep("heads4", [P, 4])
    m.heads8 = m.keep("heads8", [P, 8])
    names = ["W1l", "W1r", "W2l", "W2r"]
    m.wT = {k: m.keep(k, [P, P]) for k in names}
    m.wn = {k: m.keep(k, [P, P]) for k in ["Ws", "Wd", "W", "Wq", "Wk", "Wv", "Wo", "Wvo"]}
    m.W1 = m.keep("W1", [P, 512])
    m.W2 = m.keep("W2", [P, 4, P])
    m.bias = {k: m.keep("row_" + k, [3, P], BF16) for k in ["b1", "b2", "b", "bo", "bf2"]}
    bias_parts = m.dram("bias_parts", (3, 5 * P), BF16)
    m.attn_heads = m.keep("attn_heads", [P, P])
    m.sum_heads = m.keep("sum_heads", [P, P])
    m.col = {k: m.keep("col_" + k, [P, 1]) for k in ["bs", "bsd", "bd", "at", "bq", "bv", "g1", "b1", "g2", "b2"]}
    m.bf1 = m.keep("col_bf1", [P, 4])
    m.bo_rows = m.keep("bo_rows", [32, P])
    with ExitStack() as ctx:
        ph = Phase(m, "w", ctx)
        raw = {k: ph.sb("raw" + k, [P, P]) for k in names}
        plain = ph.sb("plain", [1, 5, P])
        parts = [ph.sb(f"part{i}", [1, 5 * P], BF16) for i in range(3)]
        WvT = ph.sb("WvT", [P, P])
        folded = {k: ph.ps("f" + k) for k in ["a", "b", "c", "d"]}
        landed, made, parted = ph.counter("landed"), ph.counter("made"), ph.counter("parted")
        chosen, turned, own, split, folded_w, more = (ph.sem(n) for n in ["chosen", "turned", "own", "split",
                                                                          "folded", "more"])
        loads = [(raw["W1l"][:, :], ins["L0_gnn_W1_l"]), (raw["W1r"][:, :], ins["L0_gnn_W1_r"]),
                 (raw["W2l"][:, :], ins["L0_gnn_W2_l"]), (raw["W2r"][:, :], ins["L0_gnn_W2_r"]),
                 (m.wn["Ws"][:, :], ins["L1_gnn_W_src"]), (m.wn["Wd"][:, :], ins["L1_gnn_W_dst"]),
                 (m.wn["W"][:, :], ins["L2_gnn_W"]), (m.wn["Wq"][:, :], ins["L3_gnn_Wq"]),
                 (m.wn["Wk"][:, :], ins["L3_gnn_Wk"]), (m.wn["Wv"][:, :], ins["L3_gnn_Wv"]),
                 (m.wn["Wo"][:, :], ins["L3_gnn_Wo"]), (m.W1[:, :], ins["L3_gnn_W1"]),
                 (m.W2[:, :, :], ins["L3_gnn_W2"].rearrange("(h p) d -> p h d", p=P)),
                 (m.bf1[:, :], ins["L3_gnn_bf1"].rearrange("(h p) -> p h", p=P)),
                 (m.col["at"][:, :], ins["L1_gnn_attn"].rearrange("h d -> (h d)").rearrange("(p o) -> p o", o=1)),
                 (m.bo_rows[:, :], ins["L3_gnn_bo"].rearrange("(o d) -> o d", o=1).broadcast_to([32, P]))]
        loads += [(m.col[k][:, :], ins[v].rearrange("(p o) -> p o", o=1)) for k, v in
                  [("bs", "L1_gnn_b_src"), ("bd", "L1_gnn_b_dst"), ("bq", "L3_gnn_bq"), ("bv", "L3_gnn_bv"),
                   ("g1", "L3_gnn_g1"), ("b1", "L3_gnn_b1"), ("g2", "L3_gnn_g2"), ("b2", "L3_gnn_b2")]]
        loads += [(plain[0:1, n, :], ins[v].rearrange("(o d) -> o d", o=1)) for n, v in
                  enumerate(["L0_gnn_b1_l", "L0_gnn_b2_l", "L2_gnn_b", "L3_gnn_bo", "L3_gnn_bf2"])]
        with nc.Block() as block:
            @block.sync
            def _(sp):
                with nc.allow_non_contiguous_dma(reason="bias columns"):
                    for dst, src in loads:
                        sp.dma_start(dst, src).then_inc(landed, 16)
                sp.wait_ge(landed, 16 * len(loads))
                sp.wait_ge(split, 1)
                sp.sem_inc(split, -1)
                for k in range(3):
                    sp.dma_start(bias_parts[k:k + 1, :], parts[k][:, :]).then_inc(parted, 16)
                sp.wait_ge(parted, 48)
                for n, k in enumerate(["b1", "b2", "b", "bo", "bf2"]):
                    sp.dma_start(m.bias[k][:, :], bias_parts[:, n * P:(n + 1) * P]).then_inc(parted, 16)
                sp.wait_ge(parted, 48 + 80)

            @block.gpsimd
            def _(pool):
                nc.gpsimd.memset(m.ident[:, :], 0.0).then_inc(made, 1)
                nc.gpsimd.memset(m.attn_heads[:, :], 1.0).then_inc(made, 1)
                nc.gpsimd.memset(m.sum_heads[:, :], 0.25).then_inc(made, 1)
                nc.gpsimd.memset(m.half[:, :], -0.5).then_inc(made, 1)
                nc.gpsimd.memset(m.heads4[:, :], 1.0 / 32).then_inc(made, 1)
                nc.gpsimd.memset(m.heads8[:, :], 1.0 / 16).then_inc(made, 1)
                nc.gpsimd.memset(m.ones_row[:, :], 1.0).then_inc(made, 1)
                pool.wait_ge(made, 7)
                nc.gpsimd.affine_select(out=m.ident[:, :], in_=m.ident[:, :], compare_op=ALU.not_equal, fill=1.0,
                                        base=0, pattern=[[-1, P]], channel_multiplier=1).then_inc(made, 1)
                n = 8
                for t, w, c in ((m.attn_heads, 32, 32), (m.sum_heads, 16, 16), (m.heads4, 32, 1), (m.heads8, 16, 1)):
                    v = t[:, :].rearrange("p (h c) -> p h c", c=c)
                    pool.wait_ge(made, n)
                    nc.gpsimd.affine_select(out=v, in_=v, compare_op=ALU.is_ge, fill=0.0, base=0,
                                            pattern=[[-w, P // w], [0, c]], channel_multiplier=1).then_inc(made, 1)
                    pool.wait_ge(made, n + 1)
                    nc.gpsimd.affine_select(out=v, in_=v, compare_op=ALU.is_ge, fill=0.0, base=w - 1,
                                            pattern=[[w, P // w], [0, c]], channel_multiplier=-1).then_inc(made, 1)
                    n += 2
                pool.wait_ge(made, n)
                pool.sem_inc(chosen, 2)

            @block.tensor
            def _(pe):
                pe.wait_ge(chosen, 1)
                pe.sem_inc(chosen, -1)
                pe.wait_ge(landed, 16 * len(loads))
                for n, k in enumerate(names):
                    last = nc.tensor.transpose(folded["a"][:, n * P:(n + 1) * P], raw[k][:, :], m.ident[:, :])
                cols = [(m.wn["Wq"][:, :], m.col["b1"]), (m.wn["Wv"][:, :], m.col["b1"])]
                cols += [(m.W1[:, h * P:(h + 1) * P], m.col["b2"]) for h in range(4)]
                for n, (w, c) in enumerate(cols):
                    last = nc.tensor.matmul(folded["b"][:, n:n + 1], w, c[:, :], start=True, stop=True)
                last.then_inc(turned, 1)
                pe.wait_ge(folded_w, 1)
                pe.sem_inc(folded_w, -1)
                nc.tensor.transpose(folded["c"][:, 0:P], m.wn["Wv"][:, :], m.ident[:, :]).then_inc(turned, 1)
                pe.wait_ge(more, 1)
                pe.sem_inc(more, -1)
                nc.tensor.matmul(folded["d"][:, 0:P], WvT[:, :], m.wn["Wo"][:, :], start=True, stop=True)
                nc.tensor.matmul(folded["c"][0:1, 0:P], m.col["bv"][:, :], m.wn["Wo"][:, :], start=True, stop=True
                                 ).then_inc(turned, 1)

            @block.vector
            def _(dve):
                dve.wait_ge(turned, 1)
                dve.sem_inc(turned, -1)
                dve.wait_ge(chosen, 1)
                dve.sem_inc(chosen, -1)
                for n, k in enumerate(names):
                    nc.vector.tensor_copy(m.wT[k][:, :], folded["a"][:, n * P:(n + 1) * P])
                nc.vector.tensor_tensor(m.col["bq"][:, :], m.col["bq"][:, :], folded["b"][:, 0:1], ALU.add)
                nc.vector.tensor_tensor(m.col["bv"][:, :], m.col["bv"][:, :], folded["b"][:, 1:2], ALU.add)
                nc.vector.tensor_tensor(m.bf1[:, :], m.bf1[:, :], folded["b"][:, 2:6], ALU.add)
                nc.vector.tensor_tensor(m.col["bsd"][:, :], m.col["bs"][:, :], m.col["bd"][:, :], ALU.add)
                for k in ("Wq", "Wk", "Wv"):
                    nc.vector.tensor_scalar(m.wn[k][:, :], m.wn[k][:, :], m.col["g1"][:, :], None, ALU.mult)
                nc.vector.tensor_scalar(m.W1[:, :], m.W1[:, :], m.col["g2"][:, :], None, ALU.mult)
                last = nc.vector.tensor_scalar(m.attn_heads[:, :], m.attn_heads[:, :], m.col["at"][:, :], None,
                                               ALU.mult)
                last.then_inc(own, 1)
                dve.wait_ge(own, 1)
                dve.sem_inc(own, -1)
                dve.sem_inc(folded_w, 1)
                dve.wait_ge(turned, 1)
                dve.sem_inc(turned, -1)
                nc.vector.tensor_copy(WvT[:, :], folded["c"][:, 0:P]).then_inc(own, 1)
                dve.wait_ge(own, 1)
                dve.sem_inc(own, -1)
                dve.sem_inc(more, 1)
                dve.wait_ge(turned, 1)
                dve.sem_inc(turned, -1)
                nc.vector.tensor_copy(m.wn["Wvo"][:, :], folded["d"][:, 0:P])
                bo = plain[0:1, 3, :]
                nc.vector.tensor_tensor(bo, bo, folded["c"][0:1, 0:P], ALU.add).then_inc(own, 1)
                dve.wait_ge(own, 1)
                dve.sem_inc(own, -1)
                rest = plain[0:1, :, :].rearrange("p a d -> p (a d)")
                for k in range(3):
                    nc.vector.tensor_copy(parts[k][:, :], rest).then_inc(own, 1)
                    dve.wait_ge(own, 1)
                    dve.sem_inc(own, -1)
                    if k < 2:
                        nc.vector.tensor_tensor(rest, rest, parts[k][:, :], ALU.subtract).then_inc(own, 1)
                        dve.wait_ge(own, 1)
                        dve.sem_inc(own, -1)
                dve.sem_inc(split, 1)



def edges(m):
    nc, ins = m.nc, m.ins
    J, G, T, E, EP = m.J, m.G, m.T, m.E, m.EP
    full, rest = E // J, E % J
    m.gather_idx = m.dram("gather_idx", (P, G, 8), I32)
    m.scatter_idx = m.dram("scatter_idx", (P, G, 4), I32)
    m.last_idx = m.dram("last_idx", (P, G, 4), I32)
    m.edge_col = m.dram("edge_col", (P, G, 8))
    m.row = {k: m.dram("row_" + k, (EP,)) for k in ["src", "dst", "key", "sidx", "lidx", "dis", "rdeg"]}
    m.keep_row = m.dram("keep_row", (EP,), BF16)
    m.neg_row = m.dram("neg_row", (EP,), BF16)
    with ExitStack() as ctx:
        ph = Phase(m, "e", ctx)
        ints = {k: ph.sb("i" + k, [P, J], I32) for k in ["dst", "prev", "next", "src"]}
        f = {k: ph.sb("f" + k, [P, J]) for k in
             ["dst", "prev", "next", "src", "same", "nsame", "cnt", "ones", "head", "tail", "tmp", "num", "sidx",
              "lidx", "rdeg", "ve", "dis", "half", "rem", "key", "tmp2"]}
        number = ph.sb("number", [P, J], I32)
        keep16, neg16 = ph.sb("keep16", [P, J], BF16), ph.sb("neg16", [P, J], BF16)
        diag = [ph.sb(f"diag{i}", [P, P]) for i in range(2)]
        link = [ph.sb(f"link{i}", [P, P]) for i in range(2)]
        upper, lower, ones = ph.sb("upper", [P, P]), ph.sb("lower", [P, P]), ph.sb("onesm", [P, P])
        in_head = ph.sb("in_head", [P, 1])
        carry = [ph.sb(f"carry{i}", [P, 1]) for i in range(2)]
        psa, psb, psc = ph.ps("a"), ph.ps("b"), ph.ps("c")
        own_pool = ph.sem("own_pool")
        landed, stored = ph.counter("landed"), ph.counter("stored")
        filled, made, own, diags, spread, links, closed, ve_ready, dis_ready = (
            ph.sem(n) for n in ["filled", "made", "own", "diags", "spread", "links", "closed", "ve", "dis"])
        dst, src = ins["dst"], ins["src"]

        def flat(v, a, b):
            return v[a:b].rearrange("(o d) -> o d", o=1)

        def block_of(v, a, n):
            return v[a:a + n * J].rearrange("(p j) -> p j", j=J)

        loads = [(ints["dst"][0:full, :], block_of(dst, 0, full)), (ints["src"][0:full, :], block_of(src, 0, full)),
                 (ints["prev"][0:1, 1:J], flat(dst, 0, J - 1)), (ints["prev"][1:full, :], block_of(dst, J - 1, full - 1))]
        if rest:
            loads += [(ints["dst"][full:full + 1, 0:rest], flat(dst, full * J, E)),
                      (ints["src"][full:full + 1, 0:rest], flat(src, full * J, E)),
                      (ints["prev"][full:full + 1, 0:rest], flat(dst, full * J - 1, E - 1)),
                      (ints["next"][0:full, :], block_of(dst, 1, full))]
            if rest > 1:
                loads += [(ints["next"][full:full + 1, 0:rest - 1], flat(dst, full * J + 1, E))]
        else:
            loads += [(ints["next"][0:full - 1, :], block_of(dst, 1, full - 1)),
                      (ints["next"][full - 1:full, 0:J - 1], flat(dst, (full - 1) * J + 1, E))]
        rows_out = [(m.row[k], f[k]) for k in ["src", "dst", "key", "sidx", "lidx", "dis", "rdeg"]]
        rows_out += [(m.keep_row, keep16), (m.neg_row, neg16)]

        with nc.Block() as block:
            @block.sync
            def _(sp):
                sp.wait_ge(filled, 1)
                sp.sem_inc(filled, -1)
                for o, i in loads:
                    sp.dma_start(o, i).then_inc(landed, 16)
                sp.wait_ge(closed, 1)
                sp.sem_inc(closed, -1)
                for o, i in rows_out:
                    sp.dma_start(o.rearrange("(p j) -> p j", j=J), i[:, :]).then_inc(stored, 16)
                sp.wait_ge(stored, 16 * len(rows_out))

            @block.gpsimd
            def _(pool):
                nc.gpsimd.memset(ints["dst"][:, :], PAD)
                nc.gpsimd.memset(ints["prev"][:, :], -1)
                nc.gpsimd.memset(ints["next"][:, :], PAD)
                nc.gpsimd.memset(ints["src"][:, :], m.N).then_inc(own_pool, 1)
                pool.wait_ge(own_pool, 1)
                pool.sem_inc(own_pool, -1)
                pool.sem_inc(filled, 1)
                nc.gpsimd.iota(number[:, :], pattern=[[1, J]], base=0, channel_multiplier=J)
                nc.gpsimd.memset(f["half"][:, :], -0.5)
                for t, b, c in ((upper, -1, -1), (lower, -1, 1)):
                    nc.gpsimd.memset(t[:, :], 1.0).then_inc(own_pool, 1)
                    pool.wait_ge(own_pool, 1)
                    pool.sem_inc(own_pool, -1)
                    nc.gpsimd.affine_select(out=t[:, :], in_=t[:, :], compare_op=ALU.is_ge, fill=0.0, base=b,
                                            pattern=[[-c, P]], channel_multiplier=c).then_inc(own_pool, 1)
                    pool.wait_ge(own_pool, 1)
                    pool.sem_inc(own_pool, -1)
                pool.sem_inc(made, 1)
                pool.wait_ge(ve_ready, 1)
                pool.sem_inc(ve_ready, -1)
                nc.gpsimd.tensor_tensor(f["dis"][:, :], f["ve"][:, :], f["half"][:, :], ALU.pow).then_inc(dis_ready, 1)

            @block.tensor
            def _(pe):
                pe.wait_ge(diags, 1)
                pe.sem_inc(diags, -1)
                nc.tensor.matmul(psa[:, 0:P], ones[:, :], diag[0][:, :], start=True, stop=True)
                nc.tensor.matmul(psb[:, 0:P], ones[:, :], diag[1][:, :], start=True, stop=True).then_inc(spread, 1)
                pe.wait_ge(links, 1)
                pe.sem_inc(links, -1)
                nc.tensor.matmul(psa[:, 0:1], link[0][:, :], f["cnt"][:, J - 1:J], start=True, stop=True)
                nc.tensor.matmul(psb[:, 0:1], link[1][:, :], in_head[:, :], start=True, stop=True).then_inc(spread, 1)

            @block.vector
            def _(dve):
                v = nc.vector
                first, last = f["dst"][:, 0:1], f["dst"][:, J - 1:J]
                dve.wait_ge(landed, 16 * len(loads))
                dve.wait_ge(made, 1)
                dve.sem_inc(made, -1)
                for k, i in [("dst", "dst"), ("prev", "prev"), ("next", "next"), ("key", "src")]:
                    v.tensor_copy(f[k][:, :], ints[i][:, :])
                v.memset(ones[:, :], 1.0)
                v.memset(f["ones"][:, :], 1.0)
                v.tensor_copy(f["num"][:, :], number[:, :]).then_inc(own, 1)
                dve.wait_ge(own, 1)
                dve.sem_inc(own, -1)
                v.tensor_tensor(f["same"][:, :], f["dst"][:, :], f["prev"][:, :], ALU.is_equal)
                v.tensor_tensor(f["nsame"][:, :], f["dst"][:, :], f["next"][:, :], ALU.is_equal)
                v.tensor_scalar(f["head"][:, :], f["dst"][:, :], first, None, ALU.is_equal)
                v.tensor_scalar(f["tail"][:, :], f["dst"][:, :], last, None, ALU.is_equal)
                v.tensor_scalar(diag[0][:, :], m.ident[:, :], first, None, ALU.mult)
                v.tensor_scalar(diag[1][:, :], m.ident[:, :], last, None, ALU.mult).then_inc(own, 1)
                dve.wait_ge(own, 1)
                dve.sem_inc(own, -1)
                dve.sem_inc(diags, 1)
                v.tensor_copy(keep16[:, :], f["same"][:, :])
                v.tensor_scalar(neg16[:, :], f["same"][:, :], -1.0, -LOW, ALU.add, ALU.mult)
                v.tensor_tensor_scan(f["cnt"][:, :], f["same"][:, :], f["ones"][:, :], 0.0, ALU.mult, ALU.add)
                v.tensor_tensor_scan(f["rem"][:, ::-1], f["nsame"][:, ::-1], f["nsame"][:, ::-1], -1.0,
                                     ALU.mult, ALU.add)
                v.reduce_sum(in_head[:, :], f["head"][:, :], mybir.AxisListType.X)
                dve.wait_ge(spread, 1)
                dve.sem_inc(spread, -1)
                v.tensor_scalar(link[0][:, :], psa[:, 0:P], last, None, ALU.is_equal)
                v.tensor_scalar(link[1][:, :], psb[:, 0:P], first, None, ALU.is_equal).then_inc(own, 1)
                dve.wait_ge(own, 1)
                dve.sem_inc(own, -1)
                v.tensor_tensor(link[0][:, :], link[0][:, :], upper[:, :], ALU.mult)
                v.tensor_tensor(link[1][:, :], link[1][:, :], lower[:, :], ALU.mult).then_inc(own, 1)
                dve.wait_ge(own, 1)
                dve.sem_inc(own, -1)
                dve.sem_inc(links, 1)
                dve.wait_ge(spread, 1)
                dve.sem_inc(spread, -1)
                v.tensor_copy(carry[0][:, :], psa[:, 0:1])
                v.tensor_copy(carry[1][:, :], psb[:, 0:1]).then_inc(own, 1)
                dve.wait_ge(own, 1)
                dve.sem_inc(own, -1)
                v.tensor_scalar(f["head"][:, :], f["head"][:, :], carry[0][:, :], None, ALU.mult)
                v.tensor_scalar(f["tail"][:, :], f["tail"][:, :], carry[1][:, :], None, ALU.mult).then_inc(own, 1)
                dve.wait_ge(own, 1)
                dve.sem_inc(own, -1)
                v.tensor_tensor(f["cnt"][:, :], f["cnt"][:, :], f["head"][:, :], ALU.add)
                v.tensor_tensor(f["rem"][:, :], f["rem"][:, :], f["tail"][:, :], ALU.add).then_inc(own, 1)
                dve.wait_ge(own, 1)
                dve.sem_inc(own, -1)
                v.tensor_tensor(f["lidx"][:, :], f["rem"][:, :], f["num"][:, :], ALU.add)
                v.tensor_scalar(f["ve"][:, :], f["cnt"][:, :], 1.0, None, ALU.add).then_inc(ve_ready, 1)
                v.reciprocal(f["rdeg"][:, :], f["cnt"][:, :])
                v.scalar_tensor_tensor(f["sidx"][:, :], f["nsame"][:, :], float(PAD), f["dst"][:, :], ALU.mult, ALU.add)
                v.tensor_scalar(f["tmp2"][:, :], f["key"][:, :], float(m.N), None, ALU.is_lt)
                v.tensor_scalar(f["tmp"][:, :], f["dst"][:, :], float(PAD), None, ALU.is_lt).then_inc(own, 1)
                dve.wait_ge(own, 1)
                dve.sem_inc(own, -1)
                v.tensor_tensor(f["src"][:, :], f["key"][:, :], f["tmp2"][:, :], ALU.mult)
                v.tensor_tensor(f["dst"][:, :], f["dst"][:, :], f["tmp"][:, :], ALU.mult).then_inc(own, 1)
                dve.wait_ge(own, 1)
                dve.sem_inc(own, -1)
                dve.wait_ge(dis_ready, 1)
                dve.sem_inc(dis_ready, -1)
                dve.sem_inc(closed, 1)

    with ExitStack() as ctx:
        ph = Phase(m, "c", ctx)
        keys = ["src", "dst", "key", "sidx", "lidx", "dis"]
        back = {k: ph.sb("back" + k, [G, 4, P]) for k in keys}
        col = {k: ph.sb("col" + k, [P, T]) for k in keys}
        gi, si, li = (ph.sb(n, [P, G, w], I32) for n, w in (("gi", 8), ("si", 4), ("li", 4)))
        ec = ph.sb("ec", [P, G, 8])
        ps = {k: ph.ps(k) for k in keys}
        landed, stored = ph.counter("landed"), ph.counter("stored")
        turned, own, closed = (ph.sem(n) for n in ["turned", "own", "closed"])
        outs = [(m.gather_idx, gi), (m.scatter_idx, si), (m.last_idx, li), (m.edge_col, ec)]
        with nc.Block() as block:
            @block.sync
            def _(sp):
                for k in keys:
                    sp.dma_start(back[k][:, :, :], m.row[k].rearrange("(b r p) -> r b p", b=4, p=P)).then_inc(landed, 16)
                sp.wait_ge(closed, 1)
                sp.sem_inc(closed, -1)
                for o, i in outs:
                    sp.dma_start(o, i[:, :, :]).then_inc(stored, 16)
                sp.wait_ge(stored, 16 * len(outs))

            @block.tensor
            def _(pe):
                pe.wait_ge(landed, 16 * len(keys))
                for k in keys:
                    for b in range(4):
                        last = nc.tensor.transpose(ps[k][:, b * G:(b + 1) * G], back[k][:, b, :], m.ident[0:G, 0:G])
                last.then_inc(turned, 1)

            @block.vector
            def _(dve):
                dve.wait_ge(turned, 1)
                dve.sem_inc(turned, -1)
                for k in keys:
                    last = nc.vector.tensor_copy(col[k][:, :], ps[k][:, 0:T])
                last.then_inc(own, 1)
                dve.wait_ge(own, 1)
                dve.sem_inc(own, -1)

                def by_group(k):
                    return col[k][:, :].rearrange("p (g a) -> p g a", a=4)
                nc.vector.tensor_copy(gi[:, :, 0:4], by_group("src"))
                nc.vector.tensor_copy(gi[:, :, 4:8], by_group("dst"))
                nc.vector.tensor_copy(si[:, :, :], by_group("sidx"))
                nc.vector.tensor_copy(li[:, :, :], by_group("lidx"))
                nc.vector.tensor_copy(ec[:, :, 0:4], by_group("dis"))
                nc.vector.tensor_copy(ec[:, :, 4:8], by_group("key")).then_inc(own, 1)
                dve.wait_ge(own, 1)
                dve.sem_inc(own, -1)
                dve.sem_inc(closed, 1)



def over_pairs(eng, lots, rest, step, of, peeled=0):
    step(of(0, 0), [], of(0, 1))
    looped = range(peeled, lots - 1 - peeled)
    for i in range(lots - 1):
        if i not in looped:
            step(of(i, 1), of(i, 0), of(i + 1, 0))
            step(of(i + 1, 0), of(i, 1), of(i + 1, 1))
        elif i == looped[0]:
            with eng.Fori(looped.start, looped.stop) as k:
                step(of(k, 1), of(k, 0), of(k + 1, 0))
                step(of(k + 1, 0), of(k, 1), of(k + 1, 1))
    pairs = [of(lots - 1, 0), of(lots - 1, 1)] + [pair for pair in rest if pair] + [[], []]
    for old, new, ahead in zip(pairs, pairs[1:], pairs[2:]):
        step(new, old, ahead)


def over_nodes(m, eng, step):
    def of(i, k):
        return [(2 * k + s, SLOTS * i + 2 * k + s, P) for s in range(2)]
    over_pairs(eng, m.node_lots, [[one for one in m.rest if one[0] // 2 == k] for k in range(2)], step, of)


def over_edge_lots(m, eng, step):
    def of(i, k):
        return [(2 * k + s, SLOTS * i + 2 * k + s, i) for s in range(2)]
    over_pairs(eng, m.edge_lots, [], step, of, 1)


def node_rows(table, g, rows):
    if isinstance(g, int):
        part = table[g * ROWS:g * ROWS + rows * TILES, :]
    else:
        part = table[bass.ds(g * ROWS, rows * TILES), :]
    return part.rearrange("(p a) d -> p a d", a=TILES)



def nodes_first(m):
    nc = m.nc
    x = m.ins["x"]
    m.h1 = m.dram("h1", (m.N, P))
    m.x1 = m.dram("x1", (m.N, WIDE))
    m.x3 = m.dram("x3", (m.N + 2 * ROWS, P))
    with ExitStack() as ctx:
        ph = Phase(m, "n", ctx, SLOTS)
        X = ph.each("x", [P, TILES, P])
        N0, H1, Y, POS, NEG, N1, X3 = (ph.each(k, [P, ROWS]) for k in ["n0", "h1", "y", "pos", "neg", "n1", "x3"])
        FIN = ph.each("fin", [P, ROWS], I32)
        HT, H1T, NT = (ph.each(k, [P, ROWS]) for k in ["ht", "h1t", "nt"])
        X1 = ph.each("x1", [P, TILES, WIDE])
        ln0, ln1 = Norm(ph, "ln0", 4), Norm(ph, "ln1", 4)
        PA, PB = ph.ps_each("a"), ph.ps_each("b")
        x_in, h1_saved, x1_saved, x3_saved = (ph.sem_each(k) for k in ["x_in", "h1_saved", "x1_saved", "x3_saved"])
        (x_free, scaled, pos, n0, t0, ht, h1_ps, h1_pe, h1_out, t1, h1t, y_ps, y_pool, y_dve, fixed, x1_out, scaled1, t2, nt,
         xl_ps, xl_read, x3_out, own_d, own_a, own_p, zeroed) = (ph.sem(k) for k in [
             "x_free", "scaled", "pos", "n0", "t0", "ht", "h1_ps", "h1_pe", "h1_out", "t1", "h1t", "y_ps", "y_pool",
             "y_dve", "fixed", "x1_out", "scaled1", "t2", "nt", "xl_ps", "xl_read", "x3_out", "own_d", "own_a", "own_p",
             "zeroed"])

        n1 = [ph.sem("n1_d"), ph.sem("n1_a")]

        with nc.Block() as block:
            @block.sync
            def _(sp):
                def load(slots):
                    for s, g, r in slots:
                        sp.wait_ge(x_free, 1)
                        sp.sem_inc(x_free, -1)
                        sp.dma_start(X[s][0:r, :, :], node_rows(x, g, r)).then_inc(x_in[s], 16)

                def step(new, old, ahead):
                    load(ahead)
                    for s, g, r in old:
                        sp.wait_ge(x1_out, 1)
                        sp.sem_inc(x1_out, -1)
                        sp.dma_start(node_rows(m.x1, g, r), X1[s][0:r, :, :]).then_inc(x1_saved[s], 16)
                    for s, g, r in new:
                        sp.wait_ge(h1_out, 1)
                        sp.sem_inc(h1_out, -1)
                        sp.dma_start(node_rows(m.h1, g, r), tiles(H1[s], r)).then_inc(h1_saved[s], 16)
                    for s, g, r in old:
                        sp.wait_ge(x3_out, 1)
                        sp.sem_inc(x3_out, -1)
                        sp.dma_start(node_rows(m.x3, g, r), tiles(X3[s], r)).then_inc(x3_saved[s], 16)

                load([(0, 0, P), (1, 1, P)])
                sp.wait_ge(zeroed, 1)
                sp.sem_inc(zeroed, -1)
                for k in range(2):
                    part = m.x3[m.N + k * ROWS:m.N + (k + 1) * ROWS, :].rearrange("(p a) d -> p a d", a=TILES)
                    sp.dma_start(part, tiles(X3[k])).then_inc(x3_saved[k], 16)
                over_nodes(m, sp, step)

            @block.gpsimd
            def _(pool):
                def step(new, old, ahead):
                    for s, g, r in new:
                        pool.wait_ge(y_pool, 1)
                        pool.sem_inc(y_pool, -1)
                        nc.gpsimd.tensor_scalar(NEG[s][0:r, :], Y[s][0:r, :], 0.0, -NAN_LIMIT, ALU.min, ALU.max
                                                ).then_inc(own_p, 1)
                        pool.wait_ge(own_p, 1)
                        pool.sem_inc(own_p, -1)
                        pool.wait_ge(pos, 1)
                        pool.sem_inc(pos, -1)
                        nc.gpsimd.tensor_tensor(POS[s][0:r, :], POS[s][0:r, :], NEG[s][0:r, :], ALU.add
                                                ).then_inc(fixed, 1)
                over_nodes(m, pool, step)

            @block.vector
            def _(dve):
                ph.prime(dve, SLOTS, x_free, xl_read)
                ph.prime(dve, 16, *h1_saved, *x1_saved, *x3_saved[2:])
                ph.primed += [(x3_saved[s], 16) for s in range(2)]
                ln0.start(dve, own_d)
                ln1.start(dve, own_d)
                nc.vector.memset(X3[0][:, :], 0.0)
                nc.vector.memset(X3[1][:, :], 0.0)
                for s in range(SLOTS):
                    last = nc.vector.memset(X1[s][:, :, :], 1.0)
                last.then_inc(own_d, 1)
                dve.wait_ge(own_d, 1)
                dve.sem_inc(own_d, -1)
                dve.sem_inc(zeroed, 1)

                def moments_ahead(slots):
                    for s, g, r in slots:
                        dve.wait_ge(x_in[s], 16)
                        dve.sem_inc(x_in[s], -16)
                        last = ln0.stats(s, four(X[s], r), r)
                    if slots:
                        last.then_inc(own_d, 1)
                        dve.wait_ge(own_d, 1)
                        dve.sem_inc(own_d, -1)
                        ln0.variances(dve, own_d, slots[0][0] // 2)

                def scales_ahead(slots):
                    if slots:
                        ln0.scales(dve, own_d, slots[0][0] // 2)
                        dve.sem_inc(scaled, 1)

                def step(new, old, ahead):
                    for s, g, r in old:
                        dve.wait_ge(fixed, 1)
                        dve.sem_inc(fixed, -1)
                        nc.vector.copy_predicated(POS[s][0:r, :], FIN[s][0:r, :], Y[s][0:r, :]).then_inc(own_d, 1)
                        dve.wait_ge(own_d, 1)
                        dve.sem_inc(own_d, -1)
                        dve.wait_ge(x1_saved[s], 16)
                        dve.sem_inc(x1_saved[s], -16)
                        nc.vector.tensor_tensor(X1[s][0:r, :, 0:P], X[s][0:r, :, :], tiles(POS[s], r),
                                                          ALU.add).then_inc(own_d, 1)
                        dve.wait_ge(own_d, 1)
                        dve.sem_inc(own_d, -1)
                        dve.sem_inc(x1_out, 1)
                        dve.sem_inc(x_free, 1)
                        last = ln1.stats(s, four(X1[s], r), r)
                    if old:
                        last.then_inc(own_d, 1)
                        dve.wait_ge(own_d, 1)
                        dve.sem_inc(own_d, -1)
                        ln1.variances(dve, own_d, old[0][0] // 2)
                    moments_ahead(ahead)
                    if old:
                        ln1.scales(dve, own_d, old[0][0] // 2)
                    if old[1:]:
                        dve.sem_inc(scaled1, 1)
                    for s, g, r in old[0:1]:
                        n = tiles(N1[s], r)
                        ln1.on_vector(s, [n[:, a, :] for a in range(4)], four(X1[s], r), r).then_inc(n1[0], 1)
                    scales_ahead(ahead)
                    for s, g, r in new:
                        dve.wait_ge(y_dve, 1)
                        dve.sem_inc(y_dve, -1)
                        nc.vector.tensor_scalar(POS[s][0:r, :], Y[s][0:r, :], 0.0, NAN_LIMIT, ALU.max, ALU.min
                                                ).then_inc(pos, 1)
                        nc.vector.tensor_scalar(FIN[s][0:r, :], Y[s][0:r, :], 0.0, 0.0, ALU.mult,
                                                          ALU.is_equal).then_inc(own_d, 1)
                        dve.wait_ge(own_d, 1)
                        dve.sem_inc(own_d, -1)
                    for s, g, r in old:
                        dve.wait_ge(xl_ps, 1)
                        dve.sem_inc(xl_ps, -1)
                        dve.wait_ge(x3_saved[s], 16)
                        dve.sem_inc(x3_saved[s], -16)
                        nc.vector.tensor_tensor(tiles(X3[s], r), tiles(PB[s], r), X1[s][0:r, :, 0:P],
                                                          ALU.add).then_inc(own_d, 1)
                        dve.wait_ge(own_d, 1)
                        dve.sem_inc(own_d, -1)
                        dve.sem_inc(x3_out, 1)
                        dve.sem_inc(xl_read, 1)
                moments_ahead([(0, 0, P), (1, 1, P)])
                scales_ahead([(0, 0, P), (1, 1, P)])
                over_nodes(m, dve, step)

            @block.tensor
            def _(pe):
                def step(new, old, ahead):
                    for s, g, r in new:
                        pe.wait_ge(n0, 1)
                        pe.sem_inc(n0, -1)
                        turn(nc, PA[s], tiles(N0[s], r), m.ident, r).then_inc(t0, 1)
                    for s, g, r in new:
                        pe.wait_ge(ht, 1)
                        pe.sem_inc(ht, -1)
                        pe.wait_ge(xl_read, 1)
                        pe.sem_inc(xl_read, -1)
                        rows_product(nc, PB[s], [(HT[s], m.wT["W1r"][:, :])], m.bias["b1"], m.ones_row, r
                                     ).then_inc(h1_ps, 1)
                    for s, g, r in new:
                        pe.wait_ge(h1_pe, 1)
                        pe.sem_inc(h1_pe, -1)
                        turn(nc, PA[s], tiles(H1[s], r), m.ident, r).then_inc(t1, 1)
                    for s, g, r in new:
                        pe.wait_ge(h1t, 1)
                        pe.sem_inc(h1t, -1)
                        rows_product(nc, PB[s], [(H1T[s], m.wT["W2r"][:, :])], m.bias["b2"], m.ones_row, r
                                     ).then_inc(y_ps, 1)
                    for s, g, r in old:
                        pe.wait_ge(n1[s % 2], 1)
                        pe.sem_inc(n1[s % 2], -1)
                        turn(nc, PA[s], tiles(N1[s], r), m.ident, r).then_inc(t2, 1)
                    for s, g, r in old:
                        pe.wait_ge(nt, 1)
                        pe.sem_inc(nt, -1)
                        rows_product(nc, PB[s], [(NT[s], m.wn["W"][:, :])], m.bias["b"], m.ones_row, r
                                     ).then_inc(xl_ps, 1)
                over_nodes(m, pe, step)

            @block.scalar
            def _(act):
                def step(new, old, ahead):
                    if new:
                        act.wait_ge(scaled, 1)
                        act.sem_inc(scaled, -1)
                    for s, g, r in new:
                        n = tiles(N0[s], r)
                        ln0.on_scalar(s, [n[:, a, :] for a in range(4)], four(X[s], r), ACT.Relu, r).then_inc(n0, 1)
                    for s, g, r in new:
                        c = r * TILES
                        act.wait_ge(t0, 1)
                        act.sem_inc(t0, -1)
                        nc.scalar.activation(HT[s][:, 0:c], PA[s][:, 0:c], ACT.Copy).then_inc(ht, 1)
                    for s, g, r in new:
                        act.wait_ge(h1_ps, 1)
                        act.sem_inc(h1_ps, -1)
                        act.wait_ge(h1_saved[s], 16)
                        act.sem_inc(h1_saved[s], -16)
                        nc.scalar.activation(H1[s][0:r, :], PB[s][0:r, :], ACT.Relu).then_inc(own_a, 1)
                        act.wait_ge(own_a, 1)
                        act.sem_inc(own_a, -1)
                        act.sem_inc(h1_pe, 1)
                        act.sem_inc(h1_out, 1)
                    for s, g, r in new:
                        c = r * TILES
                        act.wait_ge(t1, 1)
                        act.sem_inc(t1, -1)
                        nc.scalar.activation(H1T[s][:, 0:c], PA[s][:, 0:c], ACT.Copy).then_inc(h1t, 1)
                    if old:
                        ln1.root(act, old[0][0] // 2)
                    if ahead:
                        ln0.root(act, ahead[0][0] // 2)
                    for s, g, r in new:
                        act.wait_ge(y_ps, 1)
                        act.sem_inc(y_ps, -1)
                        nc.scalar.activation(Y[s][0:r, :], PB[s][0:r, :], ACT.Copy).then_inc(own_a, 1)
                        act.wait_ge(own_a, 1)
                        act.sem_inc(own_a, -1)
                        act.sem_inc(y_pool, 1)
                        act.sem_inc(y_dve, 1)
                    if old[1:]:
                        act.wait_ge(scaled1, 1)
                        act.sem_inc(scaled1, -1)
                    for s, g, r in old[1:]:
                        n = tiles(N1[s], r)
                        ln1.on_scalar(s, [n[:, a, :] for a in range(4)], four(X1[s], r), ACT.Relu, r
                                      ).then_inc(n1[1], 1)
                    for s, g, r in old:
                        c = r * TILES
                        act.wait_ge(t2, 1)
                        act.sem_inc(t2, -1)
                        nc.scalar.activation(NT[s][:, 0:c], PA[s][:, 0:c], ACT.Relu).then_inc(nt, 1)
                ln0.root(act, 0)
                over_nodes(m, act, step)
        ph.retire()



def nodes_last(m):
    nc = m.nc
    with ExitStack() as ctx:
        ph = Phase(m, "f", ctx, SLOTS)
        X, AT = ph.each("x", [P, TILES, P]), ph.each("at", [P, TILES, P])
        N0, XM, N1, R, OUT = (ph.each(k, [P, ROWS]) for k in ["n0", "xm", "n1", "r", "out"])
        NT = ph.each("nt", [P, ROWS])
        HID = ph.each("hid", [P, 4, ROWS])
        ln0, ln1 = Norm(ph, "ln0", 4), Norm(ph, "ln1", 4)
        PT = ph.ps_each("t")
        PH = [ph.ps(f"h{i}") for i in range(4)]
        x_in, saved = ph.sem_each("x_in"), ph.sem_each("saved")
        (x_free, scaled, n0, n1, t0, nt, hid_ps, hid_free, hid, o_ps, o_read, out_ready, own_d, own_a) = (
            ph.sem(k) for k in ["x_free", "scaled", "n0", "n1", "t0", "nt", "hid_ps", "hid_free", "hid",
                                "o_ps", "o_read", "out", "own_d", "own_a"])

        with nc.Block() as block:
            @block.sync
            def _(sp):
                def load(slots):
                    for s, g, r in slots:
                        sp.wait_ge(x_free, 1)
                        sp.sem_inc(x_free, -1)
                        sp.dma_start(X[s][0:r, :, :], node_rows(m.x3, g, r)).then_inc(x_in[s], 16)
                        sp.dma_start(AT[s][0:r, :, :], node_rows(m.att, g, r)).then_inc(x_in[s], 16)

                def step(new, old, ahead):
                    load(ahead)
                    for s, g, r in old:
                        sp.wait_ge(out_ready, 1)
                        sp.sem_inc(out_ready, -1)
                        sp.dma_start(node_rows(m.out, g, r), tiles(OUT[s], r)).then_inc(saved[s], 16)

                load([(0, 0, P), (1, 1, P)])
                over_nodes(m, sp, step)

            @block.gpsimd
            def _(pool):
                def step(new, old, ahead):
                    if new:
                        ln0.power(pool, new[0][0] // 2)
                        ln1.power(pool, new[0][0] // 2)
                over_nodes(m, pool, step)

            @block.vector
            def _(dve):
                ph.prime(dve, SLOTS, x_free, o_read, hid_free)
                ph.prime(dve, 16, *saved)
                ln0.start(dve, own_d)
                ln1.start(dve, own_d)

                def step(new, old, ahead):
                    if new:
                        h = new[0][0] // 2
                        for s, g, r in new:
                            dve.wait_ge(x_in[s], 32)
                            dve.sem_inc(x_in[s], -32)
                            last = ln0.stats(s, four(X[s], r), r)
                        last.then_inc(own_d, 1)
                        dve.wait_ge(own_d, 1)
                        dve.sem_inc(own_d, -1)
                        ln0.variances(dve, own_d, h)
                        ln0.shifts(dve, own_d, h)
                        dve.sem_inc(scaled, 1)
                        for s, g, r in new:
                            dve.wait_ge(n0, 1)
                            dve.sem_inc(n0, -1)
                            nc.vector.tensor_tensor(tiles(XM[s], r), tiles(N0[s], r), AT[s][0:r, :, :],
                                                              ALU.add).then_inc(own_d, 1)
                            dve.wait_ge(own_d, 1)
                            dve.sem_inc(own_d, -1)
                            last = ln1.stats(s, four(tiles(XM[s], r), r), r)
                        last.then_inc(own_d, 1)
                        dve.wait_ge(own_d, 1)
                        dve.sem_inc(own_d, -1)
                        ln1.variances(dve, own_d, h)
                        for s, g, r in new:
                            nc.vector.tensor_tensor(tiles(R[s], r), X[s][0:r, :, :], tiles(XM[s], r), ALU.add
                                                    ).then_inc(x_free, 1)
                        ln1.shifts(dve, own_d, h)
                        for s, g, r in new:
                            n = tiles(N1[s], r)
                            ln1.on_vector(s, [n[:, a, :] for a in range(4)], four(tiles(XM[s], r), r), r
                                          ).then_inc(n1, 1)
                    for s, g, r in old:
                        dve.wait_ge(o_ps, 1)
                        dve.sem_inc(o_ps, -1)
                        dve.wait_ge(saved[s], 16)
                        dve.sem_inc(saved[s], -16)
                        nc.vector.tensor_tensor(OUT[s][0:r, :], PT[s][0:r, :], R[s][0:r, :], ALU.add).then_inc(own_d, 1)
                        dve.wait_ge(own_d, 1)
                        dve.sem_inc(own_d, -1)
                        dve.sem_inc(out_ready, 1)
                        dve.sem_inc(o_read, 1)
                over_nodes(m, dve, step)

            @block.tensor
            def _(pe):
                def step(new, old, ahead):
                    for s, g, r in old:
                        c = r * TILES
                        pe.wait_ge(nt, 1)
                        pe.sem_inc(nt, -1)
                        for h in range(4):
                            pe.wait_ge(hid_free, 1)
                            pe.sem_inc(hid_free, -1)
                            nc.tensor.matmul(PH[h][:, 0:c], m.W1[:, h * P:(h + 1) * P], NT[s][:, 0:c], start=True,
                                             stop=True).then_inc(hid_ps, 1)
                    for s, g, r in old:
                        pe.wait_ge(hid, 1)
                        pe.sem_inc(hid, -1)
                        rows_product(nc, PT[s], [(HID[s][:, h, :], m.W2[:, h, :]) for h in range(4)], m.bias["bf2"],
                                     m.ones_row, r).then_inc(o_ps, 1)
                    for s, g, r in new:
                        pe.wait_ge(n1, 1)
                        pe.sem_inc(n1, -1)
                        pe.wait_ge(o_read, 1)
                        pe.sem_inc(o_read, -1)
                        turn(nc, PT[s], tiles(N1[s], r), m.ident, r).then_inc(t0, 1)
                over_nodes(m, pe, step)

            @block.scalar
            def _(act):
                def gelus(slots):
                    for s, g, r in slots:
                        c = r * TILES
                        for h in range(4):
                            act.wait_ge(hid_ps, 1)
                            act.sem_inc(hid_ps, -1)
                            one = nc.scalar.activation(HID[s][:, h, 0:c], PH[h][:, 0:c], ACT.Gelu,
                                                       bias=m.bf1[:, h:h + 1])
                            if h < 3:
                                one.then_inc(hid_free, 1)
                            else:
                                one.then_inc(own_a, 1)
                                act.wait_ge(own_a, 1)
                                act.sem_inc(own_a, -1)
                                act.sem_inc(hid_free, 1)
                                act.sem_inc(hid, 1)

                def step(new, old, ahead):
                    gelus(old[0:1])
                    if new:
                        act.wait_ge(scaled, 1)
                        act.sem_inc(scaled, -1)
                    for s, g, r in new:
                        n = tiles(N0[s], r)
                        ln0.on_scalar(s, [n[:, a, :] for a in range(4)], four(X[s], r), ACT.Relu, r).then_inc(n0, 1)
                    gelus(old[1:])
                    for s, g, r in new:
                        c = r * TILES
                        act.wait_ge(t0, 1)
                        act.sem_inc(t0, -1)
                        nc.scalar.activation(NT[s][:, 0:c], PT[s][:, 0:c], ACT.Copy).then_inc(nt, 1)
                over_nodes(m, act, step)
        ph.retire()



def over_edges(m, eng, body):
    with eng.Fori(0, m.edge_pairs) as i:
        body(i, [(0, 2 * i), (1, 2 * i + 1)])


def row_of(v, g):
    return v[bass.ds(g * ROWS, ROWS)].rearrange("(o d) -> o d", o=1).broadcast_to([P, ROWS])


def edge_rows(table, g):
    return table[bass.ds(g * ROWS, ROWS), :].rearrange("(a p) d -> p a d", p=P)


class Sockets:

    def __init__(self, ph, gathers, scatter, adds=False):
        self.ph, self.m, self.gathers, self.scatter, self.adds = ph, ph.m, gathers, scatter, adds
        self.gi = ph.each("gi", [P, 8], I32)
        self.gi_in, self.gi_free, self.buf_free = ph.sem_each("gi_in"), ph.sem("gi_free"), ph.sem("buf_free")
        self.got = [ph.counter(f"got{s}") for s in range(ph.slots)]
        self.ticks = ph.counter("ticks")
        if scatter:
            self.si = ph.each("si", [P, 4], I32)
            self.si_in, self.si_free = ph.sem_each("si_in"), ph.sem("si_free")
            self.ready, self.out_free = ph.sem("sc_ready"), ph.sem("sc_free")
            self.put = [ph.counter(f"put{s}") for s in range(ph.slots)]
            self.si_made = ph.sem("si_made")
        self.each = 64 * len(gathers)

    def prime(self, eng):
        self.ph.prime(eng, self.ph.slots, self.gi_free, self.buf_free)
        if self.scatter:
            self.ph.prime(eng, self.ph.slots, self.si_free, self.out_free)

    def load_gather_idx(self, sp, source, slots):
        for s, g, *_ in slots:
            sp.wait_ge(self.gi_free, 1)
            sp.sem_inc(self.gi_free, -1)
            w = source.shape[2]
            sp.dma_start(self.gi[s][:, 0:w], source[:, bass.ds(g, 1), :].rearrange("p o w -> p (o w)")
                         ).then_inc(self.gi_in[s], 16)

    def load_scatter_idx(self, sp, slots):
        for s, g, *_ in slots:
            sp.wait_ge(self.si_free, 1)
            sp.sem_inc(self.si_free, -1)
            sp.dma_start(self.si[s][:, :], self.m.scatter_idx[:, bass.ds(g, 1), :].rearrange("p o w -> p (o w)")
                         ).then_inc(self.si_in[s], 16)

    def gather(self, pool, slots, bounds):
        nc = self.m.nc
        for s, g, *_ in slots:
            pool.wait_ge(self.buf_free, 1)
            pool.sem_inc(self.buf_free, -1)
            pool.wait_ge(self.gi_in[s], 16)
            pool.sem_inc(self.gi_in[s], -16)
            for table, buf, c in self.gathers:
                for a in range(TILES):
                    nc.gpsimd.indirect_dma_start(
                        buf[s][:, a, :], None, table,
                        bass.IndirectOffsetOnAxis(ap=self.gi[s][:, c + a:c + a + 1], axis=0),
                        bounds_check=bounds, oob_is_err=False).then_inc(self.got[s], 16)

    def free_gather_idx(self, pool, i, slots):
        for s, g, *_ in slots:
            pool.wait_ge(self.got[s], i * self.each + self.each)
            pool.sem_inc(self.ticks, 1)
            pool.sem_inc(self.gi_free, 1)

    def scatter_rows(self, pool, slots, bounds):
        nc = self.m.nc
        table, buf = self.scatter
        for s, g, *_ in slots:
            pool.wait_ge(self.ready, 1)
            pool.sem_inc(self.ready, -1)
            if self.adds:
                pool.wait_ge(self.si_made, 1)
                pool.sem_inc(self.si_made, -1)
            else:
                pool.wait_ge(self.si_in[s], 16)
                pool.sem_inc(self.si_in[s], -16)
            for a in range(TILES):
                where = bass.IndirectOffsetOnAxis(ap=self.si[s][:, a:a + 1], axis=0)
                if self.adds:
                    nc.gpsimd.indirect_dma_start(table, where, buf[s][:, a, :], None, bounds_check=bounds,
                                                 oob_is_err=True, compute_op=ALU.add).then_inc(self.put[s], 16)
                else:
                    nc.gpsimd.indirect_dma_start(table, where, buf[s][:, a, :], None, bounds_check=bounds,
                                                 oob_is_err=False).then_inc(self.put[s], 16)

    def scattered(self, pool, i, slots):
        for s, g, *_ in slots:
            pool.wait_ge(self.put[s], i * 64 + 64)
            pool.sem_inc(self.ticks, 1)
            pool.sem_inc(self.si_free, 1)
            pool.sem_inc(self.out_free, 1)

    def drive_adds(self, pool, bounds_in, bounds_out):
        pairs = self.m.edge_pairs
        bi, bo = pool.to_reg(bounds_in), pool.to_reg(bounds_out)

        def turn_of(i, first, more):
            now, ahead = [(0, 2 * i), (1, 2 * i + 1)], [(0, 2 * i + 2), (1, 2 * i + 3)]
            self.free_gather_idx(pool, i, now)
            if more:
                self.gather(pool, ahead[0:1], bi)
            if not first:
                self.scattered(pool, i - 1, now[1:2])
            self.scatter_rows(pool, now[0:1], bo)
            if more:
                self.gather(pool, ahead[1:2], bi)
            self.scattered(pool, i, now[0:1])
            self.scatter_rows(pool, now[1:2], bo)

        self.gather(pool, [(0, 0), (1, 1)], bi)
        turn_of(0, True, pairs > 1)
        if pairs > 2:
            with pool.Fori(1, pairs - 1) as i:
                turn_of(i, False, True)
        if pairs > 1:
            turn_of(pairs - 1, False, False)
        self.scattered(pool, pairs - 1, [(1, self.m.G - 1)])

    def next_lot(self, slots):
        if not slots or (isinstance(slots[0][2], int) and slots[0][2] + 1 >= self.m.edge_lots):
            return []
        return [(s, g + SLOTS, i + 1) for s, g, i in slots]

    def drive_lots(self, pool, bounds_in, bounds_out):
        m = self.m
        bi, bo = pool.to_reg(bounds_in), pool.to_reg(bounds_out)

        def step(new, old, ahead):
            self.gather(pool, self.next_lot(new), bi)
            for s, g, i in new:
                if not (isinstance(i, int) and i == 0):
                    pool.wait_ge(self.put[s], i * 64)
                    pool.sem_inc(self.ticks, 1)
                    pool.sem_inc(self.si_free, 1)
                    pool.sem_inc(self.out_free, 1)
            self.scatter_rows(pool, old, bo)

        self.gather(pool, [(s, s, 0) for s in range(SLOTS)], bi)
        over_edge_lots(m, pool, step)
        for s in range(SLOTS):
            pool.wait_ge(self.put[s], m.edge_lots * 64)
            pool.sem_inc(self.ticks, 1)
            pool.sem_inc(self.si_free, 1)
            pool.sem_inc(self.out_free, 1)


def segment_sum(nc, out, s, keep, cols):
    return nc.vector.tensor_tensor_scan(out[s][:, :], keep, cols, out[s - 1][:, ROWS - 1:ROWS], ALU.mult, ALU.add)


def finish_guard(nc, dve, own, y, pos, neg, fin):
    nc.vector.tensor_scalar(pos[:, :], y[:, :], 0.0, NAN_LIMIT, ALU.max, ALU.min)
    nc.vector.tensor_scalar(neg[:, :], y[:, :], 0.0, -NAN_LIMIT, ALU.min, ALU.max)
    nc.vector.tensor_scalar(fin[:, :], y[:, :], 0.0, 0.0, ALU.mult, ALU.is_equal).then_inc(own, 1)
    dve.wait_ge(own, 1)
    dve.sem_inc(own, -1)
    nc.vector.tensor_tensor(pos[:, :], pos[:, :], neg[:, :], ALU.add).then_inc(own, 1)
    dve.wait_ge(own, 1)
    dve.sem_inc(own, -1)
    nc.vector.copy_predicated(pos[:, :], fin[:, :], y[:, :]).then_inc(own, 1)
    dve.wait_ge(own, 1)
    dve.sem_inc(own, -1)



def sage_first(m):
    nc = m.nc
    x = m.ins["x"]
    m.h1_edge = m.dram("h1_edge", (m.EP, P))
    m.x_edge = m.dram("x_edge", (m.EP, P))
    m.att = m.dram("att", (m.N, P))
    with ExitStack() as ctx:
        ph = Phase(m, "s", ctx, SLOTS)
        XS, XD, N0, N1, H1 = (ph.each(k, [P, TILES, P]) for k in ["xs", "xd", "n0", "n1", "h1"])
        ln0 = Norm(ph, "ln0", 8)
        KEEP, RD = ph.each("keep", [P, ROWS], BF16), ph.each("rd", [P, ROWS])
        HS, HD, AG, MEAN = (ph.each(k, [P, ROWS]) for k in ["hs", "hd", "ag", "mean"])
        PA, PB = ph.ps_each("a"), ph.ps_each("b")
        so = Sockets(ph, [(x, XS, 0), (x, XD, 4)], (m.h1, H1))
        row_in, xd_saved, h1_saved = (ph.sem_each(k) for k in ["row_in", "xd_saved", "h1_saved"])
        (row_free, n01, turned, hs, hd, mean, h1_ps, h1_read, h1_out, own_d, own_a) = (ph.sem(k) for k in [
            "row_free", "n01", "turned", "hs", "hd", "mean", "h1_ps", "h1_read", "h1_out", "own_d", "own_a"])
        filled, tick_sp, tick_d = (ph.counter(k) for k in ["filled", "tick_sp", "tick_d"])
        parts = 5
        run = m.N // 32 // parts

        with nc.Block() as block:
            @block.sync
            def _(sp):
                def rows(slots):
                    for s, g, i in slots:
                        sp.wait_ge(row_free, 1)
                        sp.sem_inc(row_free, -1)
                        sp.dma_start(KEEP[s][:, :], row_of(m.keep_row, g)).then_inc(row_in[s], 16)
                        sp.dma_start(RD[s][:, :], row_of(m.row["rdeg"], g)).then_inc(row_in[s], 16)

                def step(new, old, ahead):
                    for s, g, i in new:
                        sp.wait_ge(so.got[s], i * so.each + so.each)
                        sp.sem_inc(tick_sp, 1)
                        sp.dma_start(edge_rows(m.x_edge, g), XD[s][:, :, :]).then_inc(xd_saved[s], 16)
                    so.load_gather_idx(sp, m.gather_idx, so.next_lot(new))
                    rows(ahead)
                    so.load_scatter_idx(sp, new)
                    for s, g, i in new:
                        sp.wait_ge(h1_out, 1)
                        sp.sem_inc(h1_out, -1)
                        sp.dma_start(edge_rows(m.h1_edge, g), H1[s][:, :, :]).then_inc(h1_saved[s], 16)
                so.load_gather_idx(sp, m.gather_idx, [(s, s, 0) for s in range(SLOTS)])
                rows([(0, 0, 0), (1, 1, 0)])
                over_edge_lots(m, sp, step)

            @block.gpsimd
            def _(pool):
                so.drive_lots(pool, m.N - 1, m.N - 1)

            @block.vector
            def _(dve):
                so.prime(dve)
                ph.prime(dve, SLOTS, row_free, h1_read)
                ph.prime(dve, 16, *h1_saved)
                ln0.start(dve, own_d)
                nc.vector.memset(AG[-1][:, ROWS - 1:ROWS], 0.0).then_inc(own_d, 1)
                dve.wait_ge(own_d, 1)
                dve.sem_inc(own_d, -1)

                def step(new, old, ahead):
                    for s, g, i in new:
                        dve.wait_ge(so.got[s], i * so.each + so.each)
                        dve.sem_inc(tick_d, 1)
                        dve.sem_inc(so.gi_free, 1)
                        last = ln0.stats(s, four(XS[s]) + four(XD[s]))
                    if new:
                        last.then_inc(own_d, 1)
                        dve.wait_ge(own_d, 1)
                        dve.sem_inc(own_d, -1)
                        ln0.variances(dve, own_d, new[0][0] // 2)
                        ln0.scales(dve, own_d, new[0][0] // 2)
                    for s, g, i in new:
                        ln0.on_vector(s, four(N0[s]) + four(N1[s]), four(XS[s]) + four(XD[s])).then_inc(own_d, 1)
                        dve.wait_ge(own_d, 1)
                        dve.sem_inc(own_d, -1)
                        dve.sem_inc(n01, 1)
                        dve.wait_ge(xd_saved[s], 16)
                        dve.sem_inc(xd_saved[s], -16)
                        dve.sem_inc(so.buf_free, 1)
                    for s, g, i in new:
                        dve.wait_ge(hs, 1)
                        dve.sem_inc(hs, -1)
                        dve.wait_ge(row_in[s], 32)
                        dve.sem_inc(row_in[s], -32)
                        segment_sum(nc, AG, s, KEEP[s][:, :], HS[s][:, :]).then_inc(own_d, 1)
                        dve.wait_ge(own_d, 1)
                        dve.sem_inc(own_d, -1)
                        nc.vector.tensor_tensor(MEAN[s][:, :], AG[s][:, :], RD[s][:, :], ALU.mult).then_inc(own_d, 1)
                        dve.wait_ge(own_d, 1)
                        dve.sem_inc(own_d, -1)
                        dve.sem_inc(mean, 1)
                        dve.sem_inc(row_free, 1)
                over_edge_lots(m, dve, step)

            @block.tensor
            def _(pe):
                def step(new, old, ahead):
                    for s, g, i in new:
                        pe.wait_ge(n01, 1)
                        pe.sem_inc(n01, -1)
                        pe.wait_ge(h1_read, 1)
                        pe.sem_inc(h1_read, -1)
                        turn(nc, PA[s], N0[s], m.ident)
                        turn(nc, PB[s], N1[s], m.ident).then_inc(turned, 1)
                    for s, g, i in new:
                        pe.wait_ge(hd, 1)
                        pe.sem_inc(hd, -1)
                        pe.wait_ge(mean, 1)
                        pe.sem_inc(mean, -1)
                        rows_product(nc, PA[s], [(MEAN[s], m.wT["W1l"][:, :]), (HD[s], m.wT["W1r"][:, :])],
                                     m.bias["b1"], m.ones_row).then_inc(h1_ps, 1)
                over_edge_lots(m, pe, step)

            @block.scalar
            def _(act):
                for k in range(parts):
                    part = m.att[k * 32 * run:(k + 1) * 32 * run, :].rearrange("(p r) d -> p r d", p=32)
                    fill = m.bo_rows[:, :].rearrange("p (o d) -> p o d", o=1).broadcast_to([32, run, P])
                    act.dma_start(part, fill).then_inc(filled, 16)

                def step(new, old, ahead):
                    if new:
                        ln0.root(act, new[0][0] // 2)
                    for s, g, i in new:
                        act.wait_ge(turned, 1)
                        act.sem_inc(turned, -1)
                        nc.scalar.activation(HS[s][:, :], PA[s][:, :], ACT.Relu).then_inc(hs, 1)
                        nc.scalar.activation(HD[s][:, :], PB[s][:, :], ACT.Relu).then_inc(hd, 1)
                    for s, g, i in new:
                        act.wait_ge(h1_ps, 1)
                        act.sem_inc(h1_ps, -1)
                        act.wait_ge(h1_saved[s], 16)
                        act.sem_inc(h1_saved[s], -16)
                        act.wait_ge(so.out_free, 1)
                        act.sem_inc(so.out_free, -1)
                        nc.scalar.activation(H1[s][:, :, :].rearrange("p a d -> p (a d)"), PA[s][:, :],
                                                       ACT.Relu).then_inc(own_a, 1)
                        act.wait_ge(own_a, 1)
                        act.sem_inc(own_a, -1)
                        act.sem_inc(h1_out, 1)
                        act.sem_inc(h1_read, 1)
                        act.sem_inc(so.ready, 1)
                over_edge_lots(m, act, step)
                act.wait_ge(filled, 16 * parts)
        ph.retire()



def sage_second(m):
    nc = m.nc
    with ExitStack() as ctx:
        ph = Phase(m, "t", ctx, SLOTS)
        HS0, HD0, XD = (ph.each(k, [P, TILES, P]) for k in ["hs0", "hd0", "xd"])
        KEEP, RD = ph.each("keep", [P, ROWS], BF16), ph.each("rd", [P, ROWS])
        EC = ph.each("ec", [P, 8])
        HS, HD, AG, MEAN, Y, POS, NEG = (ph.each(k, [P, ROWS]) for k in ["hs", "hd", "ag", "mean", "y", "pos", "neg"])
        FIN = ph.each("fin", [P, ROWS], I32)
        X1 = ph.each("x1", [P, TILES, WIDE])
        PA, PB = ph.ps_each("a"), ph.ps_each("b")
        so = Sockets(ph, [(m.h1, HS0, 0)], (m.x1, X1))
        row_in, x_in = ph.sem_each("row_in"), ph.sem_each("x_in")
        (row_free, x_free, turned, hs, hd, mean, y_ps, y_read, y, own_d, own_a) = (ph.sem(k) for k in [
            "row_free", "x_free", "turned", "hs", "hd", "mean", "y_ps", "y_read", "y", "own_d", "own_a"])
        tick_pe = ph.counter("tick_pe")

        with nc.Block() as block:
            @block.sync
            def _(sp):
                def rows(slots):
                    for s, g, i in slots:
                        sp.wait_ge(row_free, 1)
                        sp.sem_inc(row_free, -1)
                        sp.dma_start(KEEP[s][:, :], row_of(m.keep_row, g)).then_inc(row_in[s], 16)
                        sp.dma_start(RD[s][:, :], row_of(m.row["rdeg"], g)).then_inc(row_in[s], 16)
                    for s, g, i in slots:
                        sp.wait_ge(x_free, 1)
                        sp.sem_inc(x_free, -1)
                        sp.dma_start(HD0[s][:, :, :], edge_rows(m.h1_edge, g)).then_inc(x_in[s], 16)
                        sp.dma_start(XD[s][:, :, :], edge_rows(m.x_edge, g)).then_inc(x_in[s], 16)
                        sp.dma_start(EC[s][:, :], m.edge_col[:, bass.ds(g, 1), :].rearrange("p o w -> p (o w)")
                                     ).then_inc(x_in[s], 16)

                def step(new, old, ahead):
                    so.load_gather_idx(sp, m.gather_idx, so.next_lot(new))
                    rows(ahead)
                    so.load_scatter_idx(sp, new)
                so.load_gather_idx(sp, m.gather_idx, [(s, s, 0) for s in range(SLOTS)])
                rows([(0, 0, 0), (1, 1, 0)])
                over_edge_lots(m, sp, step)

            @block.gpsimd
            def _(pool):
                so.drive_lots(pool, m.N - 1, m.N - 1)

            @block.vector
            def _(dve):
                so.prime(dve)
                ph.prime(dve, SLOTS, row_free, x_free, y_read)
                for s in range(SLOTS):
                    nc.vector.memset(X1[s][:, :, :], 1.0)
                nc.vector.memset(AG[-1][:, ROWS - 1:ROWS], 0.0).then_inc(own_d, 1)
                dve.wait_ge(own_d, 1)
                dve.sem_inc(own_d, -1)

                def step(new, old, ahead):
                    for s, g, i in new:
                        dve.wait_ge(hs, 1)
                        dve.sem_inc(hs, -1)
                        dve.wait_ge(row_in[s], 32)
                        dve.sem_inc(row_in[s], -32)
                        segment_sum(nc, AG, s, KEEP[s][:, :], HS[s][:, :]).then_inc(own_d, 1)
                        dve.wait_ge(own_d, 1)
                        dve.sem_inc(own_d, -1)
                        nc.vector.tensor_tensor(MEAN[s][:, :], AG[s][:, :], RD[s][:, :], ALU.mult).then_inc(own_d, 1)
                        dve.wait_ge(own_d, 1)
                        dve.sem_inc(own_d, -1)
                        dve.sem_inc(mean, 1)
                        dve.sem_inc(row_free, 1)
                    for s, g, i in new:
                        dve.wait_ge(y, 1)
                        dve.sem_inc(y, -1)
                        finish_guard(nc, dve, own_d, Y[s], POS[s], NEG[s], FIN[s])
                        dve.wait_ge(so.out_free, 1)
                        dve.sem_inc(so.out_free, -1)
                        nc.vector.tensor_copy(X1[s][:, :, P], EC[s][:, 0:4])
                        nc.vector.tensor_tensor(X1[s][:, :, 0:P], XD[s][:, :, :], tiles(POS[s]), ALU.add).then_inc(own_d, 1)
                        dve.wait_ge(own_d, 1)
                        dve.sem_inc(own_d, -1)
                        dve.sem_inc(so.ready, 1)
                        dve.sem_inc(x_free, 1)
                over_edge_lots(m, dve, step)

            @block.tensor
            def _(pe):
                def step(new, old, ahead):
                    for s, g, i in new:
                        pe.wait_ge(so.got[s], i * so.each + so.each)
                        pe.sem_inc(tick_pe, 1)
                        pe.sem_inc(so.gi_free, 1)
                        pe.wait_ge(x_in[s], 48)
                        pe.sem_inc(x_in[s], -48)
                        pe.wait_ge(y_read, 1)
                        pe.sem_inc(y_read, -1)
                        turn(nc, PA[s], HS0[s], m.ident)
                        turn(nc, PB[s], HD0[s], m.ident).then_inc(turned, 1)
                    for s, g, i in new:
                        pe.wait_ge(hd, 1)
                        pe.sem_inc(hd, -1)
                        pe.wait_ge(mean, 1)
                        pe.sem_inc(mean, -1)
                        rows_product(nc, PA[s], [(MEAN[s], m.wT["W2l"][:, :]), (HD[s], m.wT["W2r"][:, :])],
                                     m.bias["b2"], m.ones_row).then_inc(y_ps, 1)
                over_edge_lots(m, pe, step)

            @block.scalar
            def _(act):
                def step(new, old, ahead):
                    for s, g, i in new:
                        act.wait_ge(turned, 1)
                        act.sem_inc(turned, -1)
                        act.sem_inc(so.buf_free, 1)
                        nc.scalar.activation(HS[s][:, :], PA[s][:, :], ACT.Copy).then_inc(hs, 1)
                        nc.scalar.activation(HD[s][:, :], PB[s][:, :], ACT.Copy).then_inc(hd, 1)
                    for s, g, i in new:
                        act.wait_ge(y_ps, 1)
                        act.sem_inc(y_ps, -1)
                        nc.scalar.activation(Y[s][:, :], PA[s][:, :], ACT.Copy).then_inc(own_a, 1)
                        act.wait_ge(own_a, 1)
                        act.sem_inc(own_a, -1)
                        act.sem_inc(y, 1)
                        act.sem_inc(y_read, 1)
                over_edge_lots(m, act, step)
        ph.retire()



class Online:

    def __init__(self, ph):
        self.nc = ph.m.nc
        self.M = ph.each("m", [P, 1 + ROWS])
        self.D, self.W, self.V, self.Z, self.S = (ph.each(k, [P, ROWS]) for k in ["d", "w", "v", "z", "s"])
        self.diffs, self.exps = ph.sem("diffs"), ph.sem("exps")

    def start(self, dve, own):
        nc = self.nc
        for t in (self.M[-1][:, ROWS:ROWS + 1], self.Z[-1][:, ROWS - 1:ROWS], self.S[-1][:, ROWS - 1:ROWS]):
            last = nc.vector.memset(t, 0.0)
        last.then_inc(own, 1)
        dve.wait_ge(own, 1)
        dve.sem_inc(own, -1)

    def maxima(self, dve, own, s, scores, neg, keep=None):
        nc, M, D, W = self.nc, self.M, self.D, self.W
        nc.vector.tensor_copy(M[s][:, 0:1], M[s - 1][:, ROWS:ROWS + 1])
        before = M[s - 1][:, ROWS:ROWS + 1]
        if keep is None:
            one = nc.vector.tensor_tensor_scan(M[s][:, 1:], neg, scores, before, ALU.add, ALU.max)
        else:
            one = nc.vector.tensor_tensor_scan(M[s][:, 1:], keep, scores, before, ALU.mult, ALU.max)
        one.then_inc(own, 1)
        dve.wait_ge(own, 1)
        dve.sem_inc(own, -1)
        nc.vector.tensor_tensor(D[s][:, :], M[s][:, 0:ROWS], M[s][:, 1:], ALU.subtract).then_inc(own, 1)
        dve.wait_ge(own, 1)
        dve.sem_inc(own, -1)
        nc.vector.tensor_tensor(D[s][:, :], D[s][:, :], neg, ALU.min)
        nc.vector.tensor_tensor(W[s][:, :], scores, M[s][:, 1:], ALU.subtract).then_inc(self.diffs, 1)

    def exponentials(self, act, s):
        act.wait_ge(self.diffs, 1)
        act.sem_inc(self.diffs, -1)
        self.nc.scalar.activation(self.D[s][:, :], self.D[s][:, :], ACT.Exp)
        return self.nc.scalar.activation(self.W[s][:, :], self.W[s][:, :], ACT.Exp)

    def sums(self, dve, own, s, values):
        nc, Z, S = self.nc, self.Z, self.S
        dve.wait_ge(self.exps, 1)
        dve.sem_inc(self.exps, -1)
        nc.vector.tensor_tensor(self.V[s][:, :], self.W[s][:, :], values, ALU.mult).then_inc(own, 1)
        dve.wait_ge(own, 1)
        dve.sem_inc(own, -1)
        nc.vector.tensor_tensor_scan(Z[s][:, :], self.D[s][:, :], self.W[s][:, :], Z[s - 1][:, ROWS - 1:ROWS],
                                     ALU.mult, ALU.add)
        nc.vector.tensor_tensor_scan(S[s][:, :], self.D[s][:, :], self.V[s][:, :],
                                               S[s - 1][:, ROWS - 1:ROWS], ALU.mult, ALU.add).then_inc(own, 1)
        dve.wait_ge(own, 1)
        dve.sem_inc(own, -1)



def gat(m):
    nc = m.nc
    m.xl_edge = m.dram("xl_edge", (m.EP, P))
    m.dis_src = m.dram("dis_src", (P, m.G, 4))
    with ExitStack() as ctx:
        ph = Phase(m, "g", ctx, SLOTS)
        XS, XD = ph.each("xs", [P, TILES, WIDE]), ph.each("xd", [P, TILES, WIDE])
        N0, N1, XR = (ph.each(k, [P, TILES, P]) for k in ["n0", "n1", "xr"])
        ln0, ln2 = Norm(ph, "ln0", 8), Norm(ph, "ln2", 4)
        NEG = ph.each("neg", [P, ROWS], BF16)
        EC, DS, RZ = ph.each("ec", [P, 8]), ph.each("ds", [P, 4]), ph.each("rz", [P, TILES * 4])
        HS, HD, FS, E1 = (ph.each(k, [P, ROWS]) for k in ["hs", "hd", "fs", "e1"])
        X2, XL, X3 = (ph.each(k, [P, TILES, P]) for k in ["x2", "xl", "x3"])
        on = Online(ph)
        PA, PB = ph.ps_each("a"), ph.ps_each("b")
        so = Sockets(ph, [(m.x1, XS, 0), (m.x1, XD, 4)], (m.x3, X3))
        row_in, xl_saved, ds_saved = (ph.sem_each(k) for k in ["row_in", "xl_saved", "ds_saved"])
        (row_free, scaled0, scaled2, n01, turned, hs, hd, proj, e1, e2, score, summed, h_ps, n2, t2, h2, xl_ps, xl_read,
         xl_out, own_d, own_a) = (ph.sem(k) for k in [
             "row_free", "scaled0", "scaled2", "n01", "turned", "hs", "hd", "proj", "e1", "e2", "score", "summed",
             "h_ps", "n2", "t2", "h2", "xl_ps", "xl_read", "xl_out", "own_d", "own_a"])
        tick_d = ph.counter("tick_d")

        with nc.Block() as block:
            @block.sync
            def _(sp):
                def rows(slots):
                    for s, g, i in slots:
                        sp.wait_ge(row_free, 1)
                        sp.sem_inc(row_free, -1)
                        sp.dma_start(NEG[s][:, :], row_of(m.neg_row, g)).then_inc(row_in[s], 16)
                        sp.dma_start(EC[s][:, :], m.edge_col[:, bass.ds(g, 1), :].rearrange("p o w -> p (o w)")
                                     ).then_inc(row_in[s], 16)

                def step(new, old, ahead):
                    so.load_gather_idx(sp, m.gather_idx, so.next_lot(new))
                    so.load_scatter_idx(sp, old)
                    for s, g, i in old:
                        sp.wait_ge(xl_out, 1)
                        sp.sem_inc(xl_out, -1)
                        sp.dma_start(edge_rows(m.xl_edge, g), XL[s][:, :, :]).then_inc(xl_saved[s], 16)
                        sp.dma_start(m.dis_src[:, bass.ds(g, 1), :].rearrange("p o w -> p (o w)"), DS[s][:, :]
                                     ).then_inc(ds_saved[s], 16)
                    rows(ahead)
                so.load_gather_idx(sp, m.gather_idx, [(s, s, 0) for s in range(SLOTS)])
                rows([(0, 0, 0), (1, 1, 0)])
                over_edge_lots(m, sp, step)

            @block.gpsimd
            def _(pool):
                so.drive_lots(pool, m.N - 1, m.N - 1)

            @block.vector
            def _(dve):
                so.prime(dve)
                ph.prime(dve, SLOTS, row_free, xl_read)
                ph.prime(dve, 16, *xl_saved, *ds_saved)
                ln0.start(dve, own_d)
                ln2.start(dve, own_d)
                on.start(dve, own_d)

                def gathered(slots):
                    for s, g, i in slots:
                        dve.wait_ge(so.got[s], i * so.each + so.each)
                        dve.sem_inc(tick_d, 1)
                        dve.sem_inc(so.gi_free, 1)
                        last = ln0.stats(s, four(XS[s]) + four(XD[s]))
                    if slots:
                        last.then_inc(own_d, 1)
                        dve.wait_ge(own_d, 1)
                        dve.sem_inc(own_d, -1)
                        ln0.variances(dve, own_d, slots[0][0] // 2)

                def scales(slots):
                    ln0.scales(dve, own_d, slots[0][0] // 2)
                    dve.sem_inc(scaled0, 1)

                def step(new, old, ahead):
                    for s, g, i in old:
                        on.sums(dve, own_d, s, FS[s][:, :])
                        dve.sem_inc(summed, 1)
                    for s, g, i in old:
                        dve.wait_ge(h_ps, 1)
                        dve.sem_inc(h_ps, -1)
                        nc.vector.reciprocal(RZ[s][:, :], PB[s][:, 0:TILES * 4]).then_inc(own_d, 1)
                        dve.wait_ge(own_d, 1)
                        dve.sem_inc(own_d, -1)
                        rz = RZ[s][:, :].rearrange("p (a o) -> p a o", o=1).broadcast_to([P, TILES * 4, 32])
                        x2 = X2[s][:, :, :].rearrange("p a (h d) -> p (a h) d", d=32)
                        nc.vector.tensor_tensor(x2, PA[s][:, :].rearrange("p (a d) -> p a d", d=32), rz,
                                                          ALU.mult).then_inc(own_d, 1)
                        dve.wait_ge(own_d, 1)
                        dve.sem_inc(own_d, -1)
                        nc.vector.scalar_tensor_tensor(X2[s][:, :, :], X2[s][:, :, :], 0.0, XR[s][:, :, :],
                                                                 ALU.max, ALU.add).then_inc(own_d, 1)
                        dve.wait_ge(own_d, 1)
                        dve.sem_inc(own_d, -1)
                        last = ln2.stats(s, four(X2[s]))
                    if old:
                        last.then_inc(own_d, 1)
                        dve.wait_ge(own_d, 1)
                        dve.sem_inc(own_d, -1)
                        ln2.variances(dve, own_d, old[0][0] // 2)
                    gathered(ahead)
                    for s, g, i in new:
                        dve.wait_ge(e1, 1)
                        dve.sem_inc(e1, -1)
                        nc.vector.scalar_tensor_tensor(E1[s][:, :], E1[s][:, :], 0.2, E1[s][:, :], ALU.mult, ALU.max
                                                       ).then_inc(e2, 1)
                    if old:
                        ln2.scales(dve, own_d, old[0][0] // 2)
                        dve.sem_inc(scaled2, 1)
                    if ahead:
                        scales(ahead)
                    for s, g, i in new:
                        dve.wait_ge(score, 1)
                        dve.sem_inc(score, -1)
                        dve.wait_ge(row_in[s], 32)
                        dve.sem_inc(row_in[s], -32)
                        on.maxima(dve, own_d, s, PB[s][:, :], NEG[s][:, :])
                    for s, g, i in old:
                        dve.wait_ge(xl_ps, 1)
                        dve.sem_inc(xl_ps, -1)
                        dve.wait_ge(xl_saved[s], 16)
                        dve.sem_inc(xl_saved[s], -16)
                        for a in range(4):
                            last = nc.vector.tensor_scalar(XL[s][:, a, :], PB[s][:, a * P:(a + 1) * P],
                                                           EC[s][:, a:a + 1], None, ALU.mult)
                        last.then_inc(own_d, 1)
                        dve.wait_ge(own_d, 1)
                        dve.sem_inc(own_d, -1)
                        dve.sem_inc(xl_out, 1)
                        dve.sem_inc(xl_read, 1)
                        dve.wait_ge(so.out_free, 1)
                        dve.sem_inc(so.out_free, -1)
                        for a in range(4):
                            last = nc.vector.scalar_tensor_tensor(X3[s][:, a, :], XL[s][:, a, :], EC[s][:, a:a + 1],
                                                                  X2[s][:, a, :], ALU.mult, ALU.add)
                        last.then_inc(own_d, 1)
                        dve.wait_ge(own_d, 1)
                        dve.sem_inc(own_d, -1)
                        dve.sem_inc(so.ready, 1)
                        dve.sem_inc(row_free, 1)
                gathered([(0, 0, 0), (1, 1, 0)])
                scales([(0, 0, 0), (1, 1, 0)])
                over_edge_lots(m, dve, step)

            @block.tensor
            def _(pe):
                def step(new, old, ahead):
                    def turn_new(slots):
                        for s, g, i in slots:
                            pe.wait_ge(n01, 1)
                            pe.sem_inc(n01, -1)
                            pe.wait_ge(xl_read, 1)
                            pe.sem_inc(xl_read, -1)
                            turn(nc, PA[s], N0[s], m.ident)
                            turn(nc, PB[s], N1[s], m.ident).then_inc(turned, 1)
                    turn_new(new[0:1])
                    for s, g, i in old:
                        pe.wait_ge(summed, 1)
                        pe.sem_inc(summed, -1)
                        turn(nc, PA[s], tiles(on.S[s]), m.ident)
                        for a in range(TILES):
                            last = nc.tensor.matmul(PB[s][:, a * 4:a * 4 + 4], on.Z[s][:, a * P:(a + 1) * P],
                                                    m.heads4[:, :], start=True, stop=True)
                        last.then_inc(h_ps, 1)
                    turn_new(new[1:])
                    for s, g, i in new:
                        pe.wait_ge(hs, 1)
                        pe.sem_inc(hs, -1)
                        nc.tensor.matmul(PA[s][:, :], m.wn["Ws"][:, :], HS[s][:, :], start=True, stop=True)
                        pe.wait_ge(hd, 1)
                        pe.sem_inc(hd, -1)
                        nc.tensor.matmul(PB[s][:, :], m.wn["Ws"][:, :], HS[s][:, :], start=True, stop=False)
                        nc.tensor.matmul(PB[s][:, :], m.wn["Wd"][:, :], HD[s][:, :], start=False, stop=True
                                         ).then_inc(proj, 1)
                    for s, g, i in new:
                        pe.wait_ge(e2, 1)
                        pe.sem_inc(e2, -1)
                        nc.tensor.matmul(PB[s][:, :], m.attn_heads[:, :], E1[s][:, :], start=True, stop=True
                                         ).then_inc(score, 1)
                    for s, g, i in old:
                        pe.wait_ge(n2, 1)
                        pe.sem_inc(n2, -1)
                        turn(nc, PA[s], N0[s], m.ident).then_inc(t2, 1)
                    for s, g, i in old:
                        pe.wait_ge(h2, 1)
                        pe.sem_inc(h2, -1)
                        rows_product(nc, PB[s], [(HD[s], m.wn["W"][:, :])], m.bias["b"], m.ones_row
                                     ).then_inc(xl_ps, 1)
                over_edge_lots(m, pe, step)

            @block.scalar
            def _(act):
                def step(new, old, ahead):
                    if new:
                        act.wait_ge(scaled0, 1)
                        act.sem_inc(scaled0, -1)
                    for s, g, i in new:
                        ln0.on_scalar(s, four(N0[s]) + four(N1[s]), four(XS[s]) + four(XD[s]), ACT.Relu
                                      ).then_inc(n01, 1)
                        act.wait_ge(ds_saved[s], 16)
                        act.sem_inc(ds_saved[s], -16)
                        nc.scalar.activation(DS[s][:, :], XS[s][:, :, P], ACT.Copy)
                        nc.scalar.activation(XR[s][:, :, :], XD[s][:, :, 0:P], ACT.Copy).then_inc(own_a, 1)
                        act.wait_ge(own_a, 1)
                        act.sem_inc(own_a, -1)
                        act.sem_inc(so.buf_free, 1)
                    for s, g, i in new:
                        act.wait_ge(turned, 1)
                        act.sem_inc(turned, -1)
                        nc.scalar.activation(HS[s][:, :], PA[s][:, :], ACT.Copy).then_inc(hs, 1)
                        nc.scalar.activation(HD[s][:, :], PB[s][:, :], ACT.Copy).then_inc(hd, 1)
                    for s, g, i in new:
                        act.wait_ge(proj, 1)
                        act.sem_inc(proj, -1)
                        nc.scalar.activation(FS[s][:, :], PA[s][:, :], ACT.Identity, bias=m.col["bs"][:, :])
                        nc.scalar.activation(E1[s][:, :], PB[s][:, :], ACT.Identity, bias=m.col["bsd"][:, :]
                                             ).then_inc(e1, 1)
                    if old:
                        ln2.root(act, old[0][0] // 2)
                    if ahead:
                        ln0.root(act, ahead[0][0] // 2)
                    if old:
                        act.wait_ge(scaled2, 1)
                        act.sem_inc(scaled2, -1)
                    for s, g, i in old:
                        ln2.on_scalar(s, four(N0[s]), four(X2[s]), ACT.Relu).then_inc(n2, 1)
                    for s, g, i in old:
                        act.wait_ge(t2, 1)
                        act.sem_inc(t2, -1)
                        nc.scalar.activation(HD[s][:, :], PA[s][:, :], ACT.Copy).then_inc(h2, 1)
                    for s, g, i in new:
                        on.exponentials(act, s).then_inc(on.exps, 1)
                ln0.root(act, 0)
                over_edge_lots(m, act, step)
        ph.retire()



def gcn(m):
    nc = m.nc
    with ExitStack() as ctx:
        ph = Phase(m, "l", ctx)
        XL, MS, OUT = (ph.each(k, [P, TILES, P]) for k in ["xl", "ms", "out"])
        KEYS = ph.each("keys", [P, ROWS])
        EC, DS = ph.each("ec", [P, 8]), ph.each("ds", [P, 4])
        EQ = ph.each("eq", [P, TILES, ROWS])
        LATER = ph.sb("later", [P, TILES, ROWS])
        SCR = ph.each("scr", [P, TILES, ROWS])
        CNT, DF, SEL = ph.each("cnt", [P, 4]), ph.each("df", [P, 4]), ph.each("sel", [P, 4])
        TRASH, TRASHI = ph.sb("trash", [P, 4]), ph.sb("trashi", [P, 4], I32)
        PA = ph.ps_each("a")
        so = Sockets(ph, [(m.xl_edge, XL, 0)], (m.x3, OUT), adds=True)
        row_in = ph.sem_each("row_in")
        row_free, ms, sums, later, own_d, own_a, own_p, eq_free = (ph.sem(k) for k in [
            "row_free", "ms", "sums", "later", "own_d", "own_a", "own_p", "eq_free"])
        tick_d = ph.counter("tick_d")

        with nc.Block() as block:
            @block.sync
            def _(sp):
                def indices(slots):
                    so.load_gather_idx(sp, m.last_idx, slots)

                def ahead(slots):
                    for s, g in slots:
                        sp.wait_ge(row_free, 1)
                        sp.sem_inc(row_free, -1)
                        sp.dma_start(KEYS[s][:, :], row_of(m.row["key"], g)).then_inc(row_in[s], 16)
                        sp.dma_start(EC[s][:, :], m.edge_col[:, bass.ds(g, 1), :].rearrange("p o w -> p (o w)")
                                     ).then_inc(row_in[s], 16)
                        sp.dma_start(DS[s][:, :], m.dis_src[:, bass.ds(g, 1), :].rearrange("p o w -> p (o w)")
                                     ).then_inc(row_in[s], 16)
                indices([(0, 0), (1, 1)])
                ahead([(0, 0), (1, 1)])
                with sp.Fori(0, m.edge_pairs - 1) as i:
                    indices([(0, 2 * i + 2), (1, 2 * i + 3)])
                    ahead([(0, 2 * i + 2), (1, 2 * i + 3)])

            @block.gpsimd
            def _(pool):
                nc.gpsimd.iota(TRASHI[:, :], pattern=[[P, 4]], base=m.N + 1, channel_multiplier=1)
                nc.gpsimd.memset(LATER[:, :, :], 1.0).then_inc(own_p, 1)
                pool.wait_ge(own_p, 1)
                pool.sem_inc(own_p, -1)
                nc.gpsimd.affine_select(out=LATER[:, :, :], in_=LATER[:, :, :], compare_op=ALU.is_ge, fill=0.0,
                                        base=-1, pattern=[[-P, TILES], [1, ROWS]], channel_multiplier=-1
                                        ).then_inc(own_p, 1)
                pool.wait_ge(own_p, 1)
                pool.sem_inc(own_p, -1)
                pool.sem_inc(later, 1)
                so.drive_adds(pool, m.EP - 1, m.N + 2 * ROWS - 1)

            @block.vector
            def _(dve):
                so.prime(dve)
                ph.prime(dve, 2, row_free)
                ph.prime(dve, 2, eq_free)
                dve.wait_ge(later, 1)
                dve.sem_inc(later, -1)
                nc.vector.tensor_copy(TRASH[:, :], TRASHI[:, :]).then_inc(own_d, 1)
                dve.wait_ge(own_d, 1)
                dve.sem_inc(own_d, -1)

                def body(i, slots):
                    for s, g in slots:
                        dve.wait_ge(row_in[s], 48)
                        dve.sem_inc(row_in[s], -48)
                        dve.wait_ge(eq_free, 1)
                        dve.sem_inc(eq_free, -1)
                        for a in range(TILES):
                            nc.vector.tensor_scalar(EQ[s][:, a, :], KEYS[s][:, :], EC[s][:, 4 + a:5 + a], None,
                                                    ALU.is_equal)
                        nc.vector.tensor_tensor(DF[s][:, :], TRASH[:, :], EC[s][:, 4:8], ALU.subtract)
                        dve.wait_ge(so.got[s], i * so.each + so.each)
                        dve.sem_inc(tick_d, 1)
                        for a in range(TILES):
                            last = nc.vector.tensor_scalar(MS[s][:, a, :], XL[s][:, a, :], DS[s][:, a:a + 1], None,
                                                           ALU.mult)
                        last.then_inc(own_d, 1)
                        dve.wait_ge(own_d, 1)
                        dve.sem_inc(own_d, -1)
                        dve.sem_inc(ms, 1)
                        dve.sem_inc(so.buf_free, 1)
                    for s, g in slots:
                        for a in range(TILES):
                            last = nc.vector.scalar_tensor_tensor(SCR[s][:, a, :], EQ[s][:, a, :], 1.0, LATER[:, a, :],
                                                                  ALU.mult, ALU.mult, accum_out=CNT[s][:, a:a + 1])
                        last.then_inc(own_d, 1)
                        dve.wait_ge(own_d, 1)
                        dve.sem_inc(own_d, -1)
                        nc.vector.tensor_scalar(SEL[s][:, :], CNT[s][:, :], 1.0, None, ALU.min).then_inc(own_d, 1)
                        dve.wait_ge(own_d, 1)
                        dve.sem_inc(own_d, -1)
                        nc.vector.tensor_tensor(SEL[s][:, :], SEL[s][:, :], DF[s][:, :], ALU.mult).then_inc(own_d, 1)
                        dve.wait_ge(own_d, 1)
                        dve.sem_inc(own_d, -1)
                        dve.wait_ge(so.si_free, 1)
                        dve.sem_inc(so.si_free, -1)
                        nc.vector.tensor_tensor(so.si[s][:, :], SEL[s][:, :], EC[s][:, 4:8], ALU.add).then_inc(own_d, 1)
                        dve.wait_ge(own_d, 1)
                        dve.sem_inc(own_d, -1)
                        dve.sem_inc(so.si_made, 1)
                        dve.sem_inc(row_free, 1)
                over_edges(m, dve, body)

            @block.tensor
            def _(pe):
                def body(i, slots):
                    for s, g in slots:
                        pe.wait_ge(ms, 1)
                        pe.sem_inc(ms, -1)
                        for b in range(TILES):
                            for a in range(TILES):
                                last = nc.tensor.matmul(PA[s][:, b * P:(b + 1) * P], EQ[s][:, a, b * P:(b + 1) * P],
                                                        MS[s][:, a, :], start=(a == 0), stop=(a == TILES - 1))
                        last.then_inc(sums, 1)
                over_edges(m, pe, body)

            @block.scalar
            def _(act):
                def body(i, slots):
                    for s, g in slots:
                        act.wait_ge(sums, 1)
                        act.sem_inc(sums, -1)
                        act.wait_ge(so.out_free, 1)
                        act.sem_inc(so.out_free, -1)
                        nc.scalar.activation(OUT[s][:, :, :].rearrange("p a d -> p (a d)"), PA[s][:, :],
                                                       ACT.Copy).then_inc(own_a, 1)
                        act.wait_ge(own_a, 1)
                        act.sem_inc(own_a, -1)
                        act.sem_inc(so.ready, 1)
                        act.sem_inc(eq_free, 1)
                over_edges(m, act, body)
        ph.retire()



def attention(m):
    nc = m.nc
    with ExitStack() as ctx:
        ph = Phase(m, "a", ctx, SLOTS)
        XS, XD, N0, N1 = (ph.each(k, [P, TILES, P]) for k in ["xs", "xd", "n0", "n1"])
        ln0, ln1 = Norm(ph, "ln0", 8), Norm(ph, "ln1", 8)
        KEEP, NEG = ph.each("keep", [P, ROWS], BF16), ph.each("neg", [P, ROWS], BF16)
        ND, DIF, Q, PR, E0, AG, AGT = (ph.each(k, [P, ROWS]) for k in ["nd", "dif", "q", "pr", "e0", "ag", "agt"])
        RZ = ph.each("rz", [P, TILES * 8])
        AO = ph.each("ao", [P, TILES, P])
        on = Online(ph)
        PA, PB = ph.ps_each("a"), ph.ps_each("b")
        so = Sockets(ph, [(m.x3[0:m.N, :], XS, 0), (m.x3[0:m.N, :], XD, 4)], (m.att, AO))
        row_in = ph.sem_each("row_in")
        (row_free, scaled0, scaled1, n0, src_normed, dst_normed, turned, nd, dif, qk, q, pr, score, summed, s_ps, ag, ag_ps, agt, ao_ps,
         ao_read, own_d, own_a) = (
            ph.sem(k) for k in ["row_free", "scaled0", "scaled1", "n0", "src_normed", "dst_normed", "turned", "nd", "dif", "qk", "q", "pr", "score",
                                "summed", "s_ps", "ag", "ag_ps", "agt", "ao_ps", "ao_read", "own_d", "own_a"])
        tick_d = ph.counter("tick_d")

        with nc.Block() as block:
            @block.sync
            def _(sp):
                def rows(slots):
                    for s, g, i in slots:
                        sp.wait_ge(row_free, 1)
                        sp.sem_inc(row_free, -1)
                        sp.dma_start(NEG[s][:, :], row_of(m.neg_row, g)).then_inc(row_in[s], 16)
                        sp.dma_start(KEEP[s][:, :], row_of(m.keep_row, g)).then_inc(row_in[s], 16)

                def step(new, old, ahead):
                    so.load_gather_idx(sp, m.gather_idx, so.next_lot(new))
                    so.load_scatter_idx(sp, old)
                    rows(ahead)
                so.load_gather_idx(sp, m.gather_idx, [(s, s, 0) for s in range(SLOTS)])
                rows([(0, 0, 0), (1, 1, 0)])
                over_edge_lots(m, sp, step)

            @block.gpsimd
            def _(pool):
                so.drive_lots(pool, m.N - 1, m.N - 1)

            @block.vector
            def _(dve):
                so.prime(dve)
                ph.prime(dve, SLOTS, row_free, ao_read)
                ln0.start(dve, own_d)
                ln1.start(dve, own_d)
                on.start(dve, own_d)

                def gathered(slots):
                    for s, g, i in slots:
                        dve.wait_ge(so.got[s], i * so.each + so.each)
                        dve.sem_inc(tick_d, 1)
                        dve.sem_inc(so.gi_free, 1)
                        last = ln0.stats(s, four(XS[s]) + four(XD[s]))
                    if slots:
                        last.then_inc(own_d, 1)
                        dve.wait_ge(own_d, 1)
                        dve.sem_inc(own_d, -1)
                        ln0.variances(dve, own_d, slots[0][0] // 2)

                def scales(slots):
                    if slots:
                        ln0.scales(dve, own_d, slots[0][0] // 2)
                        dve.sem_inc(scaled0, 1)

                def step(new, old, ahead):
                    for s, g, i in old:
                        dve.wait_ge(score, 1)
                        dve.sem_inc(score, -1)
                        dve.wait_ge(row_in[s], 32)
                        dve.sem_inc(row_in[s], -32)
                        on.maxima(dve, own_d, s, PA[s][:, :], NEG[s][:, :], KEEP[s][:, :])
                    for s, g, i in new:
                        dve.wait_ge(n0, 1)
                        dve.sem_inc(n0, -1)
                        last = ln1.stats(s, four(N0[s]) + four(N1[s]))
                    if new:
                        last.then_inc(own_d, 1)
                        dve.wait_ge(own_d, 1)
                        dve.sem_inc(own_d, -1)
                        ln1.variances(dve, own_d, new[0][0] // 2)
                    for s, g, i in old:
                        on.sums(dve, own_d, s, PB[s][:, :])
                        dve.sem_inc(summed, 1)
                        dve.sem_inc(row_free, 1)
                    if new:
                        ln1.scales(dve, own_d, new[0][0] // 2)
                        dve.sem_inc(scaled1, 1)
                    for s, g, i in new:
                        ln1.on_vector(s, four(N0[s]), four(N0[s])).then_inc(src_normed, 1)
                    for s, g, i in old:
                        dve.wait_ge(s_ps, 1)
                        dve.sem_inc(s_ps, -1)
                        nc.vector.reciprocal(RZ[s][:, :], PB[s][:, 0:TILES * 8]).then_inc(own_d, 1)
                        dve.wait_ge(own_d, 1)
                        dve.sem_inc(own_d, -1)
                        rz = RZ[s][:, :].rearrange("p (a o) -> p a o", o=1).broadcast_to([P, TILES * 8, 16])
                        nc.vector.tensor_tensor(AG[s][:, :].rearrange("p (a d) -> p a d", d=16),
                                                PA[s][:, :].rearrange("p (a d) -> p a d", d=16), rz, ALU.mult
                                                ).then_inc(ag, 1)
                    for s, g, i in new:
                        dve.wait_ge(nd, 1)
                        dve.sem_inc(nd, -1)
                        nc.vector.tensor_tensor(DIF[s][:, :], PA[s][:, :], ND[s][:, :], ALU.subtract
                                                ).then_inc(dif, 1)
                    gathered(ahead)
                    for s, g, i in new:
                        dve.wait_ge(q, 1)
                        dve.sem_inc(q, -1)
                        nc.vector.tensor_tensor(PR[s][:, :], PB[s][:, :], Q[s][:, :], ALU.mult).then_inc(pr, 1)
                    scales(ahead)
                gathered([(0, 0, 0), (1, 1, 0)])
                scales([(0, 0, 0), (1, 1, 0)])
                over_edge_lots(m, dve, step)

            @block.tensor
            def _(pe):
                def step(new, old, ahead):
                    for s, g, i in old:
                        pe.wait_ge(summed, 1)
                        pe.sem_inc(summed, -1)
                        turn(nc, PA[s], tiles(on.S[s]), m.ident)
                        for a in range(TILES):
                            out, of_a = PB[s][:, a * 8:a * 8 + 8], slice(a * P, (a + 1) * P)
                            nc.tensor.matmul(out, on.Z[s][:, of_a], m.heads8[:, :], start=True, stop=False)
                            last = nc.tensor.matmul(out, E0[s][:, of_a], m.heads8[:, :], start=False, stop=True)
                        last.then_inc(s_ps, 1)
                    for k in range(2):
                        for s, g, i in new[k:k + 1]:
                            pe.wait_ge(src_normed, 1)
                            pe.sem_inc(src_normed, -1)
                            pe.wait_ge(ao_read, 1)
                            pe.sem_inc(ao_read, -1)
                            turn(nc, PA[s], N0[s], m.ident)
                            pe.wait_ge(dst_normed, 1)
                            pe.sem_inc(dst_normed, -1)
                            turn(nc, PB[s], N1[s], m.ident).then_inc(turned, 1)
                        for s, g, i in old[k:k + 1]:
                            pe.wait_ge(ag, 1)
                            pe.sem_inc(ag, -1)
                            turn(nc, PA[s], tiles(AG[s]), m.ident).then_inc(ag_ps, 1)
                    for s, g, i in new:
                        pe.wait_ge(dif, 1)
                        pe.sem_inc(dif, -1)
                        nc.tensor.matmul(PA[s][:, :], m.wn["Wq"][:, :], ND[s][:, :], start=True, stop=True)
                        nc.tensor.matmul(PB[s][:, :], m.wn["Wk"][:, :], DIF[s][:, :], start=True, stop=True
                                         ).then_inc(qk, 1)
                    for s, g, i in old:
                        pe.wait_ge(agt, 1)
                        pe.sem_inc(agt, -1)
                        rows_product(nc, PB[s], [(AGT[s], m.wn["Wo"][:, :]), (ND[s], m.wn["Wvo"][:, :])],
                                     m.bias["bo"], m.ones_row).then_inc(ao_ps, 1)
                    for s, g, i in new:
                        pe.wait_ge(pr, 1)
                        pe.sem_inc(pr, -1)
                        nc.tensor.matmul(PA[s][:, :], m.sum_heads[:, :], PR[s][:, :], start=True, stop=True)
                        nc.tensor.matmul(PB[s][:, :], m.wn["Wv"][:, :], DIF[s][:, :], start=True, stop=True
                                         ).then_inc(score, 1)
                over_edge_lots(m, pe, step)

            @block.scalar
            def _(act):
                def step(new, old, ahead):
                    if new:
                        act.wait_ge(scaled0, 1)
                        act.sem_inc(scaled0, -1)
                    for s, g, i in new:
                        ln0.on_scalar(s, four(N0[s]) + four(N1[s]), four(XS[s]) + four(XD[s]), ACT.Relu).then_inc(own_a, 1)
                        act.wait_ge(own_a, 1)
                        act.sem_inc(own_a, -1)
                        act.sem_inc(n0, 1)
                        act.sem_inc(so.buf_free, 1)
                    for s, g, i in old:
                        on.exponentials(act, s)
                        nc.scalar.activation(E0[s][:, :], on.M[s][:, 1:], ACT.Exp, scale=-1.0).then_inc(on.exps, 1)
                    if new:
                        ln1.root(act, new[0][0] // 2)
                        act.wait_ge(scaled1, 1)
                        act.sem_inc(scaled1, -1)
                    for s, g, i in new:
                        ln1.on_scalar(s, four(N1[s]), four(N1[s]), ACT.Identity, at=4).then_inc(dst_normed, 1)
                    for s, g, i in new:
                        act.wait_ge(turned, 1)
                        act.sem_inc(turned, -1)
                        nc.scalar.activation(ND[s][:, :], PB[s][:, :], ACT.Copy).then_inc(nd, 1)
                    for s, g, i in old:
                        act.wait_ge(ag_ps, 1)
                        act.sem_inc(ag_ps, -1)
                        nc.scalar.activation(AGT[s][:, :], PA[s][:, :], ACT.Copy).then_inc(agt, 1)
                    for s, g, i in new:
                        act.wait_ge(qk, 1)
                        act.sem_inc(qk, -1)
                        nc.scalar.activation(Q[s][:, :], PA[s][:, :], ACT.Identity, bias=m.col["bq"][:, :]
                                             ).then_inc(q, 1)
                    if ahead:
                        ln0.root(act, ahead[0][0] // 2)
                    for s, g, i in old:
                        act.wait_ge(ao_ps, 1)
                        act.sem_inc(ao_ps, -1)
                        act.wait_ge(so.out_free, 1)
                        act.sem_inc(so.out_free, -1)
                        nc.scalar.activation(AO[s][:, :, :].rearrange("p a d -> p (a d)"), PB[s][:, :],
                                                       ACT.Copy).then_inc(own_a, 1)
                        act.wait_ge(own_a, 1)
                        act.sem_inc(own_a, -1)
                        act.sem_inc(so.ready, 1)
                        act.sem_inc(ao_read, 1)
                ln0.root(act, 0)
                over_edge_lots(m, act, step)
        ph.retire()


def program(nc, ins, out):
    with ExitStack() as ctx:
        m = Machine(nc, ins, out, ctx)
        weights(m)
        edges(m)
        nodes_first(m)
        sage_first(m)
        sage_second(m)
        gat(m)
        gcn(m)
        attention(m)
        nodes_last(m)



def kernel(**inputs):
    import concourse.bacc as bacc
    from concourse.bass_utils import run_bass_kernel_spmd

    nc = bacc.Bacc("TRN2", target_bir_lowering=False, num_devices=1)
    arrays, ins = {}, {}
    for name, value in inputs.items():
        a = np.ascontiguousarray(value)
        arrays["in_" + name] = a
        ins[name] = nc.dram_tensor("in_" + name, a.shape, mybir.dt.from_np(a.dtype), kind="ExternalInput").ap()
    out = nc.dram_tensor("out", inputs["x"].shape, F32, kind="ExternalOutput").ap()
    program(nc, ins, out)
    r = run_bass_kernel_spmd(nc, [arrays], core_ids=[0])
    return r.results[0]["out"]
```
